# Optimizing a Trainium2 kernel written in Bass

```python
import numpy as np
import jax
import jax.numpy as jnp

def _softmax(x, axis=-1):
    return jax.nn.softmax(x, axis=axis)

def _gelu(x):
    return jax.nn.gelu(x, approximate=True)

def _silu(x):
    return jax.nn.silu(x)

def _sigmoid(x):
    return jax.nn.sigmoid(x)

def _layernorm(x, axis=-1, eps=1e-05):
    m = jnp.mean(x, axis=axis, keepdims=True)
    v = jnp.var(x, axis=axis, keepdims=True)
    return (x - m) / jnp.sqrt(v + eps)

def _scatter_add(tgt, idx, src, axis=0):
    return tgt.at[idx].add(src)

def _segment_sum(src, seg, n):
    return jax.ops.segment_sum(src, seg, n)
kernel_name = 'mk_flamingo_gated_d2_seqx_r4_9e6c19'

def setup_inputs(seed: int=0):
    np.random.seed(seed)
    _w = jnp.asarray

    def _rec_inputs():
        import jax
        import jax.numpy as jnp
        _rk = jax.random.key(seed)
        x = -0.0002928 + 1 * jax.random.normal(jax.random.fold_in(_rk, 1), (4, 512, 256), jnp.float32)
        _lenS = 512 - jax.random.randint(jax.random.fold_in(_rk, 7), (4,), 0, max(1, 512 // 4) + 1, jnp.int32)
        _lenS2 = 512 - jax.random.randint(jax.random.fold_in(_rk, 8), (4,), 0, max(1, 512 // 4) + 1, jnp.int32)
        _ctx_2048P = jax.random.normal(jax.random.fold_in(_rk, 11), (4, 16, 512), jnp.float32)
        _ctx_2048c = jax.random.dirichlet(jax.random.fold_in(_rk, 511), 0.3 * jnp.ones((16,), jnp.float32), (4, 512))
        _ctx_2048t = jnp.einsum('bsk,bkd->bsd', _ctx_2048c, _ctx_2048P)
        _ctx_2048t = _ctx_2048t * jax.lax.rsqrt(jnp.mean(jnp.square(_ctx_2048t)) + 1e-12) * 0.953939
        ctx_2048 = -0.000514642 + 1.00011 * (_ctx_2048t + 0.3 * jax.random.normal(jax.random.fold_in(_rk, 611), (4, 512, 512), jnp.float32))
        _g = jax.random.normal(jax.random.fold_in(_rk, 9001), (2, 2), jnp.float32)
        _g = jnp.sign(_g) * jnp.maximum(jnp.abs(_g), 1.0) + (_g == 0) * 1.0
        g_xattn = _g[0]
        g_ffn = _g[1]
        return (x, ctx_2048, g_xattn, g_ffn)
    x, ctx_2048, g_xattn, g_ffn = _rec_inputs()

    def _L0_xattn_setup():
        import jax, jax.numpy as jnp
        import numpy as np
        NUM_HEADS = 16
        key = jax.random.key(seed)
        ks = jax.random.split(key, 5)
        dim = 256
        B, N, N_c = (4, 256, 64)
        x = jax.random.normal(ks[0], (B, N, dim), dtype=jnp.float32)
        context = jax.random.normal(ks[1], (B, N_c, 2 * dim), dtype=jnp.float32)
        w_qkv = jax.random.normal(ks[2], (3 * dim, dim), dtype=jnp.float32) * 0.02
        w_proj = jax.random.normal(ks[3], (dim, dim), dtype=jnp.float32) * 0.02
        b_proj = jax.random.normal(ks[4], (dim,), dtype=jnp.float32) * 0.02
        return {'x': x, 'context': context, 'w_qkv': w_qkv, 'w_proj': w_proj, 'b_proj': b_proj}
    _L0_xattn_all = _L0_xattn_setup()
    _L0_xattn_in = {k: v for k, v in _L0_xattn_all.items() if k in ('w_qkv', 'w_proj', 'b_proj')}
    del _L0_xattn_all

    def _L0_ffn_setup():
        import jax, jax.numpy as jnp
        import numpy as np
        D_MODEL = 256
        M = 64
        INNER = 16
        key = jax.random.key(seed)
        ks = jax.random.split(key, 9)

        def init(k, shape, fan_in):
            bound = 1.0 / np.sqrt(fan_in)
            return jax.random.uniform(k, shape, jnp.float32, -bound, bound)
        x = jax.random.normal(ks[0], (16, 1024, D_MODEL), dtype=jnp.float32)
        Win = init(ks[1], (D_MODEL, M), D_MODEL)
        bin_ = init(ks[2], (M,), D_MODEL)
        W1 = init(ks[3], (M, INNER), 1)
        b1 = init(ks[4], (M, INNER), 1)
        W2 = init(ks[5], (M, INNER), INNER)
        b2 = init(ks[6], (M,), INNER)
        Wout = init(ks[7], (M, D_MODEL), M)
        bout = init(ks[8], (D_MODEL,), M)
        return {'x': x, 'Win': Win, 'bin_': bin_, 'W1': W1, 'b1': b1, 'W2': W2, 'b2': b2, 'Wout': Wout, 'bout': bout}
    _L0_ffn_all = _L0_ffn_setup()
    _L0_ffn_in = {k: v for k, v in _L0_ffn_all.items() if k in ('Win', 'bin_', 'W1', 'b1', 'W2', 'b2', 'Wout', 'bout')}
    del _L0_ffn_all

    def _L1_xattn_setup():
        import jax, jax.numpy as jnp
        import numpy as np
        B, N, DIM = (8, 1024, 256)
        M, CTX = (64, 512)
        HEADS, DH = (16, 64)
        INNER = HEADS * DH
        EPS = 1e-06

        def _split_heads(t):
            b, n, _ = t.shape
            return t.reshape(b, n, HEADS, DH).transpose(0, 2, 1, 3)
        key = jax.random.key(seed)
        ks = jax.random.split(key, 6)
        x = jax.random.normal(ks[0], (B, N, DIM), dtype=jnp.float32)
        context = jax.random.normal(ks[1], (B, M, CTX), dtype=jnp.float32)
        Wq = jax.random.normal(ks[2], (DIM, INNER), dtype=jnp.float32) / np.sqrt(DIM)
        Wkv = jax.random.normal(ks[3], (CTX, 2 * INNER), dtype=jnp.float32) / np.sqrt(CTX)
        null_kv = jax.random.normal(ks[4], (2, DH), dtype=jnp.float32) / np.sqrt(2.0)
        Wout = jax.random.normal(ks[5], (INNER, DIM), dtype=jnp.float32) / np.sqrt(INNER)
        ln_scale = jnp.ones((DIM,), dtype=jnp.float32)
        ln_bias = jnp.zeros((DIM,), dtype=jnp.float32)
        return {'x': x, 'context': context, 'Wq': Wq, 'Wkv': Wkv, 'null_kv': null_kv, 'Wout': Wout, 'ln_scale': ln_scale, 'ln_bias': ln_bias}
    _L1_xattn_all = _L1_xattn_setup()
    _L1_xattn_in = {k: v for k, v in _L1_xattn_all.items() if k in ('Wq', 'Wkv', 'null_kv', 'Wout', 'ln_scale', 'ln_bias')}
    del _L1_xattn_all

    def _L1_ffn_setup():
        import jax, jax.numpy as jnp
        import numpy as np
        B, T, D = (1, 256, 256)
        E, S, H = (8, 2, 1024)
        key = jax.random.key(seed)
        kx, kg, k1, k2, k3 = jax.random.split(key, 5)
        X = jax.random.normal(kx, (B, T, D), jnp.float32)
        Wg = jax.random.normal(kg, (D, E), jnp.float32) * 0.02
        bg = jnp.zeros((E,), jnp.float32)
        W1 = jax.random.normal(k1, (E, D, H), jnp.float32) * 0.02
        W3 = jax.random.normal(k3, (E, D, H), jnp.float32) * 0.02
        W2 = jax.random.normal(k2, (E, H, D), jnp.float32) * 0.02
        return {'X': X, 'Wg': Wg, 'bg': bg, 'W1': W1, 'W2': W2, 'W3': W3}
    _L1_ffn_all = _L1_ffn_setup()
    _L1_ffn_in = {k: v for k, v in _L1_ffn_all.items() if k in ('Wg', 'bg', 'W1', 'W2', 'W3')}
    del _L1_ffn_all
    return {'x': x, 'ctx_2048': ctx_2048, 'g_xattn': g_xattn, 'g_ffn': g_ffn, 'L0_xattn_w_qkv': _L0_xattn_in['w_qkv'], 'L0_xattn_w_proj': _L0_xattn_in['w_proj'], 'L0_xattn_b_proj': _L0_xattn_in['b_proj'], 'L0_ffn_Win': _L0_ffn_in['Win'], 'L0_ffn_bin_': _L0_ffn_in['bin_'], 'L0_ffn_W1': _L0_ffn_in['W1'], 'L0_ffn_b1': _L0_ffn_in['b1'], 'L0_ffn_W2': _L0_ffn_in['W2'], 'L0_ffn_b2': _L0_ffn_in['b2'], 'L0_ffn_Wout': _L0_ffn_in['Wout'], 'L0_ffn_bout': _L0_ffn_in['bout'], 'L1_xattn_Wq': _L1_xattn_in['Wq'], 'L1_xattn_Wkv': _L1_xattn_in['Wkv'], 'L1_xattn_null_kv': _L1_xattn_in['null_kv'], 'L1_xattn_Wout': _L1_xattn_in['Wout'], 'L1_xattn_ln_scale': _L1_xattn_in['ln_scale'], 'L1_xattn_ln_bias': _L1_xattn_in['ln_bias'], 'L1_ffn_Wg': _L1_ffn_in['Wg'], 'L1_ffn_bg': _L1_ffn_in['bg'], 'L1_ffn_W1': _L1_ffn_in['W1'], 'L1_ffn_W2': _L1_ffn_in['W2'], 'L1_ffn_W3': _L1_ffn_in['W3']}

def reference(x, ctx_2048, g_xattn, g_ffn, L0_xattn_w_qkv, L0_xattn_w_proj, L0_xattn_b_proj, L0_ffn_Win, L0_ffn_bin_, L0_ffn_W1, L0_ffn_b1, L0_ffn_W2, L0_ffn_b2, L0_ffn_Wout, L0_ffn_bout, L1_xattn_Wq, L1_xattn_Wkv, L1_xattn_null_kv, L1_xattn_Wout, L1_xattn_ln_scale, L1_xattn_ln_bias, L1_ffn_Wg, L1_ffn_bg, L1_ffn_W1, L1_ffn_W2, L1_ffn_W3):
    import jax
    import jax.numpy as jnp

    def _L0_xattn_ref(x, context, w_qkv, w_proj, b_proj):
        import jax, jax.numpy as jnp
        import numpy as np
        NUM_HEADS = 16
        B, N, C = x.shape
        H = NUM_HEADS
        D = C // H
        scale = D ** (-0.5)
        qkv = (x @ w_qkv.T).reshape(B, N, 3, H, D).transpose(2, 0, 3, 1, 4)
        q, k, v = (qkv[0], qkv[1], qkv[2])
        N_c = context.shape[1]
        kv = context.reshape(B, N_c, 2, H, D).transpose(2, 0, 3, 1, 4)
        extra_k, extra_v = (kv[0], kv[1])
        k = jnp.concatenate([extra_k, k], axis=2)
        v = jnp.concatenate([extra_v, v], axis=2)
        dtype = q.dtype
        attn = jnp.einsum('bhnd,bhmd->bhnm', q * scale, k).astype(jnp.float32)
        attn = jax.nn.softmax(attn, axis=-1).astype(dtype)
        out = jnp.einsum('bhnm,bhmd->bhnd', attn, v)
        out = out.transpose(0, 2, 1, 3).reshape(B, N, C)
        return out @ w_proj.T + b_proj

    def _L0_ffn_ref(x, Win, bin_, W1, b1, W2, b2, Wout, bout):
        import jax, jax.numpy as jnp
        import numpy as np
        D_MODEL = 256
        M = 64
        INNER = 16
        s = jnp.einsum('btd,dm->btm', x, Win) + bin_
        h = jax.nn.relu(s[..., None] * W1 + b1)
        g = jnp.einsum('btmh,mh->btm', h, W2) + b2
        out = jnp.einsum('btm,md->btd', g, Wout) + bout
        return out

    def _L1_xattn_ref(x, context, Wq, Wkv, null_kv, Wout, ln_scale, ln_bias):
        import jax, jax.numpy as jnp
        import numpy as np
        B, N, DIM = (8, 1024, 256)
        M, CTX = (64, 512)
        HEADS, DH = (16, 64)
        INNER = HEADS * DH
        EPS = 1e-06

        def _split_heads(t):
            b, n, _ = t.shape
            return t.reshape(b, n, HEADS, DH).transpose(0, 2, 1, 3)
        scale = DH ** (-0.5)
        b = x.shape[0]
        q = _split_heads(jnp.einsum('bnd,df->bnf', x, Wq))
        kv = jnp.einsum('bmc,cf->bmf', context, Wkv)
        k, v = jnp.split(kv, 2, axis=-1)
        k, v = (_split_heads(k), _split_heads(v))
        nk = jnp.broadcast_to(null_kv[0], (b, HEADS, 1, DH))
        nv = jnp.broadcast_to(null_kv[1], (b, HEADS, 1, DH))
        k = jnp.concatenate((nk, k), axis=-2)
        v = jnp.concatenate((nv, v), axis=-2)
        q = q * scale
        sim = jnp.einsum('bhid,bhjd->bhij', q, k)
        attn = jax.nn.softmax(sim, axis=-1)
        out = jnp.einsum('bhij,bhjd->bhid', attn, v)
        out = out.transpose(0, 2, 1, 3).reshape(b, -1, INNER)
        out = jnp.einsum('bnf,fd->bnd', out, Wout)
        mu = jnp.mean(out, axis=-1, keepdims=True)
        var = jnp.var(out, axis=-1, keepdims=True)
        out = (out - mu) * jax.lax.rsqrt(var + EPS) * ln_scale + ln_bias
        return out

    def _L1_ffn_ref(X, Wg, bg, W1, W2, W3):
        import jax, jax.numpy as jnp
        import numpy as np
        B, T, D = (1, 256, 256)
        E, S, H = (8, 2, 1024)
        logits = jnp.einsum('btd,de->bte', X, Wg) + bg
        topv, topi = jax.lax.top_k(logits, S)
        w = jax.nn.softmax(topv, axis=-1)
        xs = X[:, :, None, :] * w[..., None]
        out = X
        for e in range(E):
            h = jax.nn.silu(jnp.einsum('btsd,dh->btsh', xs, W1[e])) * jnp.einsum('btsd,dh->btsh', xs, W3[e])
            y = jnp.einsum('btsh,hd->btsd', h, W2[e])
            mask = (topi == e)[..., None]
            out = out + jnp.where(mask, y, 0.0).sum(axis=2)
        return out
    x = x + jnp.tanh(g_xattn[0]) * _L0_xattn_ref(_layernorm(x, axis=-1), ctx_2048, L0_xattn_w_qkv, L0_xattn_w_proj, L0_xattn_b_proj)
    x = x + jnp.tanh(g_ffn[0]) * _L0_ffn_ref(_layernorm(x, axis=-1), L0_ffn_Win, L0_ffn_bin_, L0_ffn_W1, L0_ffn_b1, L0_ffn_W2, L0_ffn_b2, L0_ffn_Wout, L0_ffn_bout)
    x = x + jnp.tanh(g_xattn[1]) * _L1_xattn_ref(_layernorm(x, axis=-1), ctx_2048, L1_xattn_Wq, L1_xattn_Wkv, L1_xattn_null_kv, L1_xattn_Wout, L1_xattn_ln_scale, L1_xattn_ln_bias)
    x = x + jnp.tanh(g_ffn[1]) * _L1_ffn_ref(_layernorm(x, axis=-1), L1_ffn_Wg, L1_ffn_bg, L1_ffn_W1, L1_ffn_W2, L1_ffn_W3)
    return x

_drawn_inputs = setup_inputs


def setup_inputs(seed=0):
    import zlib

    import numpy as np

    out = dict(_drawn_inputs(seed))
    spreads = {'g_ffn': (-1.0, 0.2),
     'L1_xattn_ln_scale': (1.0, 0.2),
     'L1_xattn_ln_bias': (0.0, 0.1),
     'L1_ffn_bg': (0.0, 0.8)}
    factors = {'L0_xattn_w_qkv': 8.0,
     'L0_xattn_b_proj': 4.984,
     'L0_ffn_bin_': 8.0,
     'L1_xattn_null_kv': 8.0,
     'L1_ffn_Wg': 3.984,
     'L1_ffn_W1': 3.273,
     'L1_ffn_W2': 3.252,
     'L1_ffn_W3': 3.283}
    for name, (base, spread) in spreads.items():
        noise = np.random.default_rng([zlib.crc32(name.encode()), seed]).standard_normal(out[name].shape)
        drawn = base * np.exp(spread * noise) if base else spread * noise
        out[name] = jnp.asarray(drawn.astype(out[name].dtype))
    for name, factor in factors.items():
        out[name] = (out[name] * factor).astype(out[name].dtype)
    return out
```

```python
from contextlib import ExitStack

import concourse.bass as bass
from concourse import mybir

F32 = mybir.dt.float32
F32R = mybir.dt.float32r
U32 = mybir.dt.uint32
ALU = mybir.AluOpType
ACT = mybir.ActivationFunctionType
AX_X = mybir.AxisListType.X

P = 128
BANK = 512
LN_EPS = 1e-5
LN_OUT_EPS = 1e-6
RSQRT_MAGIC = 0x5F3759DF


class Shapes:

    def __init__(self, x, ctx, w_win, w_router, moe_w1, null_kv, wq1):
        self.B, self.N, self.D = x.shape
        self.M, self.C = ctx.shape[1], ctx.shape[2]
        self.TT = self.N // P
        self.T = self.B * self.TT
        self.DC = self.D // P
        self.CC = self.C // P
        self.H = 16
        self.DH0 = self.D // self.H
        self.KT0 = (self.M + self.N) // P
        self.DH1 = null_kv.shape[1]
        self.I1 = wq1.shape[1]
        self.KT1 = self.M // P
        self.FM = w_win.shape[1]
        self.E = w_router.shape[1]
        self.F = moe_w1.shape[2]
        self.FT = self.F // P


class Norm:

    STEPS = 3

    def __init__(self, nc, tiles, stats, mv, work):
        self.nc, self.tiles, self.stats, self.mv, self.work = nc, tiles, stats, mv, work

    def statistics(self, dve, rows, eps):
        nc, n = self.nc, self.tiles
        for t in range(n):
            nc.vector.bn_stats(self.stats[:, t, :], rows(t))
        dve.drain()
        for t in range(n):
            nc.vector.bn_aggr(self.mv[:, t, :], self.stats[:, t, :])
        dve.drain()
        var, guess, half, tmp = (self.work[:, i, 0:n] for i in range(4))
        nc.vector.tensor_scalar(var, self.mv[:, 0:n, 1], 1.0, eps, ALU.mult, ALU.add)
        dve.drain()
        nc.vector.tensor_scalar(tmp.bitcast(U32), var.bitcast(U32), 1, None, ALU.logical_shift_right)
        nc.vector.tensor_scalar(half, var, -0.5, None, ALU.mult)
        dve.drain()
        nc.vector.tensor_scalar(guess.bitcast(U32), tmp.bitcast(U32), -1.0, float(RSQRT_MAGIC), ALU.mult, ALU.add)
        dve.drain()
        for _ in range(self.STEPS):
            nc.vector.tensor_tensor(tmp, guess, guess, ALU.mult)
            dve.drain()
            nc.vector.tensor_tensor(tmp, tmp, half, ALU.mult)
            dve.drain()
            nc.vector.scalar_tensor_tensor(out=guess, in0=tmp, scalar=1.5, in1=guess, op0=ALU.add, op1=ALU.mult)
            dve.drain()
        self.rstd = guess

    def apply(self, out, row, t):
        return self.nc.vector.tensor_scalar(out, row, self.mv[:, t, 0:1], self.work[:, 1, t:t + 1],
                                            ALU.subtract, ALU.mult)


def layer0(nc, s, g, bank, wide, dram):
    T, H, DH, N, D = s.TT, s.H, s.DH0, s.N, s.D
    ST = 64
    K_SCORE, M_ROW = 3 * DH, 3 * DH
    PAIRS, QUADS = H // 2, H // 4
    KT = s.KT0
    SCALE = float(DH) ** -0.5
    PT_RING = 8

    with ExitStack() as ctx:
        def sb(name, shape, dt=F32):
            return ctx.enter_context(nc.sbuf_tensor("l0_" + name, shape, dt))

        def sem(name):
            return ctx.enter_context(nc.semaphore(name))

        w_qkv = sb("w_qkv", [P, s.DC, 3 * D])
        w_proj = sb("w_proj", [P, QUADS, D])
        b_proj = sb("b_proj", [P, D])
        w_in = sb("w_in", [P, s.DC, P])
        w_out = sb("w_out", [P, D])
        b_out = sb("b_out", [P, D])
        b_in = sb("b_in", [P, 1])
        w1 = sb("w1", [P, 8])
        b1 = sb("b1", [P, 8])
        w2 = sb("w2", [P, 8])
        b2 = sb("b2", [P, 1])
        ctx_sb = sb("ctx_sb", [P, T, 2 * D])
        xn = sb("xn", [P, T, D])
        xT = sb("xT", [P, s.DC, N])
        q_stack = sb("q_stack", [P, T, H, ST])
        k_stack = sb("k_stack", [P, 2, H, ST])
        qT = sb("qT", [P, PAIRS, N], F32R)
        kT = sb("kT", [P, PAIRS, KT * P], F32R)
        qmT = sb("qmT", [P, 2, 2, N], F32R)
        v_ones = sb("v_ones", [P, KT, H, 2 * DH])
        probs = sb("probs", [P, PT_RING, 2 * P * 4])
        oT = sb("oT", [P, QUADS, N])
        denom = sb("denom", [P, N])
        tile_max = sb("tile_max", [P, T, H, 2])
        units = sb("units", [P, 2, N])
        gated = sb("gated", [P, N])
        s_in = sb("s_in", [P, N])
        x_bias = sb("x_bias", [P, T, D])
        stats = sb("stats", [P, T, 6])
        mv = sb("mv", [P, T, 2])
        work = sb("work", [P, 4, T])
        norm = Norm(nc, T, stats, mv, work)

        loaded = sem("l0_weights_loaded")
        filled = sem("l0_constants_filled")

        with nc.Block() as block:
            @block.sync
            def _(sp):
                sp.dma_start(w_qkv[:], dram["w_qkvT"].rearrange("(c p) n -> p c n", p=P)).then_inc(loaded, 16)
                sp.dma_start(w_proj[:], dram["w_projT"].rearrange("(g p) n -> p g n", p=P)).then_inc(loaded, 16)
                sp.dma_start(b_proj[:], dram["b_proj"].partition_broadcast(P)).then_inc(loaded, 16)
                for half in range(2):
                    sp.dma_start(w_in[:, :, half * s.FM:(half + 1) * s.FM],
                                 dram["w_in"].rearrange("(c p) n -> p c n", p=P)).then_inc(loaded, 16)
                    rows = slice(half * s.FM, (half + 1) * s.FM)
                    sp.dma_start(w_out[rows, :], dram["w_out"]).then_inc(loaded, 16)
                    sp.dma_start(b_in[rows, :], dram["b_in"].unsqueeze(1)).then_inc(loaded, 16)
                    for dst, src in ((w1, "w1"), (b1, "b1"), (w2, "w2")):
                        sp.dma_start(dst[rows, :], dram[src][:, 8 * half:8 * half + 8]).then_inc(loaded, 16)
                sp.dma_start(b2[0:s.FM, :], dram["b2"].unsqueeze(1)).then_inc(loaded, 16)
                sp.dma_start(b_out[:], dram["b_out"].partition_broadcast(P)).then_inc(loaded, 16)
                sp.wait_ge(loaded, 16 * 17)

            @block.gpsimd
            def _(pool):
                nc.gpsimd.memset(q_stack[:], 0.0)
                nc.gpsimd.memset(k_stack[:], 0.0)
                nc.gpsimd.memset(v_ones[:], 1.0)
                pool.drain()
                nc.gpsimd.memset(b2[s.FM:P, :], 0.0)
                pool.drain()
                nc.gpsimd.memset(k_stack[:, :, :, M_ROW:M_ROW + 1], 1.0)

        with nc.Block() as block:
            @block.vector
            def _(dve):
                nc.vector.tensor_scalar(b_proj[:], b_proj[:], g["gates"][:, 0:1], None, ALU.mult)
                nc.vector.tensor_scalar(b_out[:], b_out[:], g["gates"][:, 1:2], None, ALU.mult)

        ctx_ready = sem("l0_ctx_ready")
        xn_ready = sem("l0_xn_ready")
        xT_psum = sem("l0_xT_psum")
        xT_act = sem("l0_xT_act")
        xT_dve = sem("l0_xT_dve")
        qk_psum = sem("l0_qk_psum")
        v_psum = sem("l0_v_psum")
        qk_split = sem("l0_qk_split")
        v_copied = sem("l0_v_copied")
        split = sem("l0_split")
        dup = sem("l0_dup")
        tr_psum = sem("l0_tr_psum")
        tr_act = sem("l0_tr_act")
        tr_dve = sem("l0_tr_dve")

        max_psum = sem("l0_max_psum")
        max_read = sem("l0_max_read")
        negmax = sem("l0_negmax")
        qm_psum = sem("l0_qm_psum")
        qm_ready = sem("l0_qm_ready")
        s_psum = sem("l0_s_psum")
        exp_done = sem("l0_exp_done")
        pv_done = sem("l0_pv_done")
        norm_done = sem("l0_norm_done")

        bias_added = sem("l0_bias_added")
        proj_psum = sem("l0_proj_psum")
        resid = sem("l0_resid")
        xn2_ready = sem("l0_xn2_ready")
        xT2_psum = sem("l0_xT2_psum")
        xT2_act = sem("l0_xT2_act")
        xT2_dve = sem("l0_xT2_dve")
        sin_psum = sem("l0_sin_psum")
        sin_ready = sem("l0_sin_ready")
        unit_ready = sem("l0_unit_ready")
        unit_used = sem("l0_unit_used")
        ffn_psum = sem("l0_ffn_psum")
        ffn_done = sem("l0_ffn_done")

        items = [("k", t) for t in range(s.KT0 - T)] + [i for t in range(T) for i in (("k", s.KT0 - T + t), ("q", t))]
        NI = len(items)
        NCTX = s.KT0 - T

        def item_banks(i):
            return (6, 7) if i % 2 == 0 else (0, 1)

        def key_source(kt):
            return k_stack[:, kt % 2]

        for b in range(s.B):
            x_b = g["x"][:, b * T:(b + 1) * T, :]

            with nc.Block() as block:
                @block.sync
                def _(sp):
                    sp.dma_start(ctx_sb[:], dram["ctx"][b].rearrange("(t p) n -> p t n", p=P)).then_inc(ctx_ready, 16)

                @block.vector
                def _(dve):
                    n_split = b * (NCTX + 2 * T)

                    def evacuate(i):
                        kind, t = items[i]
                        dve.wait_ge(tr_psum, b * NI + i + 1)
                        dst = kT if kind == "k" else qT
                        nc.vector.tensor_copy(dst[:, 4:8, t * P:(t + 1) * P],
                                              bank(item_banks(i)[1]).rearrange("p (a n) -> p a n", a=4)
                                              ).then_inc(tr_dve, 1)

                    def split_keys(src, dst):
                        src = src.rearrange("p (h d) -> p h d", h=H)
                        nc.vector.tensor_copy(dst[:, :, 0:DH].bitcast(F32R), src)
                        dve.drain()
                        return nc.vector.tensor_tensor(dst[:, :, DH:2 * DH], src, dst[:, :, 0:DH], ALU.subtract)

                    def split_queries(src, dst):
                        src = src.rearrange("p (h d) -> p h d", h=H)
                        nc.vector.tensor_copy(dst[:, :, 0:DH].bitcast(F32R), src)
                        dve.drain()
                        return nc.vector.tensor_tensor(dst[:, :, 2 * DH:3 * DH], src, dst[:, :, 0:DH], ALU.subtract)

                    norm.statistics(dve, lambda t: x_b[:, t, :], LN_EPS)
                    for t in range(T):
                        norm.apply(xn[:, t, :], x_b[:, t, :], t).then_inc(xn_ready, 1)
                    dve.wait_ge(ctx_ready, 16 * (b + 1))
                    for t in range(NCTX):
                        if t >= 2:
                            dve.wait_ge(tr_psum, b * NI + t - 1)
                        split_keys(ctx_sb[:, t, 0:D], key_source(t)).then_inc(split, 1)
                        if t >= 1:
                            evacuate(t - 1)
                    evacuate(NCTX - 1)
                    dve.wait_ge(xT_psum, 2 * b + 2)
                    nc.vector.tensor_copy(xT[:, 1, :], bank(3)).then_inc(xT_dve, 1)
                    for t in range(T):
                        dve.wait_ge(qk_psum, b * T + t + 1)
                        kt = NCTX + t
                        dve.wait_ge(tr_psum, b * NI + (NCTX + 2 * t - 3 if t >= 2 else NCTX - 1 + t))
                        qk = bank(2 + 2 * (t % 2))
                        split_queries(qk[:, 0:D], q_stack[:, t])
                        split_keys(qk[:, D:2 * D], key_source(kt)).then_inc(split, 1)
                        if t >= 1:
                            evacuate(NCTX + 2 * t - 2)
                            evacuate(NCTX + 2 * t - 1)
                    evacuate(NI - 2)
                    evacuate(NI - 1)

                @block.gpsimd
                def _(pool):
                    pool.wait_ge(ctx_ready, 16 * (b + 1))
                    for t in range(NCTX):
                        pool.wait_ge(split, b * (NCTX + T) + t + 1)
                        nc.gpsimd.tensor_copy(key_source(t)[:, :, 2 * DH:3 * DH], key_source(t)[:, :, 0:DH]).then_inc(dup, 1)
                        nc.gpsimd.tensor_copy(v_ones[:, t, :, 0:DH],
                                              ctx_sb[:, t, D:2 * D].rearrange("p (h d) -> p h d", h=H))
                    for t in range(T):
                        pool.wait_ge(split, b * (NCTX + T) + NCTX + t + 1)
                        nc.gpsimd.tensor_copy(q_stack[:, t, :, DH:2 * DH], q_stack[:, t, :, 0:DH])
                        ks = key_source(NCTX + t)
                        pool.drain()
                        nc.gpsimd.tensor_copy(ks[:, :, 2 * DH:3 * DH], ks[:, :, 0:DH]).then_inc(dup, 1)

                @block.scalar
                def _(act):
                    def evacuate(i):
                        kind, t = items[i]
                        act.wait_ge(tr_psum, b * NI + i + 1)
                        dst = kT if kind == "k" else qT
                        nc.scalar.activation(dst[:, 0:4, t * P:(t + 1) * P],
                                             bank(item_banks(i)[0]).rearrange("p (a n) -> p a n", a=4),
                                             ACT.Copy).then_inc(tr_act, 1)

                    for t in range(NCTX):
                        evacuate(t)
                    act.wait_ge(xT_psum, 2 * b + 1)
                    nc.scalar.activation(xT[:, 0, :], bank(2), ACT.Copy).then_inc(xT_act, 1)
                    for t in range(T):
                        act.wait_ge(v_psum, b * T + t + 1)
                        nc.scalar.activation(v_ones[:, NCTX + t, :, 0:DH],
                                             bank(3 + 2 * (t % 2))[:, 0:D].rearrange("p (h d) -> p h d", h=H),
                                             ACT.Copy).then_inc(v_copied, 1)
                        if t >= 1:
                            evacuate(NCTX + 2 * t - 2)
                            evacuate(NCTX + 2 * t - 1)
                    evacuate(NI - 2)
                    evacuate(NI - 1)

                @block.tensor
                def _(pe):
                    def transposes(i):
                        kind, t = items[i]
                        if i >= 2:
                            pe.wait_ge(tr_act, b * NI + i - 1)
                            pe.wait_ge(tr_dve, b * NI + i - 1)
                        src = key_source(t) if kind == "k" else q_stack[:, t]
                        src = src.rearrange("p h r -> p (h r)")
                        for p in range(PAIRS):
                            dst = bank(item_banks(i)[p // 4])[:, (p % 4) * P:(p % 4 + 1) * P]
                            last = nc.tensor.transpose(dst, src[:, p * P:(p + 1) * P], g["ident"][:])
                        last.then_inc(tr_psum, 1)

                    for t in range(NCTX):
                        pe.wait_ge(dup, b * (NCTX + T) + t + 1)
                        transposes(t)
                    pe.wait_ge(xn_ready, (b + 1) * T)
                    for c in range(s.DC):
                        for t in range(T):
                            last = nc.tensor.transpose(bank(2 + c)[:, t * P:(t + 1) * P],
                                                       xn[:, t, c * P:(c + 1) * P], g["ident"][:])
                        last.then_inc(xT_psum, 1)
                    pe.wait_ge(xT_act, b + 1)
                    pe.wait_ge(xT_dve, b + 1)
                    for t in range(T + 1):
                        if t < T:
                            if t >= 2:
                                pe.wait_ge(split, b * (NCTX + T) + NCTX + t - 1)
                                pe.wait_ge(v_copied, b * T + t - 1)
                            for c in range(s.DC):
                                last = nc.tensor.matmul(bank(2 + 2 * (t % 2))[:, 0:2 * D], xT[:, c, t * P:(t + 1) * P],
                                                        w_qkv[:, c, 0:2 * D], start=(c == 0), stop=(c == s.DC - 1))
                            last.then_inc(qk_psum, 1)
                            for c in range(s.DC):
                                last = nc.tensor.matmul(bank(3 + 2 * (t % 2))[:, 0:D], xT[:, c, t * P:(t + 1) * P],
                                                        w_qkv[:, c, 2 * D:3 * D], start=(c == 0), stop=(c == s.DC - 1))
                            last.then_inc(v_psum, 1)
                        if t >= 1:
                            pe.wait_ge(dup, b * (NCTX + T) + NCTX + t)
                            transposes(NCTX + 2 * t - 2)
                            transposes(NCTX + 2 * t - 1)

            UNITS = H * KT // 2
            MAXES = H * T * 2
            STEPS = KT // 2
            with nc.Block() as block:
                @block.tensor
                def _(pe):
                    def max_scores(n):
                        h, r = divmod(n, 2 * T)
                        t, half = divmod(r, 2)
                        if n >= 2:
                            pe.wait_ge(max_read, b * MAXES + n - 1)
                        row = (h % 2) * ST
                        nc.tensor.matmul(bank(4 + n % 2), qT[row:row + K_SCORE, h // 2, t * P:(t + 1) * P],
                                         kT[row:row + K_SCORE, h // 2, half * BANK:(half + 1) * BANK],
                                         start=True, stop=True).then_inc(max_psum, 1)

                    def stack_with_max(quad):
                        pe.wait_ge(negmax, b * QUADS + quad + 1)
                        for pair in range(2):
                            n = b * PAIRS + 2 * quad + pair
                            if 2 * quad + pair >= 1:
                                pe.wait_ge(qm_ready, n)
                            for t in range(T):
                                src = q_stack[:, t].rearrange("p h r -> p (h r)")
                                p = 2 * quad + pair
                                last = nc.tensor.transpose(bank(7)[:, t * P:(t + 1) * P],
                                                           src[:, p * P:(p + 1) * P], g["ident"][:])
                            last.then_inc(qm_psum, 1)

                    def scores(n):
                        quad, r = divmod(n, 4 * STEPS)
                        step, j = divmod(r, 4)
                        if n >= 2:
                            pe.wait_ge(exp_done, b * UNITS + n - 1)
                        pe.wait_ge(qm_ready, b * PAIRS + 2 * quad + j // 2 + 1)
                        row = (j % 2) * ST
                        for i in range(2):
                            kt = 2 * step + i
                            last = nc.tensor.matmul(bank(2 * (n % 2) + i),
                                                    kT[row:row + M_ROW + 1, 2 * quad + j // 2, kt * P:(kt + 1) * P],
                                                    qmT[row:row + M_ROW + 1, quad % 2, j // 2, :], start=True, stop=True)
                        last.then_inc(s_psum, 1)

                    def weigh_values(group):
                        quad, step = divmod(group, STEPS)
                        pe.wait_ge(exp_done, b * UNITS + 4 * group + 4)
                        if step == 0 and quad >= 1:
                            pe.wait_ge(norm_done, b * QUADS + quad)
                        for i in range(2):
                            kt = 2 * step + i
                            for j in range(4):
                                n = 4 * group + j
                                last = nc.tensor.matmul(bank(6)[32 * j:32 * j + 32, :], v_ones[:, kt, 4 * quad + j, :],
                                                        probs[:, n % PT_RING, i * BANK:(i + 1) * BANK],
                                                        start=(kt == 0), stop=(kt == KT - 1), tile_position=(0, 32 * j),
                                                        skip_group_check=True)
                        last.then_inc(pv_done, 1)

                    for n in range(8 * T):
                        max_scores(n)
                    stack_with_max(0)
                    for quad in range(QUADS):
                        for step in range(STEPS):
                            for j in range(4):
                                u = 4 * step + j
                                scores(4 * STEPS * quad + u)
                                if quad + 1 < QUADS:
                                    max_scores(8 * T * (quad + 1) + 2 * u)
                                    max_scores(8 * T * (quad + 1) + 2 * u + 1)
                            if step >= 1:
                                weigh_values(STEPS * quad + step - 1)
                        weigh_values(STEPS * quad + STEPS - 1)
                        if quad + 1 < QUADS:
                            stack_with_max(quad + 1)

                @block.scalar
                def _(act):
                    for n in range(UNITS):
                        act.wait_ge(s_psum, b * UNITS + n + 1)
                        if n >= PT_RING:
                            act.wait_ge(pv_done, b * (UNITS // 4) + n // 4 - 1)
                        nc.scalar.activation(probs[:, n % PT_RING, :], wide(2 * (n % 2)), ACT.Exp,
                                             scale=SCALE).then_inc(exp_done, 1)

                @block.vector
                def _(dve):
                    def normalize(quad):
                        dve.wait_ge(pv_done, b * (UNITS // 4) + STEPS * (quad + 1))
                        nc.vector.stream_shuffle(denom[:], bank(6), [DH + i % DH for i in range(32)])
                        dve.drain()
                        nc.vector.reciprocal(denom[:], denom[:])
                        dve.drain()
                        nc.vector.tensor_tensor(oT[:, quad, :], bank(6), denom[:], ALU.mult).then_inc(norm_done, 1)

                    for quad in range(QUADS):
                        for n in range(8 * T * quad, 8 * T * (quad + 1)):
                            h, r = divmod(n, 2 * T)
                            t, half = divmod(r, 2)
                            dve.wait_ge(max_psum, b * MAXES + n + 1)
                            nc.vector.reduce_max(tile_max[:, t, h, half:half + 1], bank(4 + n % 2), AX_X).then_inc(max_read, 1)
                        dve.drain()
                        for t in range(T):
                            last = nc.vector.tensor_reduce(
                                out=q_stack[:, t, 4 * quad:4 * quad + 4, M_ROW:M_ROW + 1].bitcast(F32R),
                                in_=tile_max[:, t, 4 * quad:4 * quad + 4, :], axis=AX_X, op=ALU.max, negate=True)
                        last.then_inc(negmax, 1)
                        for pair in range(2):
                            dve.wait_ge(qm_psum, b * PAIRS + 2 * quad + pair + 1)
                            nc.vector.tensor_copy(qmT[:, quad % 2, pair, :], bank(7)).then_inc(qm_ready, 1)
                        if quad >= 1:
                            normalize(quad - 1)
                    normalize(QUADS - 1)

            with nc.Block() as block:
                @block.gpsimd
                def _(pool):
                    for t in range(T):
                        nc.gpsimd.tensor_tensor(x_bias[:, t, :], x_b[:, t, :], b_proj[:], ALU.add).then_inc(bias_added, 1)
                    for t in range(T):
                        pool.wait_ge(resid, b * T + t + 1)
                        nc.gpsimd.tensor_tensor(x_bias[:, t, :], x_b[:, t, :], b_out[:], ALU.add).then_inc(bias_added, 1)

                @block.tensor
                def _(pe):
                    for t in range(T):
                        for q in range(QUADS):
                            last = nc.tensor.matmul(bank(t)[:, 0:D], oT[:, q, t * P:(t + 1) * P], w_proj[:, q, :],
                                                    start=(q == 0), stop=(q == QUADS - 1))
                        last.then_inc(proj_psum, 1)
                    pe.wait_ge(xn2_ready, (b + 1) * T)
                    for c in range(s.DC):
                        for t in range(T):
                            last = nc.tensor.transpose(bank(4 + c)[:, t * P:(t + 1) * P],
                                                       xn[:, t, c * P:(c + 1) * P], g["ident"][:])
                        last.then_inc(xT2_psum, 1)
                    pe.wait_ge(xT2_act, b + 1)
                    pe.wait_ge(xT2_dve, b + 1)
                    for c in range(s.DC):
                        last = nc.tensor.matmul(bank(6), w_in[:, c, :], xT[:, c, :], start=(c == 0), stop=(c == s.DC - 1))
                    last.then_inc(sin_psum, 1)
                    pe.wait_ge(unit_used, (b + 1) * 8)
                    for t in range(T):
                        nc.tensor.matmul(bank(t)[:, 0:D], gated[:, t * P:(t + 1) * P], w_out[:],
                                         start=True, stop=True).then_inc(ffn_psum, 1)

                @block.scalar
                def _(act):
                    act.wait_ge(xT2_psum, 2 * b + 1)
                    nc.scalar.activation(xT[:, 0, :], bank(4), ACT.Copy).then_inc(xT2_act, 1)
                    act.wait_ge(sin_ready, b + 1)
                    for i in range(8):
                        if i >= 2:
                            act.wait_ge(unit_used, 8 * b + i - 1)
                        nc.scalar.activation(units[:, i % 2, :], s_in[:], ACT.Relu, bias=b1[:, i:i + 1],
                                             scale=w1[:, i:i + 1]).then_inc(unit_ready, 1)

                @block.vector
                def _(dve):
                    for t in range(T):
                        dve.wait_ge(proj_psum, b * T + t + 1)
                        dve.wait_ge(bias_added, 2 * b * T + t + 1)
                        nc.vector.scalar_tensor_tensor(out=x_b[:, t, :], in0=bank(t)[:, 0:D], scalar=g["gates"][:, 0:1],
                                                       in1=x_bias[:, t, :], op0=ALU.mult, op1=ALU.add).then_inc(resid, 1)
                    dve.drain()
                    norm.statistics(dve, lambda t: x_b[:, t, :], LN_EPS)
                    for t in range(T):
                        norm.apply(xn[:, t, :], x_b[:, t, :], t).then_inc(xn2_ready, 1)
                    dve.wait_ge(xT2_psum, 2 * b + 2)
                    nc.vector.tensor_copy(xT[:, 1, :], bank(5)).then_inc(xT2_dve, 1)
                    dve.wait_ge(sin_psum, b + 1)
                    nc.vector.tensor_scalar(s_in[:], bank(6), b_in[:, 0:1], None, ALU.add).then_inc(sin_ready, 1)
                    for i in range(8):
                        dve.wait_ge(unit_ready, 8 * b + i + 1)
                        if i == 0:
                            nc.vector.tensor_scalar(gated[:], units[:, 0, :], w2[:, 0:1], b2[:, 0:1], ALU.mult,
                                                    ALU.add).then_inc(unit_used, 1)
                        else:
                            dve.drain()
                            nc.vector.scalar_tensor_tensor(out=gated[:], in0=units[:, i % 2, :], scalar=w2[:, i:i + 1],
                                                           in1=gated[:], op0=ALU.mult, op1=ALU.add).then_inc(unit_used, 1)
                    dve.wait_ge(bias_added, 2 * (b + 1) * T)
                    for t in range(T):
                        dve.wait_ge(ffn_psum, b * T + t + 1)
                        nc.vector.scalar_tensor_tensor(out=x_b[:, t, :], in0=bank(t)[:, 0:D], scalar=g["gates"][:, 1:2],
                                                       in1=x_bias[:, t, :], op0=ALU.mult, op1=ALU.add).then_inc(ffn_done, 1)


def layer1(nc, s, g, bank, dram):
    T, H, DH, N, D = s.TT, s.H, s.DH1, s.N, s.D
    PAIRS = H // 2
    KT = s.KT1
    SCALE = float(DH) ** -0.5
    RING = 8
    UNITS = 2 * (KT + 1)
    MAXES = 2 * T + 1

    with ExitStack() as ctx:
        def sb(name, shape, dt=F32):
            return ctx.enter_context(nc.sbuf_tensor("l1_" + name, shape, dt))

        def sem(name):
            return ctx.enter_context(nc.semaphore(name))

        wq = sb("wq", [P, s.DC, s.I1])
        wk = sb("wk", [P, s.CC, s.I1])
        wv = sb("wv", [P, s.CC, s.I1])
        wo = sb("wo", [P, PAIRS, D])
        null_k = sb("null_k", [P, DH])
        null_col = sb("null_col", [P, 1])
        null_v = sb("null_v", [1, DH])
        w_null = sb("w_null", [P, s.DC, H])
        w_null_tmp = sb("w_null_tmp", [P, H, DH])
        ln_scale = sb("ln_scale", [P, D])
        ln_bias = sb("ln_bias", [P, D])
        ctxT = sb("ctxT", [P, s.CC, s.M])
        xn = sb("xn", [P, T, D])
        xT = sb("xT", [P, s.DC, N])
        v_sb = sb("v_sb", [P, KT, s.I1])
        s_null = sb("s_null", [P, T, H])
        q1 = sb("q1", [P, 2, 2, N], F32R)
        q2 = sb("q2", [P, 2, 2, N], F32R)
        k1 = sb("k1", [P, 2, 2, s.M], F32R)
        k2 = sb("k2", [P, 2, 2, s.M], F32R)
        null1 = sb("null1", [P, P], F32R)
        null2 = sb("null2", [P, P], F32R)
        probs = sb("probs", [P, RING, N])
        null_p = sb("null_p", [1, 2, N])
        p_sum = sb("p_sum", [P, 2, N])
        ones = sb("ones", [P, DH])
        denom = sb("denom", [P, N])
        oT = sb("oT", [P, PAIRS, N])
        tile_max = sb("tile_max", [P, 2, T])
        max_tmp = sb("max_tmp", [P, 2, T])
        max_cols = sb("max_cols", [P, T, P])
        x_bias = sb("x_bias", [P, T, D])
        out_n = sb("out_n", [P, T, D])
        stats = sb("stats", [P, T, 6])
        mv = sb("mv", [P, T, 2])
        work = sb("work", [P, 4, T])
        norm = Norm(nc, T, stats, mv, work)

        loaded = sem("l1_weights_loaded")
        with nc.Block() as block:
            @block.sync
            def _(sp):
                sp.dma_start(wq[:], dram["wq"].rearrange("(c p) n -> p c n", p=P)).then_inc(loaded, 16)
                sp.dma_start(wk[:], dram["wkv"][:, 0:s.I1].rearrange("(c p) n -> p c n", p=P)).then_inc(loaded, 16)
                sp.dma_start(wv[:], dram["wkv"][:, s.I1:2 * s.I1].rearrange("(c p) n -> p c n", p=P)).then_inc(loaded, 16)
                sp.dma_start(wo[:], dram["wo"].rearrange("(c p) n -> p c n", p=P)).then_inc(loaded, 16)
                sp.dma_start(null_k[:], dram["null_kv"][0].partition_broadcast(P)).then_inc(loaded, 16)
                sp.dma_start(null_col[0:DH, :], dram["null_kv"][0].unsqueeze(1)).then_inc(loaded, 16)
                sp.dma_start(null_col[DH:2 * DH, :], dram["null_kv"][0].unsqueeze(1)).then_inc(loaded, 16)
                sp.dma_start(null_v[:], dram["null_kv"][1:2, :]).then_inc(loaded, 16)
                sp.dma_start(ln_scale[:], dram["ln_scale"].partition_broadcast(P)).then_inc(loaded, 16)
                sp.dma_start(ln_bias[:], dram["ln_bias"].partition_broadcast(P)).then_inc(loaded, 16)
                sp.wait_ge(loaded, 160)

            @block.gpsimd
            def _(pool):
                nc.gpsimd.memset(null1[:].bitcast(F32), 0.0)
                nc.gpsimd.memset(null2[:].bitcast(F32), 0.0)
                nc.gpsimd.memset(ones[:], 1.0)
                nc.gpsimd.memset(max_cols[:], 0.0)
                pool.drain()
                nc.gpsimd.memset(k2[DH:DH + 1].bitcast(F32), 1.0)
                pool.drain()
                nc.gpsimd.memset(null2[DH:DH + 1, 0:1].bitcast(F32), 1.0)

        with nc.Block() as block:
            @block.vector
            def _(dve):
                nc.vector.tensor_scalar(ln_scale[:], ln_scale[:], g["gates"][:, 2:3], None, ALU.mult)
                nc.vector.tensor_scalar(ln_bias[:], ln_bias[:], g["gates"][:, 2:3], None, ALU.mult)
                for c in range(s.DC):
                    nc.vector.tensor_tensor(w_null_tmp[:], wq[:, c, :].rearrange("p (h k) -> p h k", h=H),
                                            null_k[:].unsqueeze(1).to_broadcast([P, H, DH]), ALU.mult)
                    dve.drain()
                    nc.vector.reduce_sum(w_null[:, c, :], w_null_tmp[:], AX_X)
                    dve.drain()
                nc.vector.tensor_copy(null1[:, 0:1], null_col[:])
                dve.drain()
                nc.vector.tensor_copy(null2[0:DH, 0:1], null_col[0:DH, :])
                nc.vector.tensor_tensor(null1[DH:P, 0:1], null_col[DH:P, :], null1[DH:P, 0:1].bitcast(F32), ALU.subtract)

        ctx_ready = sem("l1_ctx_ready")
        xn_ready = sem("l1_xn_ready")
        xT_psum = sem("l1_xT_psum")
        xT_act = sem("l1_xT_act")
        xT_dve = sem("l1_xT_dve")
        v_psum = sem("l1_v_psum")
        v_act = sem("l1_v_act")
        v_dve = sem("l1_v_dve")
        null_psum = sem("l1_null_psum")
        null_read = sem("l1_null_read")

        qk_psum = sem("l1_qk_psum")
        hi_done = sem("l1_hi_done")
        lo_done = sem("l1_lo_done")
        max_psum = sem("l1_max_psum")
        max_read = sem("l1_max_read")
        negmax = sem("l1_negmax")
        negmaxT = sem("l1_negmaxT")
        max_rows = sem("l1_max_rows")
        s_psum = sem("l1_s_psum")
        exp_done = sem("l1_exp_done")
        pv_done = sem("l1_pv_done")
        summed = sem("l1_summed")
        den_psum = sem("l1_den_psum")
        norm_done = sem("l1_norm_done")

        out_psum = sem("l1_out_psum")
        out_normed = sem("l1_out_normed")
        scaled = sem("l1_scaled")

        for b in range(s.B):
            x_b = g["x"][:, b * T:(b + 1) * T, :]

            with nc.Block() as block:
                @block.sync
                def _(sp):
                    sp.dma_start(ctxT[:], dram["ctxT"][b].rearrange("(c p) n -> p c n", p=P)).then_inc(ctx_ready, 16)

                @block.tensor
                def _(pe):
                    pe.wait_ge(ctx_ready, 16 * (b + 1))
                    for n in range(2 * KT):
                        kt, half = divmod(n, 2)
                        if n >= 4:
                            pe.wait_ge(v_act if n % 2 else v_dve, b * KT + (n - 4) // 2 + 1)
                        for c in range(s.CC):
                            last = nc.tensor.matmul(bank(n % 4), ctxT[:, c, kt * P:(kt + 1) * P],
                                                    wv[:, c, half * BANK:(half + 1) * BANK],
                                                    start=(c == 0), stop=(c == s.CC - 1))
                        last.then_inc(v_psum, 1)
                    pe.wait_ge(xn_ready, (b + 1) * T)
                    for c in range(s.DC):
                        for t in range(T):
                            last = nc.tensor.transpose(bank(4 + c)[:, t * P:(t + 1) * P],
                                                       xn[:, t, c * P:(c + 1) * P], g["ident"][:])
                        last.then_inc(xT_psum, 1)
                    pe.wait_ge(xT_act, b + 1)
                    pe.wait_ge(xT_dve, b + 1)
                    for t in range(T):
                        for c in range(s.DC):
                            last = nc.tensor.matmul(bank(6)[:, t * H:(t + 1) * H], xT[:, c, t * P:(t + 1) * P],
                                                    w_null[:, c, :], start=(c == 0), stop=(c == s.DC - 1))
                    last.then_inc(null_psum, 1)

                @block.scalar
                def _(act):
                    for n in range(1, 2 * KT, 2):
                        act.wait_ge(v_psum, 2 * KT * b + n + 1)
                        nc.scalar.activation(v_sb[:, n // 2, BANK:2 * BANK], bank(n % 4), ACT.Copy).then_inc(v_act, 1)
                    act.wait_ge(xT_psum, 2 * b + 1)
                    nc.scalar.activation(xT[:, 0, :], bank(4), ACT.Copy).then_inc(xT_act, 1)

                @block.vector
                def _(dve):
                    norm.statistics(dve, lambda t: x_b[:, t, :], LN_EPS)
                    for t in range(T):
                        norm.apply(xn[:, t, :], x_b[:, t, :], t).then_inc(xn_ready, 1)
                    for n in range(0, 2 * KT, 2):
                        dve.wait_ge(v_psum, 2 * KT * b + n + 1)
                        nc.vector.tensor_copy(v_sb[:, n // 2, 0:BANK], bank(n % 4)).then_inc(v_dve, 1)
                    dve.wait_ge(xT_psum, 2 * b + 2)
                    nc.vector.tensor_copy(xT[:, 1, :], bank(5)).then_inc(xT_dve, 1)
                    dve.wait_ge(null_psum, b + 1)
                    nc.vector.tensor_copy(s_null[:], bank(6)[:, 0:T * H].rearrange("p (t h) -> p t h", t=T)).then_inc(null_read, 1)

            with nc.Block() as block:
                @block.tensor
                def _(pe):
                    def project(p):
                        if p >= 1:
                            pe.wait_ge(lo_done, b * PAIRS + p)
                        for c in range(s.DC):
                            nc.tensor.matmul(bank(6), wq[:, c, p * P:(p + 1) * P], xT[:, c, :],
                                             start=(c == 0), stop=(c == s.DC - 1))
                        for c in range(s.CC):
                            last = nc.tensor.matmul(bank(7), wk[:, c, p * P:(p + 1) * P], ctxT[:, c, :],
                                                    start=(c == 0), stop=(c == s.CC - 1))
                        last.then_inc(qk_psum, 1)

                    def max_bank(p, i):
                        n = p * MAXES + i
                        if n >= 2:
                            back_p, back_i = divmod(n - 2, MAXES)
                            if back_i < MAXES - 1:
                                pe.wait_ge(max_read, b * PAIRS * 2 * T + back_p * 2 * T + back_i + 1)
                            else:
                                pe.wait_ge(max_rows, b * PAIRS + back_p + 1)
                        return bank(2 + n % 2)

                    def max_scores(p, i):
                        j, t = divmod(i, T)
                        if i == 0:
                            pe.wait_ge(lo_done, b * PAIRS + p + 1)
                        out = max_bank(p, i)
                        nc.tensor.matmul(out, q1[:, p % 2, j, t * P:(t + 1) * P], k1[:, p % 2, j, :],
                                         start=True, stop=False)
                        nc.tensor.matmul(out, q2[0:DH, p % 2, j, t * P:(t + 1) * P], k2[0:DH, p % 2, j, :],
                                         start=False, stop=True).then_inc(max_psum, 1)

                    def transpose_max(p):
                        pe.wait_ge(negmax, b * PAIRS + p + 1)
                        out = max_bank(p, MAXES - 1)
                        for t in range(T):
                            last = nc.tensor.transpose(out[:, t * P:(t + 1) * P], max_cols[:, t, :], g["ident"][:])
                        last.then_inc(negmaxT, 1)

                    def scores(p, u):
                        kt, j = divmod(u, 2)
                        n = p * UNITS + u
                        if n >= 2:
                            pe.wait_ge(exp_done, b * PAIRS * UNITS + n - 1)
                        if u == 0:
                            pe.wait_ge(max_rows, b * PAIRS + p + 1)
                        if kt < KT:
                            first, second = k1[:, p % 2, j, kt * P:(kt + 1) * P], k2[0:DH + 1, p % 2, j, kt * P:(kt + 1) * P]
                        else:
                            first, second = null1[:], null2[0:DH + 1, :]
                        nc.tensor.matmul(bank(n % 2), first, q1[:, p % 2, j, :], start=True, stop=False)
                        nc.tensor.matmul(bank(n % 2), second, q2[0:DH + 1, p % 2, j, :],
                                         start=False, stop=True).then_inc(s_psum, 1)

                    def weigh_values(p, kt):
                        pe.wait_ge(exp_done, b * PAIRS * UNITS + p * UNITS + 2 * kt + 2)
                        if kt == 0 and p >= 1:
                            pe.wait_ge(norm_done, b * PAIRS + p)
                        for j in range(2):
                            h = 2 * p + j
                            if kt < KT:
                                lhsT, rhs = v_sb[:, kt, h * DH:(h + 1) * DH], probs[:, (p * 2 * KT + 2 * kt + j) % RING, :]
                            else:
                                lhsT, rhs = null_v[:], null_p[:, j, :]
                            last = nc.tensor.matmul(bank(4)[j * DH:(j + 1) * DH, :], lhsT, rhs, start=(kt == 0),
                                                    stop=(kt == KT), tile_position=(0, j * DH), skip_group_check=True)
                        last.then_inc(pv_done, 1)

                    def denominators(p):
                        pe.wait_ge(summed, b * PAIRS + p + 1)
                        for j in range(2):
                            last = nc.tensor.matmul(bank(5)[j * DH:(j + 1) * DH, :], ones[:], p_sum[:, j, :], start=True,
                                                    stop=True, tile_position=(0, j * DH), skip_group_check=True)
                        last.then_inc(den_psum, 1)

                    project(0)
                    project(1)
                    for i in range(2 * T):
                        max_scores(0, i)
                    transpose_max(0)
                    for p in range(PAIRS):
                        for kt in range(KT + 1):
                            for j in range(2):
                                u = 2 * kt + j
                                scores(p, u)
                                if p + 1 < PAIRS and u < 2 * T:
                                    max_scores(p + 1, u)
                            if kt >= 1:
                                weigh_values(p, kt - 1)
                        weigh_values(p, KT)
                        if p + 2 < PAIRS:
                            project(p + 2)
                        denominators(p)
                        if p + 1 < PAIRS:
                            transpose_max(p + 1)

                @block.scalar
                def _(act):
                    def round_high(p):
                        act.wait_ge(qk_psum, b * PAIRS + p + 1)
                        q, k, i = bank(6), bank(7), p % 2
                        for j in range(2):
                            rows = slice(j * DH, (j + 1) * DH)
                            nc.scalar.activation(q1[0:DH, i, j, :], q[rows, :], ACT.Copy)
                            nc.scalar.activation(q1[DH:P, i, j, :], q[rows, :], ACT.Copy)
                            nc.scalar.activation(k1[rows, i, j, :], k[rows, :], ACT.Copy)
                            last = nc.scalar.activation(k2[0:DH, i, j, :], k[rows, :], ACT.Copy)
                        last.then_inc(hi_done, 1)

                    def place_max(p):
                        act.wait_ge(negmaxT, b * PAIRS + p + 1)
                        src = bank(2 + (p * MAXES + MAXES - 1) % 2)
                        for j in range(2):
                            last = nc.scalar.activation(q2[DH:DH + 1, p % 2, j, :], src[j * DH:j * DH + 1, :], ACT.Copy)
                        last.then_inc(max_rows, 1)

                    round_high(0)
                    round_high(1)
                    place_max(0)
                    for p in range(PAIRS):
                        for u in range(UNITS):
                            kt, j = divmod(u, 2)
                            n = p * UNITS + u
                            act.wait_ge(s_psum, b * PAIRS * UNITS + n + 1)
                            if kt < KT:
                                m = p * 2 * KT + u
                                if m >= RING:
                                    back_p, back_u = divmod(m - RING, 2 * KT)
                                    act.wait_ge(pv_done, b * PAIRS * (KT + 1) + back_p * (KT + 1) + back_u // 2 + 1)
                                    act.wait_ge(summed, b * PAIRS + back_p + 1)
                                nc.scalar.activation(probs[:, m % RING, :], bank(n % 2), ACT.Exp, scale=SCALE).then_inc(exp_done, 1)
                            else:
                                if p >= 1 and j == 0:
                                    act.wait_ge(pv_done, b * PAIRS * (KT + 1) + p * (KT + 1))
                                    act.wait_ge(summed, b * PAIRS + p)
                                nc.scalar.activation(null_p[:, j, :], bank(n % 2)[0:1, :], ACT.Exp, scale=SCALE).then_inc(exp_done, 1)
                        if p + 2 < PAIRS:
                            round_high(p + 2)
                        if p + 1 < PAIRS:
                            place_max(p + 1)

                @block.gpsimd
                def _(pool):
                    for p in range(PAIRS):
                        if p >= 1:
                            pool.wait_ge(den_psum, b * PAIRS + p)
                        for kt in range(1, KT):
                            pool.wait_ge(exp_done, b * PAIRS * UNITS + p * UNITS + 2 * kt + 2)
                            for j in range(2):
                                m = p * 2 * KT + 2 * kt + j
                                first = probs[:, (m - 2) % RING, :] if kt == 1 else p_sum[:, j, :]
                                nc.gpsimd.tensor_tensor(p_sum[:, j, :], first, probs[:, m % RING, :], ALU.add)
                            pool.drain()
                        pool.wait_ge(exp_done, b * PAIRS * UNITS + (p + 1) * UNITS)
                        for j in range(2):
                            last = nc.gpsimd.tensor_tensor(p_sum[0:1, j, :], p_sum[0:1, j, :], null_p[:, j, :], ALU.add)
                        last.then_inc(summed, 1)

                @block.vector
                def _(dve):
                    def split_low(p):
                        dve.wait_ge(hi_done, b * PAIRS + p + 1)
                        q, k, i = bank(6), bank(7), p % 2
                        for j in range(2):
                            rows, other = slice(j * DH, (j + 1) * DH), slice((1 - j) * DH, (2 - j) * DH)
                            nc.vector.tensor_tensor(q2[0:DH, i, j, :], q[rows, :], q1[rows, i, j, :].bitcast(F32), ALU.subtract)
                            last = nc.vector.tensor_tensor(k1[other, i, j, :], k[rows, :], k1[rows, i, j, :].bitcast(F32), ALU.subtract)
                        last.then_inc(lo_done, 1)

                    def maxima(p):
                        for i in range(2 * T):
                            j, t = divmod(i, T)
                            dve.wait_ge(max_psum, b * PAIRS * 2 * T + p * 2 * T + i + 1)
                            nc.vector.reduce_max(tile_max[:, j, t:t + 1], bank(2 + (p * MAXES + i) % 2), AX_X).then_inc(max_read, 1)
                        dve.drain()
                        nc.vector.tensor_tensor(max_tmp[:], tile_max[:],
                                                s_null[:, :, 2 * p:2 * p + 2].rearrange("p t j -> p j t"), ALU.max)
                        dve.drain()
                        nc.vector.tensor_scalar(max_cols[:, :, 0:P:DH].bitcast(F32R), max_tmp[:].rearrange("p j t -> p t j"),
                                                -1.0, None, ALU.mult).then_inc(negmax, 1)

                    def normalize(p):
                        dve.wait_ge(den_psum, b * PAIRS + p + 1)
                        nc.vector.reciprocal(denom[:], bank(5))
                        dve.drain()
                        nc.vector.tensor_tensor(oT[:, p, :], bank(4), denom[:], ALU.mult).then_inc(norm_done, 1)

                    split_low(0)
                    split_low(1)
                    maxima(0)
                    for p in range(PAIRS):
                        if p + 1 < PAIRS:
                            maxima(p + 1)
                        if p + 2 < PAIRS:
                            split_low(p + 2)
                        normalize(p)

            with nc.Block() as block:
                @block.tensor
                def _(pe):
                    for t in range(T):
                        for p in range(PAIRS):
                            last = nc.tensor.matmul(bank(t)[:, 0:D], oT[:, p, t * P:(t + 1) * P], wo[:, p, :],
                                                    start=(p == 0), stop=(p == PAIRS - 1))
                        last.then_inc(out_psum, 1)

                @block.vector
                def _(dve):
                    dve.wait_ge(out_psum, (b + 1) * T)
                    norm.statistics(dve, lambda t: bank(t)[:, 0:D], LN_OUT_EPS)
                    for t in range(T):
                        norm.apply(out_n[:, t, :], bank(t)[:, 0:D], t).then_inc(out_normed, 1)
                    for t in range(T):
                        dve.wait_ge(scaled, b * T + t + 1)
                        nc.vector.tensor_tensor(x_b[:, t, :], x_bias[:, t, :], out_n[:, t, :], ALU.add)

                @block.gpsimd
                def _(pool):
                    for t in range(T):
                        nc.gpsimd.tensor_tensor(x_bias[:, t, :], x_b[:, t, :], ln_bias[:], ALU.add)
                    for t in range(T):
                        pool.wait_ge(out_normed, b * T + t + 1)
                        nc.gpsimd.tensor_tensor(out_n[:, t, :], out_n[:, t, :], ln_scale[:], ALU.mult).then_inc(scaled, 1)


def experts(nc, s, g, bank, dram, out):
    T, D, E, N, B = s.T, s.D, s.E, s.N, s.B
    TB = s.TT
    NB = T // TB

    with ExitStack() as ctx:
        def sb(name, shape, dt=F32):
            return ctx.enter_context(nc.sbuf_tensor("moe_" + name, shape, dt))

        def sem(name):
            return ctx.enter_context(nc.semaphore(name))

        w_router = sb("w_router", [P, s.DC, E])
        b_router = sb("b_router", [P, E])
        xn = sb("xn", [P, T, D])
        xT = sb("xT", [P, s.DC, T * P])
        accT = sb("accT", [P, s.DC, T * P])
        w1 = sb("w1", [P, 2, s.DC, s.F])
        w3 = sb("w3", [P, 2, s.DC, s.F])
        w2 = sb("w2", [P, 2, s.FT, D])
        logits = sb("logits", [P, T, E])
        cmp = sb("cmp", [P, T, E, E])
        tie = sb("tie", [P, T, E, E])
        before = sb("before", [P, E, E])
        rank = sb("rank", [P, T, E])
        first = sb("first", [P, T, E])
        second = sb("second", [P, T, E])
        top = sb("top", [P, 4, T])
        route = sb("route", [P, T, E])
        xs = sb("xs", [P, s.DC, N])
        gate = sb("gate", [P, 2, N])
        hid = sb("hid", [P, 2, N])
        stats = sb("stats", [P, TB, 6])
        mv = sb("mv", [P, TB, 2])
        work = sb("work", [P, 4, TB])
        norm = Norm(nc, TB, stats, mv, work)

        loaded = sem("moe_router_loaded")
        w_ready = [sem(f"moe_w_ready_{i}") for i in range(2)]
        w_used = sem("moe_w_used")
        xn_ready = sem("moe_xn_ready")
        xT_psum = sem("moe_xT_psum")
        xT_act = sem("moe_xT_act")
        xT_dve = sem("moe_xT_dve")
        lg_psum = sem("moe_lg_psum")
        tops = sem("moe_tops")
        exped = sem("moe_exped")

        with nc.Block() as block:
            @block.sync
            def _(sp):
                sp.dma_start(w_router[:], dram["w_router"].rearrange("(c p) n -> p c n", p=P)).then_inc(loaded, 16)
                sp.dma_start(b_router[:], dram["b_router"].partition_broadcast(P)).then_inc(loaded, 16)
                for e in range(2):
                    sp.dma_start(w1[:, e], dram["moe_w1"][e].rearrange("(c p) n -> p c n", p=P)).then_inc(w_ready[e % 2], 16)
                    sp.dma_start(w3[:, e], dram["moe_w3"][e].rearrange("(c p) n -> p c n", p=P)).then_inc(w_ready[e % 2], 16)
                    sp.dma_start(w2[:, e], dram["moe_w2"][e].rearrange("(c p) n -> p c n", p=P)).then_inc(w_ready[e % 2], 16)

            @block.gpsimd
            def _(pool):
                nc.gpsimd.memset(before[:], 1.0)
                pool.drain()
                nc.gpsimd.affine_select(out=before[:], in_=before[:], compare_op=ALU.is_gt, fill=0.0, base=0,
                                        pattern=[[1, E], [-1, E]], channel_multiplier=0)

            @block.vector
            def _(dve):
                for b in range(NB):
                    rows = g["x"][:, b * TB:(b + 1) * TB, :]
                    norm.statistics(dve, lambda t: rows[:, t, :], LN_EPS)
                    for t in range(TB):
                        norm.apply(xn[:, b * TB + t, :], rows[:, t, :], t).then_inc(xn_ready, 1)
                    if b >= 1:
                        dve.wait_ge(xT_psum, 2 * b)
                        nc.vector.tensor_copy(xT[:, 1, (b - 1) * N:b * N], bank(2 * ((b - 1) % 2) + 1)).then_inc(xT_dve, 1)
                dve.wait_ge(xT_psum, 2 * NB)
                nc.vector.tensor_copy(xT[:, 1, (NB - 1) * N:NB * N], bank(2 * ((NB - 1) % 2) + 1)).then_inc(xT_dve, 1)
                dve.wait_ge(lg_psum, 1)
                dve.wait_ge(loaded, 32)
                nc.vector.tensor_tensor(logits[:], bank(4)[:, 0:T * E].rearrange("p (t e) -> p t e", t=T),
                                        b_router[:].unsqueeze(1).to_broadcast([P, T, E]), ALU.add)

            @block.scalar
            def _(act):
                for b in range(NB):
                    act.wait_ge(xT_psum, 2 * b + 1)
                    nc.scalar.activation(xT[:, 0, b * N:(b + 1) * N], bank(2 * (b % 2)), ACT.Copy).then_inc(xT_act, 1)

            @block.tensor
            def _(pe):
                for b in range(NB):
                    pe.wait_ge(xn_ready, (b + 1) * TB)
                    if b >= 2:
                        pe.wait_ge(xT_act, b - 1)
                        pe.wait_ge(xT_dve, b - 1)
                    for c in range(s.DC):
                        for t in range(TB):
                            last = nc.tensor.transpose(bank(2 * (b % 2) + c)[:, t * P:(t + 1) * P],
                                                       xn[:, b * TB + t, c * P:(c + 1) * P], g["ident"][:])
                        last.then_inc(xT_psum, 1)
                pe.wait_ge(loaded, 32)
                pe.wait_ge(xT_act, NB)
                pe.wait_ge(xT_dve, NB)
                for t in range(T):
                    for c in range(s.DC):
                        last = nc.tensor.matmul(bank(4)[:, t * E:(t + 1) * E], xT[:, c, t * P:(t + 1) * P],
                                                w_router[:, c, :], start=(c == 0), stop=(c == s.DC - 1))
                last.then_inc(lg_psum, 1)

        with nc.Block() as block:
            @block.vector
            def _(dve):
                mine = logits[:].unsqueeze(3).to_broadcast([P, T, E, E])
                other = logits[:].unsqueeze(2).to_broadcast([P, T, E, E])
                nc.vector.tensor_tensor(cmp[:], other, mine, ALU.is_gt)
                nc.vector.tensor_tensor(tie[:], other, mine, ALU.is_equal)
                dve.drain()
                for t in range(T):
                    nc.vector.tensor_tensor(tie[:, t], tie[:, t], before[:], ALU.mult)
                dve.drain()
                nc.vector.tensor_tensor(cmp[:], cmp[:], tie[:], ALU.add)
                dve.drain()
                nc.vector.reduce_sum(rank[:], cmp[:], AX_X)
                dve.drain()
                nc.vector.tensor_scalar(first[:], rank[:], 0.0, None, ALU.is_equal)
                nc.vector.tensor_scalar(second[:], rank[:], 1.0, None, ALU.is_equal)
                dve.drain()
                nc.vector.tensor_tensor(route[:], second[:], logits[:], ALU.mult)
                nc.vector.reduce_max(top[:, 0, :], logits[:], AX_X)
                dve.drain()
                nc.vector.reduce_sum(top[:, 1, :], route[:], AX_X)
                dve.drain()
                nc.vector.tensor_tensor(top[:, 2, :], top[:, 1, :], top[:, 0, :], ALU.subtract).then_inc(tops, 1)
                dve.wait_ge(exped, 1)
                nc.vector.tensor_scalar(top[:, 0, :], top[:, 3, :], 1.0, None, ALU.add)
                dve.drain()
                nc.vector.reciprocal(top[:, 0, :], top[:, 0, :])
                dve.drain()
                nc.vector.tensor_tensor(top[:, 1, :], top[:, 3, :], top[:, 0, :], ALU.mult)
                dve.drain()
                nc.vector.tensor_tensor(first[:], first[:], top[:, 0, :].unsqueeze(2).to_broadcast([P, T, E]), ALU.mult)
                nc.vector.tensor_tensor(second[:], second[:], top[:, 1, :].unsqueeze(2).to_broadcast([P, T, E]), ALU.mult)
                dve.drain()
                nc.vector.tensor_tensor(route[:], first[:], second[:], ALU.add)

            @block.scalar
            def _(act):
                act.wait_ge(tops, 1)
                nc.scalar.activation(top[:, 3, :], top[:, 2, :], ACT.Exp).then_inc(exped, 1)

            @block.gpsimd
            def _(pool):
                nc.gpsimd.memset(accT[:], 0.0)

        route_psum = sem("moe_route_psum")
        xs_ready = sem("moe_xs_ready")
        up_psum = sem("moe_up_psum")
        gate_done = sem("moe_gate_done")
        hid_ready = sem("moe_hid_ready")
        y_psum = sem("moe_y_psum")
        y_done = sem("moe_y_done")
        FT = s.FT

        with nc.Block() as block:
            @block.sync
            def _(sp):
                for e in range(2, E):
                    sp.wait_ge(w_used, e - 1)
                    sp.dma_start(w1[:, e % 2], dram["moe_w1"][e].rearrange("(c p) n -> p c n", p=P)).then_inc(w_ready[e % 2], 16)
                    sp.dma_start(w3[:, e % 2], dram["moe_w3"][e].rearrange("(c p) n -> p c n", p=P)).then_inc(w_ready[e % 2], 16)
                    sp.dma_start(w2[:, e % 2], dram["moe_w2"][e].rearrange("(c p) n -> p c n", p=P)).then_inc(w_ready[e % 2], 16)

            @block.tensor
            def _(pe):
                def down(n, f):
                    e, b = divmod(n, NB)
                    pe.wait_ge(hid_ready, n * FT + f + 1)
                    if f == 0 and n >= 1:
                        pe.wait_ge(y_done, n)
                    for c in range(s.DC):
                        last = nc.tensor.matmul(bank(4 + c), w2[:, e % 2, f, c * P:(c + 1) * P], hid[:, f % 2, :],
                                                start=(f == 0), stop=(f == FT - 1))
                    if f == FT - 1:
                        last.then_inc(y_psum, 1)
                        if b == NB - 1:
                            return
                    return

                for n in range(E * NB):
                    e, b = divmod(n, NB)
                    if b == 0:
                        pe.wait_ge(w_ready[e % 2], 48 * (e // 2 + 1))
                    if n >= 1:
                        pe.wait_ge(xs_ready, n)
                    for t in range(TB):
                        last = nc.tensor.transpose(bank(6)[:, t * P:(t + 1) * P],
                                                   route[:, b * TB + t, e:e + 1].to_broadcast([P, P]), g["ident"][:])
                    last.then_inc(route_psum, 1)
                    pe.wait_ge(xs_ready, n + 1)
                    for f in range(FT):
                        k = n * FT + f
                        if k >= 2:
                            pe.wait_ge(hid_ready, k - 1)
                        for w, at in ((w1, 0), (w3, 2)):
                            for c in range(s.DC):
                                last = nc.tensor.matmul(bank(at + k % 2), w[:, e % 2, c, f * P:(f + 1) * P], xs[:, c, :],
                                                        start=(c == 0), stop=(c == s.DC - 1))
                        last.then_inc(up_psum, 1)
                        if f >= 1:
                            down(n, f - 1)
                    down(n, FT - 1)

            @block.scalar
            def _(act):
                for k in range(E * NB * FT):
                    act.wait_ge(up_psum, k + 1)
                    if k >= 2:
                        act.wait_ge(hid_ready, k - 1)
                    nc.scalar.activation(gate[:, k % 2, :], bank(k % 2), ACT.Silu).then_inc(gate_done, 1)

            @block.vector
            def _(dve):
                def scale_tokens(n):
                    b = n % NB
                    dve.wait_ge(route_psum, n + 1)
                    for c in range(s.DC):
                        last = nc.vector.tensor_tensor(xs[:, c, :], xT[:, c, b * N:(b + 1) * N], bank(6), ALU.mult)
                    last.then_inc(xs_ready, 1)

                def add_up(n):
                    e, b = divmod(n, NB)
                    dve.wait_ge(y_psum, n + 1)
                    for c in range(s.DC):
                        last = nc.vector.tensor_tensor(accT[:, c, b * N:(b + 1) * N], bank(4 + c),
                                                       accT[:, c, b * N:(b + 1) * N], ALU.add)
                    last.then_inc(y_done, 1)
                    if b == NB - 1:
                        dve.sem_inc(w_used, 1)

                for n in range(E * NB):
                    scale_tokens(n)
                    for f in range(FT):
                        k = n * FT + f
                        dve.wait_ge(gate_done, k + 1)
                        nc.vector.tensor_tensor(hid[:, k % 2, :], bank(2 + k % 2), gate[:, k % 2, :], ALU.mult).then_inc(hid_ready, 1)
                    add_up(n)
                    dve.drain()

            @block.gpsimd
            def _(pool):
                for t in range(T):
                    nc.gpsimd.tensor_scalar(xn[:, t, :], xn[:, t, :], g["gates"][:, 3:4], None, ALU.mult)
                pool.drain()
                for t in range(T):
                    nc.gpsimd.tensor_tensor(g["x"][:, t, :], g["x"][:, t, :], xn[:, t, :], ALU.add)

        y_tok = sem("moe_y_tok")
        fin = sem("moe_fin")
        stored = sem("moe_stored")
        with nc.Block() as block:
            @block.tensor
            def _(pe):
                for t in range(T):
                    if t >= 4:
                        pe.wait_ge(fin, t - 3)
                    for c in range(s.DC):
                        last = nc.tensor.transpose(bank(t % 4)[:, c * P:(c + 1) * P], accT[:, c, t * P:(t + 1) * P],
                                                   g["ident"][:])
                    last.then_inc(y_tok, 1)

            @block.vector
            def _(dve):
                for t in range(T):
                    dve.wait_ge(y_tok, t + 1)
                    nc.vector.scalar_tensor_tensor(out=g["x"][:, t, :], in0=bank(t % 4)[:, 0:D], scalar=g["gates"][:, 3:4],
                                                   in1=g["x"][:, t, :], op0=ALU.mult, op1=ALU.add).then_inc(fin, 1)

            @block.sync
            def _(sp):
                for b in range(B):
                    sp.wait_ge(fin, (b + 1) * TB)
                    sp.dma_start(out[b].rearrange("(t p) n -> p t n", p=P), g["x"][:, b * TB:(b + 1) * TB, :]).then_inc(stored, 16)
                sp.wait_ge(stored, 16 * B)


def flamingo(nc, dram, out):
    s = Shapes(dram["x"], dram["ctx"], dram["w_in"], dram["w_router"], dram["moe_w1"], dram["null_kv"], dram["wq"])
    with ExitStack() as ctx:
        def sb(name, shape, dt=F32):
            return ctx.enter_context(nc.sbuf_tensor(name, shape, dt))

        psum = ctx.enter_context(nc.psum_tensor("psum", [P, 8 * BANK], F32))

        def bank(i):
            return psum[:, i * BANK:(i + 1) * BANK]

        def wide(i):
            return psum[:, i * BANK:(i + 2) * BANK]

        g = {"x": sb("x_resid", [P, s.T, s.D]), "ident": sb("ident", [P, P]), "gates": sb("gates", [P, 4])}
        gates_raw = sb("gates_raw", [P, 4])
        x_loaded = ctx.enter_context(nc.semaphore("x_loaded"))
        gates_loaded = ctx.enter_context(nc.semaphore("gates_loaded"))
        with nc.Block() as block:
            @block.sync
            def _(sp):
                for i in range(2):
                    for j, name in enumerate(("g_xattn", "g_ffn")):
                        sp.dma_start(gates_raw[:, 2 * i + j:2 * i + j + 1],
                                     dram[name][i:i + 1].partition_broadcast(P)).then_inc(gates_loaded, 16)
                for b in range(s.B):
                    sp.dma_start(g["x"][:, b * s.TT:(b + 1) * s.TT, :],
                                 dram["x"][b].rearrange("(t p) n -> p t n", p=P)).then_inc(x_loaded, 16)
                sp.wait_ge(x_loaded, 16 * s.B)

            @block.gpsimd
            def _(pool):
                nc.gpsimd.memset(g["ident"][:], 0.0)
                pool.drain()
                nc.gpsimd.affine_select(out=g["ident"][:], in_=g["ident"][:], compare_op=ALU.not_equal, fill=1.0,
                                        base=0, pattern=[[-1, P]], channel_multiplier=1)

            @block.scalar
            def _(act):
                act.wait_ge(gates_loaded, 64)
                nc.scalar.activation(g["gates"][:], gates_raw[:], ACT.Tanh)

        layer0(nc, s, g, bank, wide, dram)
        layer1(nc, s, g, bank, dram)
        experts(nc, s, g, bank, dram, out)


def kernel(**inputs):
    import numpy as np
    import concourse.bacc as bacc
    from concourse.bass_utils import run_bass_kernel_spmd

    a = {k: np.asarray(v) for k, v in inputs.items()}
    heads, dim = 16, a["x"].shape[2]
    dh = dim // heads
    projT = np.zeros((heads, 32, dim), a["L0_xattn_w_proj"].dtype)
    projT[:, 0:dh, :] = a["L0_xattn_w_proj"].T.reshape(heads, dh, dim)
    arrays = {
        "x": a["x"], "ctx": a["ctx_2048"], "ctxT": a["ctx_2048"].transpose(0, 2, 1),
        "g_xattn": a["g_xattn"], "g_ffn": a["g_ffn"],
        "w_qkvT": a["L0_xattn_w_qkv"].T, "w_projT": projT.reshape(heads * 32, dim), "b_proj": a["L0_xattn_b_proj"],
        "w_in": a["L0_ffn_Win"], "b_in": a["L0_ffn_bin_"], "w1": a["L0_ffn_W1"], "b1": a["L0_ffn_b1"],
        "w2": a["L0_ffn_W2"], "b2": a["L0_ffn_b2"], "w_out": a["L0_ffn_Wout"], "b_out": a["L0_ffn_bout"],
        "wq": a["L1_xattn_Wq"], "wkv": a["L1_xattn_Wkv"], "null_kv": a["L1_xattn_null_kv"], "wo": a["L1_xattn_Wout"],
        "ln_scale": a["L1_xattn_ln_scale"], "ln_bias": a["L1_xattn_ln_bias"],
        "w_router": a["L1_ffn_Wg"], "b_router": a["L1_ffn_bg"],
        "moe_w1": a["L1_ffn_W1"], "moe_w2": a["L1_ffn_W2"], "moe_w3": a["L1_ffn_W3"],
    }
    arrays = {f"in_{k}": np.ascontiguousarray(v) for k, v in arrays.items()}
    nc = bacc.Bacc("TRN2", target_bir_lowering=False, num_devices=1)
    dram = {k[3:]: nc.dram_tensor(k, v.shape, mybir.dt.from_np(v.dtype), kind="ExternalInput").ap()
            for k, v in arrays.items()}
    out = nc.dram_tensor("out_x", a["x"].shape, F32, kind="ExternalOutput").ap()
    flamingo(nc, dram, out)
    result = run_bass_kernel_spmd(nc, [arrays], core_ids=[0])
    return result.results[0]["out_x"]
```

```python
from contextlib import ExitStack

import concourse.bass as bass
from concourse import mybir

F32 = mybir.dt.float32
F32R = mybir.dt.float32r
U32 = mybir.dt.uint32
ALU = mybir.AluOpType
ACT = mybir.ActivationFunctionType
AX_X = mybir.AxisListType.X

P = 128
BANK = 512
LN_EPS = 1e-5
LN_OUT_EPS = 1e-6
RSQRT_MAGIC = 0x5F3759DF


class Shapes:

    def __init__(self, x, ctx, w_win, w_router, moe_w1, null_kv, wq1):
        self.B, self.N, self.D = x.shape
        self.M, self.C = ctx.shape[1], ctx.shape[2]
        self.TT = self.N // P
        self.T = self.B * self.TT
        self.DC = self.D // P
        self.CC = self.C // P
        self.H = 16
        self.DH0 = self.D // self.H
        self.KT0 = (self.M + self.N) // P
        self.DH1 = null_kv.shape[1]
        self.I1 = wq1.shape[1]
        self.KT1 = self.M // P
        self.FM = w_win.shape[1]
        self.E = w_router.shape[1]
        self.F = moe_w1.shape[2]
        self.FT = self.F // P


class Norm:

    STEPS = 3

    def __init__(self, nc, tiles, stats, mv, work):
        self.nc, self.tiles, self.stats, self.mv, self.work = nc, tiles, stats, mv, work

    def statistics(self, dve, rows, eps):
        nc, n = self.nc, self.tiles
        for t in range(n):
            nc.vector.bn_stats(self.stats[:, t, :], rows(t))
        dve.drain()
        for t in range(n):
            nc.vector.bn_aggr(self.mv[:, t, :], self.stats[:, t, :])
        dve.drain()
        var, guess, half, tmp = (self.work[:, i, 0:n] for i in range(4))
        nc.vector.tensor_scalar(var, self.mv[:, 0:n, 1], 1.0, eps, ALU.mult, ALU.add)
        dve.drain()
        nc.vector.tensor_scalar(tmp.bitcast(U32), var.bitcast(U32), 1, None, ALU.logical_shift_right)
        nc.vector.tensor_scalar(half, var, -0.5, None, ALU.mult)
        dve.drain()
        nc.vector.tensor_scalar(guess.bitcast(U32), tmp.bitcast(U32), -1.0, float(RSQRT_MAGIC), ALU.mult, ALU.add)
        dve.drain()
        for _ in range(self.STEPS):
            nc.vector.tensor_tensor(tmp, guess, guess, ALU.mult)
            dve.drain()
            nc.vector.tensor_tensor(tmp, tmp, half, ALU.mult)
            dve.drain()
            nc.vector.scalar_tensor_tensor(out=guess, in0=tmp, scalar=1.5, in1=guess, op0=ALU.add, op1=ALU.mult)
            dve.drain()
        self.rstd = guess

    def apply(self, out, row, t):
        return self.nc.vector.tensor_scalar(out, row, self.mv[:, t, 0:1], self.work[:, 1, t:t + 1],
                                            ALU.subtract, ALU.mult)


def layer0(nc, s, g, bank, wide, dram):
    T, H, DH, N, D = s.TT, s.H, s.DH0, s.N, s.D
    ST = 64
    K_SCORE, M_ROW = 3 * DH, 3 * DH
    PAIRS, QUADS = H // 2, H // 4
    KT = s.KT0
    SCALE = float(DH) ** -0.5
    PT_RING = 6

    with ExitStack() as ctx:
        def sb(name, shape, dt=F32):
            return ctx.enter_context(nc.sbuf_tensor("l0_" + name, shape, dt))

        def sem(name):
            return ctx.enter_context(nc.semaphore(name))

        w_qkv = sb("w_qkv", [P, s.DC, 3 * D])
        w_proj = sb("w_proj", [P, s.DC, D])
        b_proj = sb("b_proj", [P, D])
        w_in = sb("w_in", [P, s.DC, P])
        w_out = sb("w_out", [P, D])
        b_out = sb("b_out", [P, D])
        b_in = sb("b_in", [P, 1])
        w1 = sb("w1", [P, 8])
        b1 = sb("b1", [P, 8])
        w2 = sb("w2", [P, 8])
        b2 = sb("b2", [P, 1])
        ctx_sb = sb("ctx_sb", [P, T, 2 * D])
        xn = sb("xn", [P, T, D])
        xT = sb("xT", [P, s.DC, N])
        q_stack = sb("q_stack", [P, T, H, ST])
        k_stack = sb("k_stack", [P, 2, H, ST])
        kT = sb("kT", [P, PAIRS, KT * P], F32R)
        qT = sb("qT", [P, 2, 4, N], F32R)
        v_ones = sb("v_ones", [P, KT, H, 2 * DH])
        probs = sb("probs", [P, PT_RING, 2, N])
        pv = sb("pv", [P, N])
        o_tok = sb("o_tok", [P, T, H, DH])
        recip = sb("recip", [P, T, 4])
        oT = sb("oT", [P, s.DC, N])
        tile_max = sb("tile_max", [P, T, H, 2])
        units = sb("units", [P, 2, N])
        gated = sb("gated", [P, N])
        s_in = sb("s_in", [P, N])
        x_bias = sb("x_bias", [P, T, D])
        stats = sb("stats", [P, T, 6])
        mv = sb("mv", [P, T, 2])
        work = sb("work", [P, 4, T])
        norm = Norm(nc, T, stats, mv, work)

        loaded = sem("l0_weights_loaded")
        filled = sem("l0_constants_filled")

        with nc.Block() as block:
            @block.sync
            def _(sp):
                sp.dma_start(w_qkv[:], dram["w_qkvT"].rearrange("(c p) n -> p c n", p=P)).then_inc(loaded, 16)
                sp.dma_start(w_proj[:], dram["w_projT"].rearrange("(c p) n -> p c n", p=P)).then_inc(loaded, 16)
                sp.dma_start(b_proj[:], dram["b_proj"].partition_broadcast(P)).then_inc(loaded, 16)
                for half in range(2):
                    sp.dma_start(w_in[:, :, half * s.FM:(half + 1) * s.FM],
                                 dram["w_in"].rearrange("(c p) n -> p c n", p=P)).then_inc(loaded, 16)
                    rows = slice(half * s.FM, (half + 1) * s.FM)
                    sp.dma_start(w_out[rows, :], dram["w_out"]).then_inc(loaded, 16)
                    sp.dma_start(b_in[rows, :], dram["b_in"].unsqueeze(1)).then_inc(loaded, 16)
                    for dst, src in ((w1, "w1"), (b1, "b1"), (w2, "w2")):
                        sp.dma_start(dst[rows, :], dram[src][:, 8 * half:8 * half + 8]).then_inc(loaded, 16)
                sp.dma_start(b2[0:s.FM, :], dram["b2"].unsqueeze(1)).then_inc(loaded, 16)
                sp.dma_start(b_out[:], dram["b_out"].partition_broadcast(P)).then_inc(loaded, 16)
                sp.wait_ge(loaded, 16 * 17)

            @block.gpsimd
            def _(pool):
                nc.gpsimd.memset(q_stack[:], 0.0)
                nc.gpsimd.memset(k_stack[:], 0.0)
                nc.gpsimd.memset(v_ones[:], 1.0)
                nc.gpsimd.memset(qT[:].bitcast(F32), 0.0)
                pool.drain()
                nc.gpsimd.memset(b2[s.FM:P, :], 0.0)
                pool.drain()
                nc.gpsimd.memset(k_stack[:, :, :, M_ROW:M_ROW + 1], 1.0)

        with nc.Block() as block:
            @block.vector
            def _(dve):
                nc.vector.tensor_scalar(b_proj[:], b_proj[:], g["gates"][:, 0:1], None, ALU.mult)
                nc.vector.tensor_scalar(b_out[:], b_out[:], g["gates"][:, 1:2], None, ALU.mult)

        ctx_ready = sem("l0_ctx_ready")
        xn_ready = sem("l0_xn_ready")
        xT_psum = sem("l0_xT_psum")
        xT_act = sem("l0_xT_act")
        xT_dve = sem("l0_xT_dve")
        qk_psum = sem("l0_qk_psum")
        v_psum = sem("l0_v_psum")
        qk_split = sem("l0_qk_split")
        v_copied = sem("l0_v_copied")
        split = sem("l0_split")
        dup = sem("l0_dup")
        tr_psum = sem("l0_tr_psum")
        tr_act = sem("l0_tr_act")
        tr_dve = sem("l0_tr_dve")

        max_psum = sem("l0_max_psum")
        max_read = sem("l0_max_read")
        negmax = sem("l0_negmax")
        q_psum = sem("l0_q_psum")
        q_ready = sem("l0_q_ready")
        s_psum = sem("l0_s_psum")
        exp_done = sem("l0_exp_done")
        pv_done = sem("l0_pv_done")
        pv_copied = sem("l0_pv_copied")
        o_psum = sem("l0_o_psum")
        o_ready = sem("l0_o_ready")

        bias_added = sem("l0_bias_added")
        oT_psum = sem("l0_oT_psum")
        oT_act = sem("l0_oT_act")
        oT_dve = sem("l0_oT_dve")
        proj_psum = sem("l0_proj_psum")
        resid = sem("l0_resid")
        xn2_ready = sem("l0_xn2_ready")
        xT2_psum = sem("l0_xT2_psum")
        xT2_act = sem("l0_xT2_act")
        xT2_dve = sem("l0_xT2_dve")
        sin_psum = sem("l0_sin_psum")
        sin_ready = sem("l0_sin_ready")
        unit_ready = sem("l0_unit_ready")
        unit_used = sem("l0_unit_used")
        ffn_psum = sem("l0_ffn_psum")
        ffn_done = sem("l0_ffn_done")

        NI = s.KT0
        NCTX = s.KT0 - T

        def item_banks(i):
            return (6, 7) if i % 2 == 0 else (0, 1)

        def key_source(kt):
            return k_stack[:, kt % 2]

        for b in range(s.B):
            x_b = g["x"][:, b * T:(b + 1) * T, :]

            with nc.Block() as block:
                @block.sync
                def _(sp):
                    sp.dma_start(ctx_sb[:], dram["ctx"][b].rearrange("(t p) n -> p t n", p=P)).then_inc(ctx_ready, 16)

                @block.vector
                def _(dve):
                    n_split = b * (NCTX + 2 * T)

                    def evacuate(i):
                        dve.wait_ge(tr_psum, b * NI + i + 1)
                        nc.vector.tensor_copy(kT[:, 4:8, i * P:(i + 1) * P],
                                              bank(item_banks(i)[1]).rearrange("p (a n) -> p a n", a=4)
                                              ).then_inc(tr_dve, 1)

                    def split_keys(src, dst):
                        src = src.rearrange("p (h d) -> p h d", h=H)
                        nc.vector.tensor_copy(dst[:, :, 0:DH].bitcast(F32R), src)
                        dve.drain()
                        return nc.vector.tensor_tensor(dst[:, :, DH:2 * DH], src, dst[:, :, 0:DH], ALU.subtract)

                    def split_queries(src, dst):
                        src = src.rearrange("p (h d) -> p h d", h=H)
                        nc.vector.tensor_copy(dst[:, :, 0:DH].bitcast(F32R), src)
                        dve.drain()
                        return nc.vector.tensor_tensor(dst[:, :, 2 * DH:3 * DH], src, dst[:, :, 0:DH], ALU.subtract)

                    norm.statistics(dve, lambda t: x_b[:, t, :], LN_EPS)
                    for t in range(T):
                        norm.apply(xn[:, t, :], x_b[:, t, :], t).then_inc(xn_ready, 1)
                    dve.wait_ge(ctx_ready, 16 * (b + 1))
                    for t in range(NCTX):
                        if t >= 2:
                            dve.wait_ge(tr_psum, b * NI + t - 1)
                        split_keys(ctx_sb[:, t, 0:D], key_source(t)).then_inc(split, 1)
                        if t >= 1:
                            evacuate(t - 1)
                    evacuate(NCTX - 1)
                    dve.wait_ge(xT_psum, 2 * b + 2)
                    nc.vector.tensor_copy(xT[:, 1, :], bank(3)).then_inc(xT_dve, 1)
                    for t in range(T):
                        dve.wait_ge(qk_psum, b * T + t + 1)
                        kt = NCTX + t
                        dve.wait_ge(tr_psum, b * NI + kt - 1)
                        qk = bank(2 + 2 * (t % 2))
                        split_queries(qk[:, 0:D], q_stack[:, t])
                        split_keys(qk[:, D:2 * D], key_source(kt)).then_inc(split, 1)
                        if t >= 1:
                            evacuate(kt - 1)
                    evacuate(NI - 1)

                @block.gpsimd
                def _(pool):
                    nc.gpsimd.memset(q_stack[:, :, :, M_ROW:M_ROW + 1], 0.0)
                    pool.wait_ge(ctx_ready, 16 * (b + 1))
                    for t in range(NCTX):
                        pool.wait_ge(split, b * (NCTX + T) + t + 1)
                        nc.gpsimd.tensor_copy(key_source(t)[:, :, 2 * DH:3 * DH], key_source(t)[:, :, 0:DH]).then_inc(dup, 1)
                        nc.gpsimd.tensor_copy(v_ones[:, t, :, 0:DH],
                                              ctx_sb[:, t, D:2 * D].rearrange("p (h d) -> p h d", h=H))
                    for t in range(T):
                        pool.wait_ge(split, b * (NCTX + T) + NCTX + t + 1)
                        nc.gpsimd.tensor_copy(q_stack[:, t, :, DH:2 * DH], q_stack[:, t, :, 0:DH])
                        ks = key_source(NCTX + t)
                        pool.drain()
                        nc.gpsimd.tensor_copy(ks[:, :, 2 * DH:3 * DH], ks[:, :, 0:DH]).then_inc(dup, 1)

                @block.scalar
                def _(act):
                    def evacuate(i):
                        act.wait_ge(tr_psum, b * NI + i + 1)
                        nc.scalar.activation(kT[:, 0:4, i * P:(i + 1) * P],
                                             bank(item_banks(i)[0]).rearrange("p (a n) -> p a n", a=4),
                                             ACT.Copy).then_inc(tr_act, 1)

                    for t in range(NCTX):
                        evacuate(t)
                    act.wait_ge(xT_psum, 2 * b + 1)
                    nc.scalar.activation(xT[:, 0, :], bank(2), ACT.Copy).then_inc(xT_act, 1)
                    for t in range(T):
                        act.wait_ge(v_psum, b * T + t + 1)
                        nc.scalar.activation(v_ones[:, NCTX + t, :, 0:DH],
                                             bank(3 + 2 * (t % 2))[:, 0:D].rearrange("p (h d) -> p h d", h=H),
                                             ACT.Copy).then_inc(v_copied, 1)
                        if t >= 1:
                            evacuate(NCTX + t - 1)
                    evacuate(NI - 1)

                @block.tensor
                def _(pe):
                    def transposes(i):
                        if i >= 2:
                            pe.wait_ge(tr_act, b * NI + i - 1)
                            pe.wait_ge(tr_dve, b * NI + i - 1)
                        src = key_source(i).rearrange("p h r -> p (h r)")
                        for p in range(PAIRS):
                            dst = bank(item_banks(i)[p // 4])[:, (p % 4) * P:(p % 4 + 1) * P]
                            last = nc.tensor.transpose(dst, src[:, p * P:(p + 1) * P], g["ident"][:])
                        last.then_inc(tr_psum, 1)

                    for t in range(NCTX):
                        pe.wait_ge(dup, b * (NCTX + T) + t + 1)
                        transposes(t)
                    pe.wait_ge(xn_ready, (b + 1) * T)
                    for c in range(s.DC):
                        for t in range(T):
                            last = nc.tensor.transpose(bank(2 + c)[:, t * P:(t + 1) * P],
                                                       xn[:, t, c * P:(c + 1) * P], g["ident"][:])
                        last.then_inc(xT_psum, 1)
                    pe.wait_ge(xT_act, b + 1)
                    pe.wait_ge(xT_dve, b + 1)
                    for t in range(T + 1):
                        if t < T:
                            if t >= 2:
                                pe.wait_ge(split, b * (NCTX + T) + NCTX + t - 1)
                                pe.wait_ge(v_copied, b * T + t - 1)
                            for c in range(s.DC):
                                last = nc.tensor.matmul(bank(2 + 2 * (t % 2))[:, 0:2 * D], xT[:, c, t * P:(t + 1) * P],
                                                        w_qkv[:, c, 0:2 * D], start=(c == 0), stop=(c == s.DC - 1))
                            last.then_inc(qk_psum, 1)
                            for c in range(s.DC):
                                last = nc.tensor.matmul(bank(3 + 2 * (t % 2))[:, 0:D], xT[:, c, t * P:(t + 1) * P],
                                                        w_qkv[:, c, 2 * D:3 * D], start=(c == 0), stop=(c == s.DC - 1))
                            last.then_inc(v_psum, 1)
                        if t >= 1:
                            pe.wait_ge(dup, b * (NCTX + T) + NCTX + t)
                            transposes(NCTX + t - 1)

            UNITS = QUADS * KT * 2
            MAXES = H * T * 2
            Q_ITEMS = 2 * PAIRS
            with nc.Block() as block:
                @block.tensor
                def _(pe):
                    q_items = [0]

                    def stack_queries(quad, with_max):
                        if with_max:
                            pe.wait_ge(negmax, b * QUADS + quad + 1)
                        for c in range(2):
                            if q_items[0] >= 1:
                                pe.wait_ge(q_ready, b * Q_ITEMS + q_items[0])
                            p = 2 * quad + c
                            for t in range(T):
                                src = q_stack[:, t].rearrange("p h r -> p (h r)")
                                last = nc.tensor.transpose(bank(7)[:, t * P:(t + 1) * P],
                                                           src[:, p * P:(p + 1) * P], g["ident"][:])
                            last.then_inc(q_psum, 1)
                            q_items[0] += 1

                    def max_scores(n):
                        h, r = divmod(n, 2 * T)
                        t, half = divmod(r, 2)
                        if n >= 2:
                            pe.wait_ge(max_read, b * MAXES + n - 1)
                        nc.tensor.matmul(bank(4 + n % 2), qT[:, (h // 4) % 2, h % 4, t * P:(t + 1) * P],
                                         kT[:, h // 2, half * BANK:(half + 1) * BANK],
                                         start=True, stop=True).then_inc(max_psum, 1)

                    def scores(n):
                        quad, r = divmod(n, 2 * KT)
                        kt, c = divmod(r, 2)
                        if n >= 2:
                            pe.wait_ge(exp_done, b * UNITS + n - 1)
                        for i in range(2):
                            last = nc.tensor.matmul(bank(2 * (n % 2) + i),
                                                    kT[:, 2 * quad + c, kt * P:(kt + 1) * P],
                                                    qT[:, quad % 2, 2 * c + i, :], start=True, stop=True)
                        last.then_inc(s_psum, 1)

                    def weigh_values(quad, kt):
                        n = 2 * (quad * KT + kt)
                        pe.wait_ge(exp_done, b * UNITS + n + 2)
                        if kt == 0 and quad >= 1:
                            pe.wait_ge(pv_copied, b * QUADS + quad)
                        for j in range(4):
                            last = nc.tensor.matmul(bank(6)[32 * j:32 * j + 32, :], v_ones[:, kt, 4 * quad + j, :],
                                                    probs[:, (n + j // 2) % PT_RING, j % 2, :],
                                                    start=(kt == 0), stop=(kt == KT - 1), tile_position=(0, 32 * j),
                                                    skip_group_check=True)
                        last.then_inc(pv_done, 1)

                    def tokens_first(quad):
                        pe.wait_ge(pv_copied, b * QUADS + quad + 1)
                        if quad >= 1:
                            pe.wait_ge(o_ready, b * QUADS + quad)
                        pe.wait_ge(q_ready, b * Q_ITEMS + q_items[0])
                        for t in range(T):
                            last = nc.tensor.transpose(bank(7)[:, t * P:(t + 1) * P], pv[:, t * P:(t + 1) * P], g["ident"][:])
                        last.then_inc(o_psum, 1)

                    stack_queries(0, False)
                    pe.wait_ge(q_ready, b * Q_ITEMS + 2)
                    for n in range(8 * T):
                        max_scores(n)
                        if n == T:
                            stack_queries(1, False)
                    stack_queries(0, True)
                    for quad in range(QUADS):
                        pe.wait_ge(q_ready, b * Q_ITEMS + q_items[0])
                        if quad >= 1:
                            tokens_first(quad - 1)
                        for kt in range(KT):
                            for c in range(2):
                                u = 2 * kt + c
                                scores(2 * KT * quad + u)
                                if quad + 1 < QUADS:
                                    max_scores(8 * T * (quad + 1) + 2 * u)
                                    max_scores(8 * T * (quad + 1) + 2 * u + 1)
                            if kt >= 1:
                                weigh_values(quad, kt - 1)
                        if quad + 2 < QUADS:
                            if quad >= 1:
                                pe.wait_ge(o_ready, b * QUADS + quad)
                            stack_queries(quad + 2, False)
                        weigh_values(quad, KT - 1)
                        if quad + 1 < QUADS:
                            if quad + 2 >= QUADS:
                                pe.wait_ge(o_ready, b * QUADS + quad)
                            stack_queries(quad + 1, True)
                    tokens_first(QUADS - 1)

                @block.scalar
                def _(act):
                    q_items = [0]

                    def place_queries(quad):
                        for c in range(2):
                            act.wait_ge(q_psum, b * Q_ITEMS + q_items[0] + 1)
                            for i in range(2):
                                rows = slice(i * ST, (i + 1) * ST)
                                last = nc.scalar.activation(qT[rows, quad % 2, 2 * c + i, :], bank(7)[rows, :], ACT.Copy)
                            last.then_inc(q_ready, 1)
                            q_items[0] += 1

                    def copy_values(quad):
                        act.wait_ge(pv_done, b * QUADS * KT + (quad + 1) * KT)
                        if quad >= 1:
                            act.wait_ge(o_psum, b * QUADS + quad)
                        nc.scalar.activation(pv[:], bank(6), ACT.Copy).then_inc(pv_copied, 1)

                    place_queries(0)
                    place_queries(1)
                    place_queries(0)
                    for quad in range(QUADS):
                        for u in range(2 * KT):
                            n = 2 * KT * quad + u
                            act.wait_ge(s_psum, b * UNITS + n + 1)
                            if n >= PT_RING:
                                act.wait_ge(pv_done, b * QUADS * KT + (n - PT_RING) // 2 + 1)
                            nc.scalar.activation(probs[:, n % PT_RING], wide(2 * (n % 2)), ACT.Exp,
                                                 scale=SCALE).then_inc(exp_done, 1)
                        if quad + 2 < QUADS:
                            place_queries(quad + 2)
                        copy_values(quad)
                        if quad + 1 < QUADS:
                            place_queries(quad + 1)

                @block.vector
                def _(dve):
                    def normalize(quad):
                        dve.wait_ge(o_psum, b * QUADS + quad + 1)
                        o = bank(7).rearrange("p (t j d) -> p t j d", t=T, j=4)
                        nc.vector.reciprocal(recip[:], o[:, :, :, DH])
                        dve.drain()
                        for t in range(T):
                            last = nc.vector.tensor_tensor(o_tok[:, t, 4 * quad:4 * quad + 4, :], o[:, t, :, 0:DH],
                                                           recip[:, t, :].unsqueeze(2).to_broadcast([P, 4, DH]), ALU.mult)
                        last.then_inc(o_ready, 1)

                    for quad in range(QUADS):
                        for n in range(8 * T * quad, 8 * T * (quad + 1)):
                            h, r = divmod(n, 2 * T)
                            t, half = divmod(r, 2)
                            dve.wait_ge(max_psum, b * MAXES + n + 1)
                            nc.vector.reduce_max(tile_max[:, t, h, half:half + 1], bank(4 + n % 2), AX_X).then_inc(max_read, 1)
                            if quad >= 2 and n == 8 * T * quad:
                                normalize(quad - 2)
                        dve.drain()
                        for t in range(T):
                            last = nc.vector.tensor_reduce(
                                out=q_stack[:, t, 4 * quad:4 * quad + 4, M_ROW:M_ROW + 1].bitcast(F32R),
                                in_=tile_max[:, t, 4 * quad:4 * quad + 4, :], axis=AX_X, op=ALU.max, negate=True)
                        last.then_inc(negmax, 1)
                    normalize(QUADS - 2)
                    normalize(QUADS - 1)

            with nc.Block() as block:
                @block.gpsimd
                def _(pool):
                    for t in range(T):
                        nc.gpsimd.tensor_tensor(x_bias[:, t, :], x_b[:, t, :], b_proj[:], ALU.add).then_inc(bias_added, 1)
                    for t in range(T):
                        pool.wait_ge(resid, b * T + t + 1)
                        nc.gpsimd.tensor_tensor(x_bias[:, t, :], x_b[:, t, :], b_out[:], ALU.add).then_inc(bias_added, 1)

                @block.tensor
                def _(pe):
                    for c in range(s.DC):
                        for t in range(T):
                            src = o_tok[:, t].rearrange("p h d -> p (h d)")
                            last = nc.tensor.transpose(bank(4 + c)[:, t * P:(t + 1) * P], src[:, c * P:(c + 1) * P],
                                                       g["ident"][:])
                        last.then_inc(oT_psum, 1)
                    pe.wait_ge(oT_act, b + 1)
                    pe.wait_ge(oT_dve, b + 1)
                    for t in range(T):
                        for c in range(s.DC):
                            last = nc.tensor.matmul(bank(t)[:, 0:D], oT[:, c, t * P:(t + 1) * P], w_proj[:, c, :],
                                                    start=(c == 0), stop=(c == s.DC - 1))
                        last.then_inc(proj_psum, 1)
                    pe.wait_ge(xn2_ready, (b + 1) * T)
                    for c in range(s.DC):
                        for t in range(T):
                            last = nc.tensor.transpose(bank(4 + c)[:, t * P:(t + 1) * P],
                                                       xn[:, t, c * P:(c + 1) * P], g["ident"][:])
                        last.then_inc(xT2_psum, 1)
                    pe.wait_ge(xT2_act, b + 1)
                    pe.wait_ge(xT2_dve, b + 1)
                    for c in range(s.DC):
                        last = nc.tensor.matmul(bank(6), w_in[:, c, :], xT[:, c, :], start=(c == 0), stop=(c == s.DC - 1))
                    last.then_inc(sin_psum, 1)
                    pe.wait_ge(unit_used, (b + 1) * 8)
                    for t in range(T):
                        nc.tensor.matmul(bank(t)[:, 0:D], gated[:, t * P:(t + 1) * P], w_out[:],
                                         start=True, stop=True).then_inc(ffn_psum, 1)

                @block.scalar
                def _(act):
                    act.wait_ge(oT_psum, 2 * b + 1)
                    nc.scalar.activation(oT[:, 0, :], bank(4), ACT.Copy).then_inc(oT_act, 1)
                    act.wait_ge(xT2_psum, 2 * b + 1)
                    nc.scalar.activation(xT[:, 0, :], bank(4), ACT.Copy).then_inc(xT2_act, 1)
                    act.wait_ge(sin_ready, b + 1)
                    for i in range(8):
                        if i >= 2:
                            act.wait_ge(unit_used, 8 * b + i - 1)
                        nc.scalar.activation(units[:, i % 2, :], s_in[:], ACT.Relu, bias=b1[:, i:i + 1],
                                             scale=w1[:, i:i + 1]).then_inc(unit_ready, 1)

                @block.vector
                def _(dve):
                    dve.wait_ge(oT_psum, 2 * b + 2)
                    nc.vector.tensor_copy(oT[:, 1, :], bank(5)).then_inc(oT_dve, 1)
                    for t in range(T):
                        dve.wait_ge(proj_psum, b * T + t + 1)
                        dve.wait_ge(bias_added, 2 * b * T + t + 1)
                        nc.vector.scalar_tensor_tensor(out=x_b[:, t, :], in0=bank(t)[:, 0:D], scalar=g["gates"][:, 0:1],
                                                       in1=x_bias[:, t, :], op0=ALU.mult, op1=ALU.add).then_inc(resid, 1)
                    dve.drain()
                    norm.statistics(dve, lambda t: x_b[:, t, :], LN_EPS)
                    for t in range(T):
                        norm.apply(xn[:, t, :], x_b[:, t, :], t).then_inc(xn2_ready, 1)
                    dve.wait_ge(xT2_psum, 2 * b + 2)
                    nc.vector.tensor_copy(xT[:, 1, :], bank(5)).then_inc(xT2_dve, 1)
                    dve.wait_ge(sin_psum, b + 1)
                    nc.vector.tensor_scalar(s_in[:], bank(6), b_in[:, 0:1], None, ALU.add).then_inc(sin_ready, 1)
                    for i in range(8):
                        dve.wait_ge(unit_ready, 8 * b + i + 1)
                        if i == 0:
                            nc.vector.tensor_scalar(gated[:], units[:, 0, :], w2[:, 0:1], b2[:, 0:1], ALU.mult,
                                                    ALU.add).then_inc(unit_used, 1)
                        else:
                            dve.drain()
                            nc.vector.scalar_tensor_tensor(out=gated[:], in0=units[:, i % 2, :], scalar=w2[:, i:i + 1],
                                                           in1=gated[:], op0=ALU.mult, op1=ALU.add).then_inc(unit_used, 1)
                    dve.wait_ge(bias_added, 2 * (b + 1) * T)
                    for t in range(T):
                        dve.wait_ge(ffn_psum, b * T + t + 1)
                        nc.vector.scalar_tensor_tensor(out=x_b[:, t, :], in0=bank(t)[:, 0:D], scalar=g["gates"][:, 1:2],
                                                       in1=x_bias[:, t, :], op0=ALU.mult, op1=ALU.add).then_inc(ffn_done, 1)


def layer1(nc, s, g, bank, dram):
    T, H, DH, N, D = s.TT, s.H, s.DH1, s.N, s.D
    PAIRS = H // 2
    KT = s.KT1
    SCALE = float(DH) ** -0.5
    RING = 8
    UNITS = 2 * (KT + 1)

    with ExitStack() as ctx:
        def sb(name, shape, dt=F32):
            return ctx.enter_context(nc.sbuf_tensor("l1_" + name, shape, dt))

        def sem(name):
            return ctx.enter_context(nc.semaphore(name))

        wq = sb("wq", [P, s.DC, s.I1])
        wk = sb("wk", [P, s.CC, s.I1])
        wv = sb("wv", [P, s.CC, s.I1])
        wo = sb("wo", [P, PAIRS, D])
        null_k = sb("null_k", [P, DH])
        null_col = sb("null_col", [P, 1])
        null_v = sb("null_v", [1, DH])
        w_null = sb("w_null", [P, s.DC, H])
        w_null_tmp = sb("w_null_tmp", [P, H, DH])
        ln_scale = sb("ln_scale", [P, D])
        ln_bias = sb("ln_bias", [P, D])
        ctxT = sb("ctxT", [P, s.CC, s.M])
        xn = sb("xn", [P, T, D])
        xT = sb("xT", [P, s.DC, N])
        v_sb = sb("v_sb", [P, KT, s.I1])
        s_null = sb("s_null", [P, T, H])
        q1 = sb("q1", [P, 2, 2, N], F32R)
        q2 = sb("q2", [P, 2, 2, N], F32R)
        k1 = sb("k1", [P, 2, 2, s.M], F32R)
        k2 = sb("k2", [P, 2, 2, s.M], F32R)
        null1 = sb("null1", [P, P], F32R)
        null2 = sb("null2", [P, P], F32R)
        probs = sb("probs", [P, RING, N])
        null_p = sb("null_p", [1, 2, N])
        p_sum = sb("p_sum", [P, 2, N])
        ones = sb("ones", [P, DH])
        denom = sb("denom", [P, N])
        oT = sb("oT", [P, PAIRS, N])
        tile_max = sb("tile_max", [P, 2, T])
        max_tmp = sb("max_tmp", [P, 2, T])
        max_cols = sb("max_cols", [P, T, P])
        x_bias = sb("x_bias", [P, T, D])
        out_n = sb("out_n", [P, T, D])
        stats = sb("stats", [P, T, 6])
        mv = sb("mv", [P, T, 2])
        work = sb("work", [P, 4, T])
        norm = Norm(nc, T, stats, mv, work)
        norm_out = Norm(nc, T, sb("out_stats", [P, T, 6]), sb("out_mv", [P, T, 2]), sb("out_work", [P, 4, T]))

        loaded = sem("l1_weights_loaded")
        with nc.Block() as block:
            @block.sync
            def _(sp):
                sp.dma_start(wq[:], dram["wq"].rearrange("(c p) n -> p c n", p=P)).then_inc(loaded, 16)
                sp.dma_start(wk[:], dram["wkv"][:, 0:s.I1].rearrange("(c p) n -> p c n", p=P)).then_inc(loaded, 16)
                sp.dma_start(wv[:], dram["wkv"][:, s.I1:2 * s.I1].rearrange("(c p) n -> p c n", p=P)).then_inc(loaded, 16)
                sp.dma_start(wo[:], dram["wo"].rearrange("(c p) n -> p c n", p=P)).then_inc(loaded, 16)
                sp.dma_start(null_k[:], dram["null_kv"][0].partition_broadcast(P)).then_inc(loaded, 16)
                sp.dma_start(null_col[0:DH, :], dram["null_kv"][0].unsqueeze(1)).then_inc(loaded, 16)
                sp.dma_start(null_col[DH:2 * DH, :], dram["null_kv"][0].unsqueeze(1)).then_inc(loaded, 16)
                sp.dma_start(null_v[:], dram["null_kv"][1:2, :]).then_inc(loaded, 16)
                sp.dma_start(ln_scale[:], dram["ln_scale"].partition_broadcast(P)).then_inc(loaded, 16)
                sp.dma_start(ln_bias[:], dram["ln_bias"].partition_broadcast(P)).then_inc(loaded, 16)
                sp.wait_ge(loaded, 160)

            @block.gpsimd
            def _(pool):
                nc.gpsimd.memset(null1[:].bitcast(F32), 0.0)
                nc.gpsimd.memset(null2[:].bitcast(F32), 0.0)
                nc.gpsimd.memset(ones[:], 1.0)
                nc.gpsimd.memset(max_cols[:], 0.0)
                pool.drain()
                nc.gpsimd.memset(k2[DH:DH + 1].bitcast(F32), 1.0)
                pool.drain()
                nc.gpsimd.memset(null2[DH:DH + 1, 0:1].bitcast(F32), 1.0)

        with nc.Block() as block:
            @block.vector
            def _(dve):
                nc.vector.tensor_scalar(ln_scale[:], ln_scale[:], g["gates"][:, 2:3], None, ALU.mult)
                nc.vector.tensor_scalar(ln_bias[:], ln_bias[:], g["gates"][:, 2:3], None, ALU.mult)
                for c in range(s.DC):
                    nc.vector.tensor_tensor(w_null_tmp[:], wq[:, c, :].rearrange("p (h k) -> p h k", h=H),
                                            null_k[:].unsqueeze(1).to_broadcast([P, H, DH]), ALU.mult)
                    dve.drain()
                    nc.vector.reduce_sum(w_null[:, c, :], w_null_tmp[:], AX_X)
                    dve.drain()
                nc.vector.tensor_copy(null1[:, 0:1], null_col[:])
                dve.drain()
                nc.vector.tensor_copy(null2[0:DH, 0:1], null_col[0:DH, :])
                nc.vector.tensor_tensor(null1[DH:P, 0:1], null_col[DH:P, :], null1[DH:P, 0:1].bitcast(F32), ALU.subtract)

        ctx_ready = sem("l1_ctx_ready")
        xn_ready = sem("l1_xn_ready")
        xT_psum = sem("l1_xT_psum")
        xT_act = sem("l1_xT_act")
        xT_dve = sem("l1_xT_dve")
        v_psum = sem("l1_v_psum")
        v_act = sem("l1_v_act")
        v_dve = sem("l1_v_dve")
        null_psum = sem("l1_null_psum")

        qk_psum = sem("l1_qk_psum")
        hi_done = sem("l1_hi_done")
        lo_done = sem("l1_lo_done")
        max_psum = sem("l1_max_psum")
        max_read = sem("l1_max_read")
        negmax = sem("l1_negmax")
        negmaxT = sem("l1_negmaxT")
        max_rows = sem("l1_max_rows")
        s_psum = sem("l1_s_psum")
        exp_done = sem("l1_exp_done")
        pv_done = sem("l1_pv_done")
        summed = sem("l1_summed")
        sums_psum = sem("l1_sums_psum")
        sums_read = sem("l1_sums_read")
        norm_done = sem("l1_norm_done")

        out_psum = sem("l1_out_psum")
        out_normed = sem("l1_out_normed")
        scaled = sem("l1_scaled")

        def tokens(b):
            return g["x"][:, b * T:(b + 1) * T, :]

        def begin_tensor(pe, b):
            pe.wait_ge(ctx_ready, 16 * (b + 1))
            for n in range(2 * KT):
                kt, half = divmod(n, 2)
                if n >= 4:
                    pe.wait_ge(v_act if n % 2 else v_dve, b * KT + (n - 4) // 2 + 1)
                for c in range(s.CC):
                    last = nc.tensor.matmul(bank(4 + n % 4), ctxT[:, c, kt * P:(kt + 1) * P],
                                            wv[:, c, half * BANK:(half + 1) * BANK],
                                            start=(c == 0), stop=(c == s.CC - 1))
                last.then_inc(v_psum, 1)
            pe.wait_ge(xn_ready, (b + 1) * T)
            for c in range(s.DC):
                pe.wait_ge(v_act if c else v_dve, (b + 1) * KT - 1)
                for t in range(T):
                    last = nc.tensor.transpose(bank(4 + c)[:, t * P:(t + 1) * P],
                                               xn[:, t, c * P:(c + 1) * P], g["ident"][:])
                last.then_inc(xT_psum, 1)
            pe.wait_ge(xT_act, b + 1)
            pe.wait_ge(xT_dve, b + 1)
            for t in range(T):
                for c in range(s.DC):
                    last = nc.tensor.matmul(bank(4)[:, t * H:(t + 1) * H], xT[:, c, t * P:(t + 1) * P],
                                            w_null[:, c, :], start=(c == 0), stop=(c == s.DC - 1))
            last.then_inc(null_psum, 1)

        def begin_scalar(act, b):
            for n in range(1, 2 * KT, 2):
                act.wait_ge(v_psum, 2 * KT * b + n + 1)
                nc.scalar.activation(v_sb[:, n // 2, BANK:2 * BANK], bank(4 + n % 4), ACT.Copy).then_inc(v_act, 1)
            act.wait_ge(xT_psum, 2 * b + 1)
            nc.scalar.activation(xT[:, 0, :], bank(4), ACT.Copy).then_inc(xT_act, 1)

        def begin_vector(dve, b):
            x_b = tokens(b)
            norm.statistics(dve, lambda t: x_b[:, t, :], LN_EPS)
            for t in range(T):
                norm.apply(xn[:, t, :], x_b[:, t, :], t).then_inc(xn_ready, 1)
            for n in range(0, 2 * KT, 2):
                dve.wait_ge(v_psum, 2 * KT * b + n + 1)
                nc.vector.tensor_copy(v_sb[:, n // 2, 0:BANK], bank(4 + n % 4)).then_inc(v_dve, 1)
            dve.wait_ge(xT_psum, 2 * b + 2)
            nc.vector.tensor_copy(xT[:, 1, :], bank(5)).then_inc(xT_dve, 1)
            dve.wait_ge(null_psum, b + 1)
            nc.vector.tensor_copy(s_null[:], bank(4)[:, 0:T * H].rearrange("p (t h) -> p t h", t=T))

        def end_tensor(pe, b):
            for t in range(T):
                for p in range(PAIRS):
                    last = nc.tensor.matmul(bank(t)[:, 0:D], oT[:, p, t * P:(t + 1) * P], wo[:, p, :],
                                            start=(p == 0), stop=(p == PAIRS - 1))
                last.then_inc(out_psum, 1)

        def end_vector(dve, b):
            x_b = tokens(b)
            dve.wait_ge(out_psum, (b + 1) * T)
            norm_out.statistics(dve, lambda t: bank(t)[:, 0:D], LN_OUT_EPS)
            for t in range(T):
                norm_out.apply(out_n[:, t, :], bank(t)[:, 0:D], t).then_inc(out_normed, 1)
            for t in range(T):
                dve.wait_ge(scaled, b * T + t + 1)
                nc.vector.tensor_tensor(x_b[:, t, :], x_bias[:, t, :], out_n[:, t, :], ALU.add)

        def end_gpsimd(pool, b):
            x_b = tokens(b)
            for t in range(T):
                nc.gpsimd.tensor_tensor(x_bias[:, t, :], x_b[:, t, :], ln_bias[:], ALU.add)
            for t in range(T):
                pool.wait_ge(out_normed, b * T + t + 1)
                nc.gpsimd.tensor_tensor(out_n[:, t, :], out_n[:, t, :], ln_scale[:], ALU.mult).then_inc(scaled, 1)

        for b in range(s.B + 1):
            with nc.Block() as block:
                if b < s.B:
                    @block.sync
                    def _(sp):
                        sp.dma_start(ctxT[:], dram["ctxT"][b].rearrange("(c p) n -> p c n", p=P)).then_inc(ctx_ready, 16)

                    @block.scalar
                    def _(act):
                        begin_scalar(act, b)

                @block.tensor
                def _(pe):
                    if b >= 1:
                        end_tensor(pe, b - 1)
                    if b < s.B:
                        begin_tensor(pe, b)

                @block.vector
                def _(dve):
                    if b >= 1:
                        end_vector(dve, b - 1)
                    if b < s.B:
                        begin_vector(dve, b)

                if b >= 1:
                    @block.gpsimd
                    def _(pool):
                        end_gpsimd(pool, b - 1)
            if b == s.B:
                break

            FIRST_MAX = 4
            with nc.Block() as block:
                @block.tensor
                def _(pe):
                    def project(p):
                        if p >= 1:
                            pe.wait_ge(lo_done, b * PAIRS + p)
                        for c in range(s.DC):
                            nc.tensor.matmul(bank(6), wq[:, c, p * P:(p + 1) * P], xT[:, c, :],
                                             start=(c == 0), stop=(c == s.DC - 1))
                        for c in range(s.CC):
                            last = nc.tensor.matmul(bank(7), wk[:, c, p * P:(p + 1) * P], ctxT[:, c, :],
                                                    start=(c == 0), stop=(c == s.CC - 1))
                        last.then_inc(qk_psum, 1)

                    def max_scores(p, i):
                        j, t = divmod(i, T)
                        if i == 0:
                            pe.wait_ge(lo_done, b * PAIRS + p + 1)
                            if p >= 1:
                                pe.wait_ge(max_rows, b * PAIRS + p)
                        elif i == 1:
                            if p >= 2:
                                pe.wait_ge(sums_read, b * PAIRS + p - 1)
                        else:
                            pe.wait_ge(max_read, (b * PAIRS + p) * 2 * T + i - 1)
                        out = bank(2 + i % 2)
                        nc.tensor.matmul(out, q1[:, p % 2, j, t * P:(t + 1) * P], k1[:, p % 2, j, :],
                                         start=True, stop=False)
                        nc.tensor.matmul(out, q2[0:DH, p % 2, j, t * P:(t + 1) * P], k2[0:DH, p % 2, j, :],
                                         start=False, stop=True).then_inc(max_psum, 1)

                    def transpose_max(p):
                        pe.wait_ge(negmax, b * PAIRS + p + 1)
                        for t in range(T):
                            last = nc.tensor.transpose(bank(2)[:, t * P:(t + 1) * P], max_cols[:, t, :], g["ident"][:])
                        last.then_inc(negmaxT, 1)

                    def scores(p, u):
                        kt, j = divmod(u, 2)
                        n = p * UNITS + u
                        if n >= 2:
                            pe.wait_ge(exp_done, b * PAIRS * UNITS + n - 1)
                        if u == 0:
                            pe.wait_ge(max_rows, b * PAIRS + p + 1)
                        if kt < KT:
                            first, second = k1[:, p % 2, j, kt * P:(kt + 1) * P], k2[0:DH + 1, p % 2, j, kt * P:(kt + 1) * P]
                        else:
                            first, second = null1[:], null2[0:DH + 1, :]
                        nc.tensor.matmul(bank(n % 2), first, q1[:, p % 2, j, :], start=True, stop=False)
                        nc.tensor.matmul(bank(n % 2), second, q2[0:DH + 1, p % 2, j, :],
                                         start=False, stop=True).then_inc(s_psum, 1)

                    def weigh_values(p, kt):
                        pe.wait_ge(exp_done, b * PAIRS * UNITS + p * UNITS + 2 * kt + 2)
                        if kt == 0 and p >= 2:
                            pe.wait_ge(norm_done, b * PAIRS + p - 1)
                        for j in range(2):
                            h = 2 * p + j
                            if kt < KT:
                                lhsT, rhs = v_sb[:, kt, h * DH:(h + 1) * DH], probs[:, (p * 2 * KT + 2 * kt + j) % RING, :]
                            else:
                                lhsT, rhs = null_v[:], null_p[:, j, :]
                            last = nc.tensor.matmul(bank(4 + p % 2)[j * DH:(j + 1) * DH, :], lhsT, rhs, start=(kt == 0),
                                                    stop=(kt == KT), tile_position=(0, j * DH), skip_group_check=True)
                        last.then_inc(pv_done, 1)

                    def sums(p):
                        pe.wait_ge(summed, b * PAIRS + p + 1)
                        if p == PAIRS - 1:
                            pe.wait_ge(sums_read, b * PAIRS + p)
                        elif p + 1 < PAIRS:
                            pe.wait_ge(max_read, (b * PAIRS + p + 2) * 2 * T)
                        for j in range(2):
                            last = nc.tensor.matmul(bank(3)[j * DH:(j + 1) * DH, :], ones[:], p_sum[:, j, :], start=True,
                                                    stop=True, tile_position=(0, j * DH), skip_group_check=True)
                        last.then_inc(sums_psum, 1)

                    project(0)
                    for i in range(2 * T):
                        max_scores(0, i)
                    project(1)
                    transpose_max(0)
                    for p in range(PAIRS):
                        later = iter(range(2 * T))
                        for kt in range(KT + 1):
                            for j in range(2):
                                u = 2 * kt + j
                                scores(p, u)
                                if p + 1 < PAIRS and u >= FIRST_MAX:
                                    max_scores(p + 1, next(later))
                            if kt >= 1:
                                weigh_values(p, kt - 1)
                        if p + 1 < PAIRS:
                            for i in later:
                                max_scores(p + 1, i)
                        weigh_values(p, KT)
                        if p + 2 < PAIRS:
                            project(p + 2)
                        if p + 1 < PAIRS:
                            transpose_max(p + 1)
                        sums(p)

                @block.scalar
                def _(act):
                    def high_parts(p):
                        q, k, i = bank(6), bank(7), p % 2
                        for j in range(2):
                            rows = slice(j * DH, (j + 1) * DH)
                            for dst, src in ((q1[0:DH, i, j, :], q), (q1[DH:P, i, j, :], q),
                                             (k1[rows, i, j, :], k), (k2[0:DH, i, j, :], k)):
                                yield nc.scalar.activation(dst, src[rows, :], ACT.Copy)

                    def place_max(p):
                        act.wait_ge(negmaxT, b * PAIRS + p + 1)
                        for j in range(2):
                            last = nc.scalar.activation(q2[DH:DH + 1, p % 2, j, :], bank(2)[j * DH:j * DH + 1, :], ACT.Copy)
                        last.then_inc(max_rows, 1)

                    act.wait_ge(qk_psum, b * PAIRS + 1)
                    for last in high_parts(0):
                        pass
                    last.then_inc(hi_done, 1)
                    place_max(0)
                    for p in range(PAIRS):
                        parts = high_parts(p + 1) if p + 1 < PAIRS else iter(())
                        for u in range(UNITS):
                            kt, j = divmod(u, 2)
                            n = p * UNITS + u
                            act.wait_ge(s_psum, b * PAIRS * UNITS + n + 1)
                            if kt < KT:
                                m = p * 2 * KT + u
                                if m >= RING:
                                    back_p, back_u = divmod(m - RING, 2 * KT)
                                    act.wait_ge(pv_done, b * PAIRS * (KT + 1) + back_p * (KT + 1) + back_u // 2 + 1)
                                    act.wait_ge(summed, b * PAIRS + back_p + 1)
                                nc.scalar.activation(probs[:, m % RING, :], bank(n % 2), ACT.Exp, scale=SCALE).then_inc(exp_done, 1)
                            else:
                                if p >= 1 and j == 0:
                                    act.wait_ge(pv_done, b * PAIRS * (KT + 1) + p * (KT + 1))
                                    act.wait_ge(summed, b * PAIRS + p)
                                nc.scalar.activation(null_p[:, j, :], bank(n % 2)[0:1, :], ACT.Exp, scale=SCALE).then_inc(exp_done, 1)
                            if p + 1 < PAIRS:
                                if u == 0:
                                    act.wait_ge(qk_psum, b * PAIRS + p + 2)
                                for _ in range(2):
                                    last = next(parts, None)
                                    if last is not None and u == 3 and _ == 1:
                                        last.then_inc(hi_done, 1)
                        if p + 1 < PAIRS:
                            place_max(p + 1)

                @block.gpsimd
                def _(pool):
                    for p in range(PAIRS):
                        if p >= 1:
                            pool.wait_ge(sums_psum, b * PAIRS + p)
                        for kt in range(1, KT):
                            pool.wait_ge(exp_done, b * PAIRS * UNITS + p * UNITS + 2 * kt + 2)
                            for j in range(2):
                                m = p * 2 * KT + 2 * kt + j
                                first = probs[:, (m - 2) % RING, :] if kt == 1 else p_sum[:, j, :]
                                nc.gpsimd.tensor_tensor(p_sum[:, j, :], first, probs[:, m % RING, :], ALU.add)
                            pool.drain()
                        pool.wait_ge(exp_done, b * PAIRS * UNITS + (p + 1) * UNITS)
                        for j in range(2):
                            last = nc.gpsimd.tensor_tensor(p_sum[0:1, j, :], p_sum[0:1, j, :], null_p[:, j, :], ALU.add)
                        last.then_inc(summed, 1)

                @block.vector
                def _(dve):
                    def split_low(p):
                        dve.wait_ge(hi_done, b * PAIRS + p + 1)
                        q, k, i = bank(6), bank(7), p % 2
                        for j in range(2):
                            rows, other = slice(j * DH, (j + 1) * DH), slice((1 - j) * DH, (2 - j) * DH)
                            nc.vector.tensor_tensor(q2[0:DH, i, j, :], q[rows, :], q1[rows, i, j, :].bitcast(F32), ALU.subtract)
                            last = nc.vector.tensor_tensor(k1[other, i, j, :], k[rows, :], k1[rows, i, j, :].bitcast(F32), ALU.subtract)
                        last.then_inc(lo_done, 1)

                    def maxima(p):
                        for i in range(2 * T):
                            j, t = divmod(i, T)
                            dve.wait_ge(max_psum, b * PAIRS * 2 * T + p * 2 * T + i + 1)
                            nc.vector.reduce_max(tile_max[:, j, t:t + 1], bank(2 + i % 2), AX_X).then_inc(max_read, 1)
                        dve.drain()
                        nc.vector.tensor_tensor(max_tmp[:], tile_max[:],
                                                s_null[:, :, 2 * p:2 * p + 2].rearrange("p t j -> p j t"), ALU.max)
                        dve.drain()
                        nc.vector.tensor_scalar(max_cols[:, :, 0:P:DH].bitcast(F32R), max_tmp[:].rearrange("p j t -> p t j"),
                                                -1.0, None, ALU.mult).then_inc(negmax, 1)

                    def normalize(p):
                        dve.wait_ge(sums_psum, b * PAIRS + p + 1)
                        dve.drain()
                        nc.vector.reciprocal(denom[:], bank(3)).then_inc(sums_read, 1)
                        dve.drain()
                        nc.vector.tensor_tensor(oT[:, p, :], bank(4 + p % 2), denom[:], ALU.mult).then_inc(norm_done, 1)

                    split_low(0)
                    maxima(0)
                    for p in range(PAIRS):
                        if p >= 1:
                            normalize(p - 1)
                        if p + 1 < PAIRS:
                            split_low(p + 1)
                            maxima(p + 1)
                    normalize(PAIRS - 1)


def experts(nc, s, g, bank, dram, out):
    T, D, E, N, B = s.T, s.D, s.E, s.N, s.B
    TB = s.TT
    NB = T // TB
    TOP = 2
    ROWS = 256
    HALVES = ROWS // P
    TILES = TOP * T * P // ROWS + E - 1
    MOST = -(-T * P // ROWS)
    FT = s.FT

    xs_dram = nc.dram_tensor("moe_sorted_x", [TILES * ROWS, D], F32).ap()
    y_dram = nc.dram_tensor("moe_sorted_y", [TILES * ROWS, D], F32).ap()

    with ExitStack() as ctx:
        def sb(name, shape, dt=F32):
            return ctx.enter_context(nc.sbuf_tensor("moe_" + name, shape, dt))

        def sem(name):
            return ctx.enter_context(nc.semaphore(name))

        w_router = sb("w_router", [P, s.DC, E])
        b_router = sb("b_router", [P, E])
        xn = sb("xn", [P, T, D])
        xT = sb("xT", [P, s.DC, T * P])
        w1 = sb("w1", [P, 2, s.DC, s.F])
        w3 = sb("w3", [P, 2, s.DC, s.F])
        w2 = sb("w2", [P, 2, s.FT, D])
        zeros = sb("zeros", [P, D])
        lower = sb("lower", [P, P])
        ones = sb("ones", [P, P])
        logits = sb("logits", [P, T, E])
        cmp = sb("cmp", [P, T, E, E])
        tie = sb("tie", [P, T, E, E])
        before = sb("before", [P, E, E])
        steps = sb("steps", [P, MOST])
        tile_no = sb("tile_no", [P, TILES])
        rank = sb("rank", [P, T, E])
        chosen = sb("chosen", [P, TOP, T, E])
        either = sb("either", [P, T, E])
        work8 = sb("work8", [P, T, E])
        top = sb("top", [P, 4, T])
        weight = sb("weight", [P, TOP, T])
        sums = sb("sums", [P, 2, T + 1, E])
        full = sb("full", [P, E, MOST])
        n_tiles = sb("n_tiles", [P, 2, E + 1])
        past = sb("past", [P, TILES, E])
        tile_expert = sb("tile_expert", [P, TILES])
        expert_ids = sb("expert_ids", [P, TILES], U32)
        slot = sb("slot", [P, TOP, T])
        slot_ids = sb("slot_ids", [P, TOP, T], U32)
        rows = sb("rows", [P, TOP * T, D])
        xs = sb("xs", [P, 2, HALVES, D])
        xsT = sb("xsT", [P, 2, s.DC, ROWS])
        gate = sb("gate", [P, 3, ROWS])
        hid = sb("hid", [P, 3, ROWS])
        y_sb = sb("y_sb", [P, 2, HALVES, D])
        stats = sb("stats", [P, TB, 6])
        mv = sb("mv", [P, TB, 2])
        work = sb("work", [P, 4, TB])
        norm = Norm(nc, TB, stats, mv, work)

        loaded = sem("moe_router_loaded")
        zeroed = sem("moe_zeroed")
        cleared = sem("moe_cleared")
        xn_ready = sem("moe_xn_ready")
        xT_psum = sem("moe_xT_psum")
        xT_act = sem("moe_xT_act")
        xT_dve = sem("moe_xT_dve")
        lg_psum = sem("moe_lg_psum")
        tops = sem("moe_tops")
        exped = sem("moe_exped")
        either_ready = sem("moe_either_ready")
        prefix_psum = sem("moe_prefix_psum")
        scaled = sem("moe_scaled")
        scattered = sem("moe_scattered")

        with nc.Block() as block:
            @block.sync
            def _(sp):
                sp.dma_start(w_router[:], dram["w_router"].rearrange("(c p) n -> p c n", p=P)).then_inc(loaded, 16)
                sp.dma_start(b_router[:], dram["b_router"].partition_broadcast(P)).then_inc(loaded, 16)
                sp.wait_ge(zeroed, 1)
                sp.dma_start(xs_dram.rearrange("(n p) d -> p n d", p=P),
                             zeros[:].unsqueeze(1).to_broadcast([P, TILES * HALVES, D])).then_inc(cleared, 16)

            @block.gpsimd
            def _(pool):
                nc.gpsimd.memset(zeros[:], 0.0).then_inc(zeroed, 1)
                nc.gpsimd.memset(before[:], 1.0)
                nc.gpsimd.memset(ones[:], 1.0)
                nc.gpsimd.memset(lower[:], 1.0)
                nc.gpsimd.iota(steps[:], pattern=[[ROWS, MOST]], base=0, channel_multiplier=0,
                               allow_small_or_imprecise_dtypes=True)
                nc.gpsimd.iota(tile_no[:], pattern=[[1, TILES]], base=0, channel_multiplier=0,
                               allow_small_or_imprecise_dtypes=True)
                pool.drain()
                nc.gpsimd.affine_select(out=before[:], in_=before[:], compare_op=ALU.is_gt, fill=0.0, base=0,
                                        pattern=[[1, E], [-1, E]], channel_multiplier=0)
                nc.gpsimd.affine_select(out=lower[:], in_=lower[:], compare_op=ALU.is_gt, fill=0.0, base=0,
                                        pattern=[[1, P]], channel_multiplier=-1)

            @block.vector
            def _(dve):
                for b in range(NB):
                    x_b = g["x"][:, b * TB:(b + 1) * TB, :]
                    norm.statistics(dve, lambda t: x_b[:, t, :], LN_EPS)
                    for t in range(TB):
                        norm.apply(xn[:, b * TB + t, :], x_b[:, t, :], t).then_inc(xn_ready, 1)
                    if b >= 1:
                        dve.wait_ge(xT_psum, 2 * b)
                        nc.vector.tensor_copy(xT[:, 1, (b - 1) * N:b * N], bank(2 * ((b - 1) % 2) + 1)).then_inc(xT_dve, 1)
                dve.wait_ge(xT_psum, 2 * NB)
                nc.vector.tensor_copy(xT[:, 1, (NB - 1) * N:NB * N], bank(2 * ((NB - 1) % 2) + 1)).then_inc(xT_dve, 1)
                dve.wait_ge(lg_psum, 1)
                dve.wait_ge(loaded, 32)
                nc.vector.tensor_tensor(logits[:], bank(4)[:, 0:T * E].rearrange("p (t e) -> p t e", t=T),
                                        b_router[:].unsqueeze(1).to_broadcast([P, T, E]), ALU.add)

            @block.scalar
            def _(act):
                for b in range(NB):
                    act.wait_ge(xT_psum, 2 * b + 1)
                    nc.scalar.activation(xT[:, 0, b * N:(b + 1) * N], bank(2 * (b % 2)), ACT.Copy).then_inc(xT_act, 1)

            @block.tensor
            def _(pe):
                for b in range(NB):
                    pe.wait_ge(xn_ready, (b + 1) * TB)
                    if b >= 2:
                        pe.wait_ge(xT_act, b - 1)
                        pe.wait_ge(xT_dve, b - 1)
                    for c in range(s.DC):
                        for t in range(TB):
                            last = nc.tensor.transpose(bank(2 * (b % 2) + c)[:, t * P:(t + 1) * P],
                                                       xn[:, b * TB + t, c * P:(c + 1) * P], g["ident"][:])
                        last.then_inc(xT_psum, 1)
                pe.wait_ge(loaded, 32)
                pe.wait_ge(xT_act, NB)
                pe.wait_ge(xT_dve, NB)
                for t in range(T):
                    for c in range(s.DC):
                        last = nc.tensor.matmul(bank(4)[:, t * E:(t + 1) * E], xT[:, c, t * P:(t + 1) * P],
                                                w_router[:, c, :], start=(c == 0), stop=(c == s.DC - 1))
                last.then_inc(lg_psum, 1)

        with nc.Block() as block:
            @block.vector
            def _(dve):
                mine = logits[:].unsqueeze(3).to_broadcast([P, T, E, E])
                other = logits[:].unsqueeze(2).to_broadcast([P, T, E, E])
                nc.vector.tensor_tensor(cmp[:], other, mine, ALU.is_gt)
                nc.vector.tensor_tensor(tie[:], other, mine, ALU.is_equal)
                dve.drain()
                nc.vector.tensor_tensor(tie[:].rearrange("p t e j -> p t (e j)"), tie[:].rearrange("p t e j -> p t (e j)"),
                                        before[:].rearrange("p e j -> p (e j)").unsqueeze(1).to_broadcast([P, T, E * E]),
                                        ALU.mult)
                dve.drain()
                nc.vector.tensor_tensor(cmp[:], cmp[:], tie[:], ALU.add)
                dve.drain()
                nc.vector.reduce_sum(rank[:], cmp[:], AX_X)
                dve.drain()
                for k in range(TOP):
                    nc.vector.tensor_scalar(chosen[:, k], rank[:], float(k), None, ALU.is_equal)
                nc.vector.tensor_scalar(either[:], rank[:], float(TOP), None, ALU.is_lt).then_inc(either_ready, 1)
                dve.drain()
                nc.vector.tensor_tensor(work8[:], chosen[:, 1], logits[:], ALU.mult)
                nc.vector.reduce_max(top[:, 0, :], logits[:], AX_X)
                dve.drain()
                nc.vector.reduce_sum(top[:, 1, :], work8[:], AX_X)
                dve.drain()
                nc.vector.tensor_tensor(top[:, 2, :], top[:, 1, :], top[:, 0, :], ALU.subtract).then_inc(tops, 1)
                dve.wait_ge(exped, 1)
                nc.vector.tensor_scalar(top[:, 0, :], top[:, 3, :], 1.0, None, ALU.add)
                dve.drain()
                nc.vector.reciprocal(weight[:, 0, :], top[:, 0, :])
                dve.drain()
                nc.vector.tensor_tensor(weight[:, 1, :], top[:, 3, :], weight[:, 0, :], ALU.mult)
                dve.drain()
                for t in range(T):
                    for k in range(TOP):
                        nc.vector.tensor_scalar(rows[:, TOP * t + k, :], xn[:, t, :], weight[:, k, t:t + 1], None, ALU.mult)

                dve.wait_ge(prefix_psum, 2)
                nc.vector.memset(sums[:, 0, 0:1, :], 0.0)
                nc.vector.tensor_copy(sums[:, 0, 1:T + 1, :], bank(1)[:, 0:T * E].rearrange("p (t e) -> p t e", t=T))
                src, d = 0, 1
                while d <= T:
                    dve.drain()
                    nc.vector.tensor_copy(sums[:, 1 - src, 0:d, :], sums[:, src, 0:d, :])
                    nc.vector.tensor_tensor(sums[:, 1 - src, d:T + 1, :], sums[:, src, d:T + 1, :],
                                            sums[:, src, 0:T + 1 - d, :], ALU.add)
                    src, d = 1 - src, 2 * d
                dve.drain()
                nc.vector.tensor_tensor(full[:], sums[:, src, T, :].unsqueeze(2).to_broadcast([P, E, MOST]),
                                        steps[:].unsqueeze(1).to_broadcast([P, E, MOST]), ALU.is_gt)
                nc.vector.tensor_tensor(work8[:], sums[:, src, 0:T, :],
                                        bank(0)[:, 0:T * E].rearrange("p (t e) -> p t e", t=T), ALU.add)
                dve.drain()
                nc.vector.memset(n_tiles[:, 0, 0:1], 0.0)
                nc.vector.reduce_sum(n_tiles[:, 0, 1:E + 1], full[:], AX_X)
                src, d = 0, 1
                while d <= E:
                    dve.drain()
                    nc.vector.tensor_copy(n_tiles[:, 1 - src, 0:d], n_tiles[:, src, 0:d])
                    nc.vector.tensor_tensor(n_tiles[:, 1 - src, d:E + 1], n_tiles[:, src, d:E + 1],
                                            n_tiles[:, src, 0:E + 1 - d], ALU.add)
                    src, d = 1 - src, 2 * d
                dve.drain()
                nc.vector.tensor_tensor(past[:], tile_no[:].unsqueeze(2).to_broadcast([P, TILES, E]),
                                        n_tiles[:, src, 1:E + 1].unsqueeze(1).to_broadcast([P, TILES, E]), ALU.is_ge)
                nc.vector.tensor_scalar(n_tiles[:, 1 - src, 0:E], n_tiles[:, src, 0:E], float(ROWS), None, ALU.mult)
                dve.drain()
                nc.vector.reduce_sum(tile_expert[:], past[:], AX_X)
                nc.vector.tensor_tensor(work8[:], work8[:], n_tiles[:, 1 - src, 0:E].unsqueeze(1).to_broadcast([P, T, E]),
                                        ALU.add)
                dve.drain()
                nc.vector.tensor_scalar(expert_ids[:], tile_expert[:], float(E - 1), None, ALU.min)
                for k in range(TOP):
                    nc.vector.tensor_tensor(chosen[:, k], chosen[:, k], work8[:], ALU.mult)
                dve.drain()
                for k in range(TOP):
                    nc.vector.reduce_sum(slot[:, k, :], chosen[:, k], AX_X)
                dve.drain()
                nc.vector.tensor_copy(slot_ids[:], slot[:]).then_inc(scaled, 1)

            @block.scalar
            def _(act):
                act.wait_ge(tops, 1)
                nc.scalar.activation(top[:, 3, :], top[:, 2, :], ACT.Exp).then_inc(exped, 1)

            @block.tensor
            def _(pe):
                pe.wait_ge(either_ready, 1)
                flat = either[:].rearrange("p t e -> p (t e)")
                nc.tensor.matmul(bank(0)[:, 0:T * E], lower[:], flat, start=True, stop=True).then_inc(prefix_psum, 1)
                nc.tensor.matmul(bank(1)[:, 0:T * E], ones[:], flat, start=True, stop=True).then_inc(prefix_psum, 1)

            @block.gpsimd
            def _(pool):
                pool.wait_ge(cleared, 16)
                pool.wait_ge(scaled, 1)
                for t in range(T):
                    for k in range(TOP):
                        nc.gpsimd.indirect_dma_start(
                            out=xs_dram, out_offset=bass.IndirectOffsetOnAxis(ap=slot_ids[:, k, t:t + 1], axis=0),
                            in_=rows[:, TOP * t + k, :], in_offset=None).then_inc(scattered, 16)
                pool.wait_ge(scattered, 16 * TOP * T)

        w_ready = [sem(f"moe_w_ready_{i}") for i in range(2)]
        xs_ready = [sem(f"moe_xs_ready_{i}") for i in range(2)]
        xsT_psum = sem("moe_xsT_psum")
        xsT_ready = sem("moe_xsT_ready")
        up_psum = sem("moe_up_psum")
        gate_done = sem("moe_gate_done")
        hid_ready = sem("moe_hid_ready")
        y_psum = sem("moe_y_psum")
        y_ready = sem("moe_y_ready")
        y_stored = [sem(f"moe_y_stored_{i}") for i in range(2)]

        with nc.Block() as block:
            @block.sync
            def _(sp):
                for i in range(TILES):
                    slot_i = i % 2
                    if i >= 2:
                        sp.wait_ge(y_psum, i - 1)
                    e = sp.value_load(expert_ids[0:1, i:i + 1], min_val=0, max_val=E - 1)
                    sp.dma_start(xs[:, slot_i], xs_dram[i * ROWS:(i + 1) * ROWS, :].rearrange("(h p) d -> p h d", p=P)
                                 ).then_inc(xs_ready[slot_i], 16)
                    for dst, name in ((w1, "moe_w1"), (w3, "moe_w3"), (w2, "moe_w2")):
                        sp.dma_start(dst[:, slot_i], dram[name][bass.ds(e, 1)].rearrange("o (c p) n -> p (o c) n", p=P)
                                     ).then_inc(w_ready[slot_i], 16)

            @block.tensor
            def _(pe):
                def transposes(i):
                    pe.wait_ge(xs_ready[i % 2], 16 * (i // 2 + 1))
                    if i >= 1:
                        pe.wait_ge(xsT_ready, i)
                    for c in range(s.DC):
                        for h in range(HALVES):
                            last = nc.tensor.transpose(bank(7)[:, c * ROWS + h * P:c * ROWS + (h + 1) * P],
                                                       xs[:, i % 2, h, c * P:(c + 1) * P], g["ident"][:])
                    last.then_inc(xsT_psum, 1)

                def down(i, f):
                    k = i * FT + f
                    pe.wait_ge(hid_ready, k + 1)
                    if f == 0 and i >= 2:
                        pe.wait_ge(y_ready, i - 1)
                    for h in range(HALVES):
                        last = nc.tensor.matmul(bank(3 + 2 * (i % 2) + h)[:, 0:D], hid[:, k % 3, h * P:(h + 1) * P],
                                                w2[:, i % 2, f, :], start=(f == 0), stop=(f == FT - 1))
                    if f == FT - 1:
                        last.then_inc(y_psum, 1)

                transposes(0)
                for i in range(TILES):
                    pe.wait_ge(w_ready[i % 2], 48 * (i // 2 + 1))
                    pe.wait_ge(xsT_ready, i + 1)
                    for f in range(FT):
                        k = i * FT + f
                        if k >= 3:
                            pe.wait_ge(hid_ready, k - 2)
                        for n, w in enumerate((w1, w3)):
                            for c in range(s.DC):
                                last = nc.tensor.matmul(bank(k % 3)[:, n * ROWS:(n + 1) * ROWS],
                                                        w[:, i % 2, c, f * P:(f + 1) * P], xsT[:, i % 2, c, :],
                                                        start=(c == 0), stop=(c == s.DC - 1))
                        last.then_inc(up_psum, 1)
                        if f >= 1:
                            down(i, f - 1)
                        if f == FT - 2 and i + 1 < TILES:
                            transposes(i + 1)
                    down(i, FT - 1)

            @block.scalar
            def _(act):
                for k in range(TILES * FT):
                    act.wait_ge(up_psum, k + 1)
                    if k >= 3:
                        act.wait_ge(hid_ready, k - 2)
                    nc.scalar.activation(gate[:, k % 3, :], bank(k % 3)[:, 0:ROWS], ACT.Silu).then_inc(gate_done, 1)

            @block.vector
            def _(dve):
                def evacuate_xsT(i):
                    dve.wait_ge(xsT_psum, i + 1)
                    nc.vector.tensor_copy(xsT[:, i % 2], bank(7).rearrange("p (c n) -> p c n", c=s.DC)).then_inc(xsT_ready, 1)

                def evacuate_y(i):
                    dve.wait_ge(y_psum, i + 1)
                    if i >= 2:
                        dve.wait_ge(y_stored[i % 2], 16 * (i // 2))
                    for h in range(HALVES):
                        last = nc.vector.tensor_copy(y_sb[:, i % 2, h, :], bank(3 + 2 * (i % 2) + h)[:, 0:D])
                    last.then_inc(y_ready, 1)

                evacuate_xsT(0)
                for i in range(TILES):
                    for f in range(FT):
                        k = i * FT + f
                        dve.wait_ge(gate_done, k + 1)
                        nc.vector.tensor_tensor(hid[:, k % 3, :], bank(k % 3)[:, ROWS:2 * ROWS], gate[:, k % 3, :],
                                                ALU.mult).then_inc(hid_ready, 1)
                        if f == 1 and i >= 1:
                            evacuate_y(i - 1)
                    if i + 1 < TILES:
                        evacuate_xsT(i + 1)
                evacuate_y(TILES - 1)

            @block.gpsimd
            def _(pool):
                for t in range(T):
                    nc.gpsimd.tensor_scalar(xn[:, t, :], xn[:, t, :], g["gates"][:, 3:4], None, ALU.mult)
                pool.drain()
                for t in range(T):
                    nc.gpsimd.tensor_tensor(g["x"][:, t, :], g["x"][:, t, :], xn[:, t, :], ALU.add)
                for i in range(TILES):
                    pool.wait_ge(y_ready, i + 1)
                    pool.dma_start(y_dram[i * ROWS:(i + 1) * ROWS, :].rearrange("(h p) d -> p h d", p=P),
                                   y_sb[:, i % 2]).then_inc(y_stored[i % 2], 16)
                pool.wait_ge(y_stored[0], 16 * ((TILES + 1) // 2))
                pool.wait_ge(y_stored[1], 16 * (TILES // 2))

        gathered = [sem(f"moe_gathered_{t}") for t in range(T)]
        added = sem("moe_added")
        fin = sem("moe_fin")
        stored = sem("moe_stored")
        with nc.Block() as block:
            @block.gpsimd
            def _(pool):
                for t in range(T):
                    for k in range(TOP):
                        nc.gpsimd.indirect_dma_start(
                            out=rows[:, TOP * t + k, :], out_offset=None, in_=y_dram,
                            in_offset=bass.IndirectOffsetOnAxis(ap=slot_ids[:, k, t:t + 1], axis=0)).then_inc(gathered[t], 16)

            @block.vector
            def _(dve):
                for t in range(T):
                    dve.wait_ge(gathered[t], 16 * TOP)
                    nc.vector.tensor_tensor(rows[:, TOP * t, :], rows[:, TOP * t, :], rows[:, TOP * t + 1, :], ALU.add)
                    dve.drain()
                    nc.vector.scalar_tensor_tensor(out=g["x"][:, t, :], in0=rows[:, TOP * t, :], scalar=g["gates"][:, 3:4],
                                                   in1=g["x"][:, t, :], op0=ALU.mult, op1=ALU.add).then_inc(fin, 1)

            @block.sync
            def _(sp):
                for b in range(B):
                    sp.wait_ge(fin, (b + 1) * TB)
                    sp.dma_start(out[b].rearrange("(t p) n -> p t n", p=P), g["x"][:, b * TB:(b + 1) * TB, :]).then_inc(stored, 16)
                sp.wait_ge(stored, 16 * B)


def flamingo(nc, dram, out):
    s = Shapes(dram["x"], dram["ctx"], dram["w_in"], dram["w_router"], dram["moe_w1"], dram["null_kv"], dram["wq"])
    with ExitStack() as ctx:
        def sb(name, shape, dt=F32):
            return ctx.enter_context(nc.sbuf_tensor(name, shape, dt))

        psum = ctx.enter_context(nc.psum_tensor("psum", [P, 8 * BANK], F32))

        def bank(i):
            return psum[:, i * BANK:(i + 1) * BANK]

        def wide(i):
            return psum[:, i * BANK:(i + 2) * BANK]

        g = {"x": sb("x_resid", [P, s.T, s.D]), "ident": sb("ident", [P, P]), "gates": sb("gates", [P, 4])}
        gates_raw = sb("gates_raw", [P, 4])
        x_loaded = ctx.enter_context(nc.semaphore("x_loaded"))
        gates_loaded = ctx.enter_context(nc.semaphore("gates_loaded"))
        with nc.Block() as block:
            @block.sync
            def _(sp):
                for i in range(2):
                    for j, name in enumerate(("g_xattn", "g_ffn")):
                        sp.dma_start(gates_raw[:, 2 * i + j:2 * i + j + 1],
                                     dram[name][i:i + 1].partition_broadcast(P)).then_inc(gates_loaded, 16)
                for b in range(s.B):
                    sp.dma_start(g["x"][:, b * s.TT:(b + 1) * s.TT, :],
                                 dram["x"][b].rearrange("(t p) n -> p t n", p=P)).then_inc(x_loaded, 16)
                sp.wait_ge(x_loaded, 16 * s.B)

            @block.gpsimd
            def _(pool):
                nc.gpsimd.memset(g["ident"][:], 0.0)
                pool.drain()
                nc.gpsimd.affine_select(out=g["ident"][:], in_=g["ident"][:], compare_op=ALU.not_equal, fill=1.0,
                                        base=0, pattern=[[-1, P]], channel_multiplier=1)

            @block.scalar
            def _(act):
                act.wait_ge(gates_loaded, 64)
                nc.scalar.activation(g["gates"][:], gates_raw[:], ACT.Tanh)

        layer0(nc, s, g, bank, wide, dram)
        layer1(nc, s, g, bank, dram)
        experts(nc, s, g, bank, dram, out)


def kernel(**inputs):
    import numpy as np
    import concourse.bacc as bacc
    from concourse.bass_utils import run_bass_kernel_spmd

    a = {k: np.asarray(v) for k, v in inputs.items()}
    arrays = {
        "x": a["x"], "ctx": a["ctx_2048"], "ctxT": a["ctx_2048"].transpose(0, 2, 1),
        "g_xattn": a["g_xattn"], "g_ffn": a["g_ffn"],
        "w_qkvT": a["L0_xattn_w_qkv"].T, "w_projT": a["L0_xattn_w_proj"].T, "b_proj": a["L0_xattn_b_proj"],
        "w_in": a["L0_ffn_Win"], "b_in": a["L0_ffn_bin_"], "w1": a["L0_ffn_W1"], "b1": a["L0_ffn_b1"],
        "w2": a["L0_ffn_W2"], "b2": a["L0_ffn_b2"], "w_out": a["L0_ffn_Wout"], "b_out": a["L0_ffn_bout"],
        "wq": a["L1_xattn_Wq"], "wkv": a["L1_xattn_Wkv"], "null_kv": a["L1_xattn_null_kv"], "wo": a["L1_xattn_Wout"],
        "ln_scale": a["L1_xattn_ln_scale"], "ln_bias": a["L1_xattn_ln_bias"],
        "w_router": a["L1_ffn_Wg"], "b_router": a["L1_ffn_bg"],
        "moe_w1": a["L1_ffn_W1"], "moe_w2": a["L1_ffn_W2"], "moe_w3": a["L1_ffn_W3"],
    }
    arrays = {f"in_{k}": np.ascontiguousarray(v) for k, v in arrays.items()}
    nc = bacc.Bacc("TRN2", target_bir_lowering=False, num_devices=1)
    dram = {k[3:]: nc.dram_tensor(k, v.shape, mybir.dt.from_np(v.dtype), kind="ExternalInput").ap()
            for k, v in arrays.items()}
    out = nc.dram_tensor("out_x", a["x"].shape, F32, kind="ExternalOutput").ap()
    flamingo(nc, dram, out)
    result = run_bass_kernel_spmd(nc, [arrays], core_ids=[0])
    return result.results[0]["out_x"]
```

```python
from contextlib import ExitStack

import concourse.bass as bass
from concourse import mybir

F32 = mybir.dt.float32
F32R = mybir.dt.float32r
U32 = mybir.dt.uint32
ALU = mybir.AluOpType
ACT = mybir.ActivationFunctionType
AX_X = mybir.AxisListType.X

P = 128
BANK = 512
LN_EPS = 1e-5
LN_OUT_EPS = 1e-6
RSQRT_MAGIC = 0x5F3759DF
ROW_PAD = 16


class Shapes:

    def __init__(self, x, ctx, w_win, w_router, moe_w1, null_kv, wq1):
        self.B, self.N, self.D = x.shape
        self.M, self.C = ctx.shape[1], ctx.shape[2]
        self.TT = self.N // P
        self.T = self.B * self.TT
        self.DC = self.D // P
        self.CC = self.C // P
        self.H = 16
        self.DH0 = self.D // self.H
        self.KT0 = (self.M + self.N) // P
        self.DH1 = null_kv.shape[1]
        self.I1 = wq1.shape[1]
        self.KT1 = self.M // P
        self.FM = w_win.shape[1]
        self.E = w_router.shape[1]
        self.F = moe_w1.shape[2]
        self.FT = self.F // P


class Norm:

    STEPS = 3

    def __init__(self, nc, tiles, stats, mv, work):
        self.nc, self.tiles, self.stats, self.mv, self.work = nc, tiles, stats, mv, work

    def statistics(self, dve, rows, eps):
        nc, n = self.nc, self.tiles
        for t in range(n):
            nc.vector.bn_stats(self.stats[:, t, :], rows(t))
        dve.drain()
        for t in range(n):
            nc.vector.bn_aggr(self.mv[:, t, :], self.stats[:, t, :])
        dve.drain()
        var, guess, half, tmp = (self.work[:, i, 0:n] for i in range(4))
        nc.vector.tensor_scalar(var, self.mv[:, 0:n, 1], 1.0, eps, ALU.mult, ALU.add)
        dve.drain()
        nc.vector.tensor_scalar(tmp.bitcast(U32), var.bitcast(U32), 1, None, ALU.logical_shift_right)
        nc.vector.tensor_scalar(half, var, -0.5, None, ALU.mult)
        dve.drain()
        nc.vector.tensor_scalar(guess.bitcast(U32), tmp.bitcast(U32), -1.0, float(RSQRT_MAGIC), ALU.mult, ALU.add)
        dve.drain()
        for _ in range(self.STEPS):
            nc.vector.tensor_tensor(tmp, guess, guess, ALU.mult)
            dve.drain()
            nc.vector.tensor_tensor(tmp, tmp, half, ALU.mult)
            dve.drain()
            nc.vector.scalar_tensor_tensor(out=guess, in0=tmp, scalar=1.5, in1=guess, op0=ALU.add, op1=ALU.mult)
            dve.drain()
        self.rstd = guess

    def apply(self, out, row, t):
        return self.nc.vector.tensor_scalar(out, row, self.mv[:, t, 0:1], self.work[:, 1, t:t + 1],
                                            ALU.subtract, ALU.mult)


def norm_rows(dve, norm, x, out, b, tiles, with_statistics=True):
    if with_statistics:
        norm.statistics(dve, lambda t: x[:, b * tiles + t, :], LN_EPS)
    for t in range(tiles):
        last = norm.apply(out[:, b * tiles + t, :], x[:, b * tiles + t, :], t)
    return last


def layer0(nc, s, g, bank, wide, dram):
    T, H, DH, N, D = s.TT, s.H, s.DH0, s.N, s.D
    ST = 64
    M_ROW = 2 * DH
    LAST = slice(M_ROW + 1, M_ROW + 1 + DH)
    SLOTS = 3
    PAIRS, QUADS = H // 2, H // 4
    KT = s.KT0
    SCALE = float(DH) ** -0.5
    PT_RING = 6

    with ExitStack() as ctx:
        def sb(name, shape, dt=F32):
            return ctx.enter_context(nc.sbuf_tensor("l0_" + name, shape, dt))

        def sem(name):
            return ctx.enter_context(nc.semaphore(name))

        w_qkv = sb("w_qkv", [P, s.DC, 3 * D])
        w_proj = sb("w_proj", [P, s.DC, D])
        b_proj = sb("b_proj", [P, D])
        w_in = sb("w_in", [P, s.DC, P])
        w_out = sb("w_out", [P, D])
        b_out = sb("b_out", [P, D])
        b_in = sb("b_in", [P, 1])
        w1 = sb("w1", [P, 8])
        b1 = sb("b1", [P, 8])
        w2 = sb("w2", [P, 8])
        b2 = sb("b2", [P, 1])
        ctx_sb = sb("ctx_sb", [P, T, 2 * D])
        xn = sb("xn", [P, T, D])
        xT = sb("xT", [P, s.DC, N])
        gates_raw = sb("gates_raw", [P, 4])
        ffn_xn = sb("ffn_xn", [P, T, D])
        ffn_xT = sb("ffn_xT", [P, s.DC, N])
        q_stack = sb("q_stack", [P, T, H, ST])
        k_stack = sb("k_stack", [P, 2, H, ST])
        kT = sb("kT", [P, PAIRS, KT * P], F32R)
        qT = sb("qT", [P, SLOTS, 4, N], F32R)
        max_cols = sb("max_cols", [P, T, P])
        v_ones = sb("v_ones", [P, KT, H, 2 * DH])
        probs = sb("probs", [P, PT_RING, 2, N])
        pv = sb("pv", [P, N])
        o_tok = sb("o_tok", [P, T, H, DH])
        recip = sb("recip", [P, T, 4])
        oT = sb("oT", [P, s.DC, N])
        tile_max = sb("tile_max", [P, T, H, 2])
        units = sb("units", [P, 2, N])
        gated = sb("gated", [P, N])
        s_in = sb("s_in", [P, N])
        x_bias = sb("x_bias", [P, T, D])
        stats = sb("stats", [P, T, 6])
        mv = sb("mv", [P, T, 2])
        work = sb("work", [P, 4, T])
        norm = Norm(nc, T, stats, mv, work)
        norm_ffn = Norm(nc, T, sb("ffn_stats", [P, T, 6]), sb("ffn_mv", [P, T, 2]), sb("ffn_work", [P, 4, T]))

        gates_loaded = sem("gates_loaded")
        gates_ready = sem("gates_ready")
        x_loaded = [sem(f"x_loaded_{b}") for b in range(s.B)]
        biases_loaded = sem("l0_biases_loaded")
        loaded = sem("l0_weights_loaded")
        ctx_ready = sem("l0_ctx_ready")
        xn_ready = sem("l0_xn_ready")
        xT_psum = sem("l0_xT_psum")
        xT_act = sem("l0_xT_act")
        xT_dve = sem("l0_xT_dve")
        qk_psum = sem("l0_qk_psum")
        v_psum = sem("l0_v_psum")
        v_copied = sem("l0_v_copied")
        q_split = sem("l0_q_split")
        split = sem("l0_split")
        dup = sem("l0_dup")
        tr_psum = sem("l0_tr_psum")
        tr_act = sem("l0_tr_act")

        max_psum = sem("l0_max_psum")
        max_read = sem("l0_max_read")
        negmax = sem("l0_negmax")
        negmaxT = sem("l0_negmaxT")
        rows_act = sem("l0_rows_act")
        rows_dve = sem("l0_rows_dve")
        q_psum = sem("l0_q_psum")
        q_ready = sem("l0_q_ready")
        s_psum = sem("l0_s_psum")
        exp_done = sem("l0_exp_done")
        pv_done = sem("l0_pv_done")
        pv_copied = sem("l0_pv_copied")
        o_psum = sem("l0_o_psum")
        o_ready = sem("l0_o_ready")

        bias_added = sem("l0_bias_added")
        oT_psum = sem("l0_oT_psum")
        oT_act = sem("l0_oT_act")
        oT_dve = sem("l0_oT_dve")
        proj_psum = sem("l0_proj_psum")
        resid = sem("l0_resid")
        xn2_ready = sem("l0_xn2_ready")
        xT2_psum = sem("l0_xT2_psum")
        xT2_act = sem("l0_xT2_act")
        xT2_dve = sem("l0_xT2_dve")
        sin_psum = sem("l0_sin_psum")
        sin_ready = sem("l0_sin_ready")
        unit_ready = sem("l0_unit_ready")
        unit_used = sem("l0_unit_used")
        ffn_psum = sem("l0_ffn_psum")

        NI = s.KT0
        NCTX = s.KT0 - T
        EARLY = 2

        def tokens(b):
            return g["x"][:, b * T:(b + 1) * T, :]

        def item_banks(i):
            return 4 if i < NCTX and i % 2 == 0 else 6

        def projected(t):
            return (bank(4), bank(5)) if t % 2 == 0 else (bank(2), bank(3))

        def split_parts(src, dst, low):
            src = src.rearrange("p (h d) -> p h d", h=H)
            nc.vector.tensor_copy(dst[:, :, 0:DH].bitcast(F32R), src)
            nc.vector.drain()
            return nc.vector.tensor_tensor(dst[:, :, low], src, dst[:, :, 0:DH], ALU.subtract)

        def split_keys(src, kt):
            return split_parts(src, k_stack[:, kt % 2], slice(DH, 2 * DH))

        def split_context(dve, b, t):
            if t >= 2:
                dve.wait_ge(tr_psum, b * NI + t - 1)
            split_keys(ctx_sb[:, t, 0:D], t).then_inc(split, 1)

        def norm_tokens(dve, b):
            dve.drain()
            norm.statistics(dve, lambda t: tokens(b)[:, t, :], LN_EPS)
            for t in range(T):
                norm.apply(xn[:, t, :], tokens(b)[:, t, :], t).then_inc(xn_ready, 1)

        def copy_high(pool, b, kt):
            pool.wait_ge(split, b * (NCTX + T) + kt + 1)
            k = k_stack[:, kt % 2]
            nc.gpsimd.tensor_copy(k[:, :, LAST], k[:, :, 0:DH]).then_inc(dup, 1)

        with nc.Block() as block:
            @block.sync
            def _(sp):
                def load_tokens(b):
                    sp.dma_start(tokens(b), dram["x"][b].rearrange("(t p) n -> p t n", p=P)).then_inc(x_loaded[b], 16)

                load_tokens(0)
                sp.dma_start(ctx_sb[:], dram["ctx"][0].rearrange("(t p) n -> p t n", p=P)).then_inc(ctx_ready, 16)
                for i in range(2):
                    for j, name in enumerate(("g_xattn", "g_ffn")):
                        sp.dma_start(gates_raw[:, 2 * i + j:2 * i + j + 1],
                                     dram[name][i:i + 1].partition_broadcast(P)).then_inc(gates_loaded, 16)
                sp.dma_start(b_proj[:], dram["b_proj"].partition_broadcast(P)).then_inc(biases_loaded, 16)
                sp.dma_start(b_out[:], dram["b_out"].partition_broadcast(P)).then_inc(biases_loaded, 16)
                sp.dma_start(w_qkv[:], dram["w_qkvT"].rearrange("(c p) n -> p c n", p=P)).then_inc(loaded, 16)
                sp.dma_start(w_proj[:], dram["w_projT"].rearrange("(c p) n -> p c n", p=P)).then_inc(loaded, 16)
                for half in range(2):
                    sp.dma_start(w_in[:, :, half * s.FM:(half + 1) * s.FM],
                                 dram["w_in"].rearrange("(c p) n -> p c n", p=P)).then_inc(loaded, 16)
                    rows = slice(half * s.FM, (half + 1) * s.FM)
                    sp.dma_start(w_out[rows, :], dram["w_out"]).then_inc(loaded, 16)
                    sp.dma_start(b_in[rows, :], dram["b_in"].unsqueeze(1)).then_inc(loaded, 16)
                    for dst, src in ((w1, "w1"), (b1, "b1"), (w2, "w2")):
                        sp.dma_start(dst[rows, :], dram[src][:, 8 * half:8 * half + 8]).then_inc(loaded, 16)
                sp.dma_start(b2[0:s.FM, :], dram["b2"].unsqueeze(1)).then_inc(loaded, 16)
                for b in range(1, s.B):
                    load_tokens(b)
                sp.wait_ge(loaded, 16 * 15)
                for b in range(1, s.B):
                    sp.wait_ge(x_loaded[b], 16)

            @block.scalar
            def _(act):
                act.wait_ge(gates_loaded, 64)
                nc.scalar.activation(g["gates"][:], gates_raw[:], ACT.Tanh).then_inc(gates_ready, 1)

            @block.vector
            def _(dve):
                nc.vector.memset(k_stack[:], 0.0)
                dve.drain()
                nc.vector.memset(k_stack[:, :, :, M_ROW:M_ROW + 1], 1.0)
                dve.wait_ge(x_loaded[0], 16)
                norm_tokens(dve, 0)
                dve.wait_ge(ctx_ready, 16)
                for t in range(EARLY):
                    split_context(dve, 0, t)
                nc.vector.memset(q_stack[:], 0.0)
                dve.wait_ge(gates_ready, 1)
                dve.wait_ge(biases_loaded, 32)
                nc.vector.tensor_scalar(b_proj[:], b_proj[:], g["gates"][:, 0:1], None, ALU.mult)
                nc.vector.tensor_scalar(b_out[:], b_out[:], g["gates"][:, 1:2], None, ALU.mult)

            @block.gpsimd
            def _(pool):
                nc.gpsimd.memset(g["ident"][:], 0.0)
                nc.gpsimd.memset(v_ones[:], 1.0)
                nc.gpsimd.memset(qT[:].bitcast(F32), 0.0)
                nc.gpsimd.memset(max_cols[:], 0.0)
                pool.drain()
                nc.gpsimd.memset(b2[s.FM:P, :], 0.0)
                pool.drain()
                nc.gpsimd.affine_select(out=g["ident"][:], in_=g["ident"][:], compare_op=ALU.not_equal, fill=1.0,
                                        base=0, pattern=[[-1, P]], channel_multiplier=1)
                for t in range(EARLY):
                    copy_high(pool, 0, t)

        for b in range(s.B + 1):
            before, now = b >= 1, b < s.B

            with nc.Block() as block:
                @block.tensor
                def _(pe):
                    def transpose_keys(i):
                        if i >= 2:
                            pe.wait_ge(tr_act, b * NI + (i - 1 if i < NCTX else i))
                        pe.wait_ge(dup, b * (NCTX + T) + i + 1)
                        src = k_stack[:, i % 2].rearrange("p h r -> p (h r)")
                        for p in range(PAIRS):
                            dst = bank(item_banks(i) + p // 4)[:, (p % 4) * P:(p % 4 + 1) * P]
                            last = nc.tensor.transpose(dst, src[:, p * P:(p + 1) * P], g["ident"][:])
                        last.then_inc(tr_psum, 1)

                    def project(t):
                        if t >= 2:
                            pe.wait_ge(q_split, b * T + t - 1)
                            pe.wait_ge(v_copied, b * T + t - 1)
                        elif t == 1 and before:
                            pe.wait_ge(sin_ready, b)
                        qk, v = projected(t)
                        for c in range(s.DC):
                            last = nc.tensor.matmul(qk[:, 0:2 * D], xT[:, c, t * P:(t + 1) * P], w_qkv[:, c, 0:2 * D],
                                                    start=(c == 0), stop=(c == s.DC - 1))
                        last.then_inc(qk_psum, 1)
                        for c in range(s.DC):
                            last = nc.tensor.matmul(v[:, 0:D], xT[:, c, t * P:(t + 1) * P], w_qkv[:, c, 2 * D:3 * D],
                                                    start=(c == 0), stop=(c == s.DC - 1))
                        last.then_inc(v_psum, 1)

                    def result(t):
                        return bank(t // 2)[:, t % 2 * D:(t % 2 + 1) * D]

                    if before:
                        for c in range(s.DC):
                            for t in range(T):
                                src = o_tok[:, t].rearrange("p h d -> p (h d)")
                                last = nc.tensor.transpose(bank(2 + c)[:, t * P:(t + 1) * P], src[:, c * P:(c + 1) * P],
                                                           g["ident"][:])
                            last.then_inc(oT_psum, 1)
                    if now:
                        transpose_keys(0)
                        transpose_keys(1)
                    if before:
                        pe.wait_ge(oT_act, b)
                        pe.wait_ge(oT_dve, b)
                        for t in range(T):
                            for c in range(s.DC):
                                last = nc.tensor.matmul(result(t), oT[:, c, t * P:(t + 1) * P], w_proj[:, c, :],
                                                        start=(c == 0), stop=(c == s.DC - 1))
                            last.then_inc(proj_psum, 1)
                    if now:
                        transpose_keys(2)
                    if before:
                        pe.wait_ge(xn2_ready, b * T)
                        for c in range(s.DC):
                            for t in range(T):
                                last = nc.tensor.transpose(bank(2 + c)[:, t * P:(t + 1) * P],
                                                           ffn_xn[:, t, c * P:(c + 1) * P], g["ident"][:])
                            last.then_inc(xT2_psum, 1)
                        pe.wait_ge(xT2_act, b)
                        pe.wait_ge(xT2_dve, b)
                        for c in range(s.DC):
                            last = nc.tensor.matmul(bank(2), w_in[:, c, :], ffn_xT[:, c, :], start=(c == 0),
                                                    stop=(c == s.DC - 1))
                        last.then_inc(sin_psum, 1)
                    if now:
                        transpose_keys(3)
                        pe.wait_ge(xn_ready, (b + 1) * T)
                        pe.wait_ge(tr_act, b * NI + NCTX - 1)
                        for c in range(s.DC):
                            for t in range(T):
                                last = nc.tensor.transpose(bank(4 + c)[:, t * P:(t + 1) * P],
                                                           xn[:, t, c * P:(c + 1) * P], g["ident"][:])
                            last.then_inc(xT_psum, 1)
                        pe.wait_ge(xT_act, b + 1)
                        pe.wait_ge(xT_dve, b + 1)
                        project(0)
                        project(1)
                    if before:
                        pe.wait_ge(unit_used, b * 8)
                        for t in range(T):
                            nc.tensor.matmul(result(t), gated[:, t * P:(t + 1) * P], w_out[:],
                                             start=True, stop=True).then_inc(ffn_psum, 1)
                    if now:
                        for t in range(T):
                            transpose_keys(NCTX + t)
                            if t + 2 < T:
                                project(t + 2)

                @block.scalar
                def _(act):
                    def keep_keys(i):
                        act.wait_ge(tr_psum, b * NI + i + 1)
                        nc.scalar.activation(kT[:, :, i * P:(i + 1) * P],
                                             wide(item_banks(i)).rearrange("p (a n) -> p a n", a=PAIRS),
                                             ACT.Copy).then_inc(tr_act, 1)

                    if before:
                        act.wait_ge(oT_psum, 2 * b - 1)
                        nc.scalar.activation(oT[:, 0, :], bank(2), ACT.Copy).then_inc(oT_act, 1)
                    if now:
                        for i in range(NCTX - 1):
                            keep_keys(i)
                    if before:
                        act.wait_ge(xT2_psum, 2 * b - 1)
                        nc.scalar.activation(ffn_xT[:, 0, :], bank(2), ACT.Copy).then_inc(xT2_act, 1)
                    if now:
                        keep_keys(NCTX - 1)
                        act.wait_ge(xT_psum, 2 * b + 1)
                        nc.scalar.activation(xT[:, 0, :], bank(4), ACT.Copy).then_inc(xT_act, 1)
                    if before:
                        act.wait_ge(sin_ready, b)
                        for i in range(8):
                            if i >= 2:
                                act.wait_ge(unit_used, 8 * (b - 1) + i - 1)
                            nc.scalar.activation(units[:, i % 2, :], s_in[:], ACT.Relu, bias=b1[:, i:i + 1],
                                                 scale=w1[:, i:i + 1]).then_inc(unit_ready, 1)
                    if now:
                        for t in range(T):
                            act.wait_ge(v_psum, b * T + t + 1)
                            nc.scalar.activation(v_ones[:, NCTX + t, :, 0:DH],
                                                 projected(t)[1][:, 0:D].rearrange("p (h d) -> p h d", h=H),
                                                 ACT.Copy).then_inc(v_copied, 1)
                            keep_keys(NCTX + t)

                @block.gpsimd
                def _(pool):
                    def keep_values(t):
                        nc.gpsimd.tensor_copy(v_ones[:, t, :, 0:DH], ctx_sb[:, t, D:2 * D].rearrange("p (h d) -> p h d", h=H))

                    def add_bias(bias):
                        for t in range(T):
                            nc.gpsimd.tensor_tensor(x_bias[:, t, :], tokens(b - 1)[:, t, :], bias[:],
                                                    ALU.add).then_inc(bias_added, 1)

                    if before:
                        add_bias(b_proj)
                    if now:
                        copy_high(pool, b, 2)
                        for t in range(NCTX):
                            keep_values(t)
                    if before:
                        pool.wait_ge(resid, b * T)
                        add_bias(b_out)
                    if now:
                        copy_high(pool, b, 3)
                        for t in range(T):
                            kt = NCTX + t
                            copy_high(pool, b, kt)
                            pool.wait_ge(q_split, b * T + t + 1)
                            nc.gpsimd.tensor_copy(q_stack[:, t, :, DH:2 * DH], q_stack[:, t, :, 0:DH])

                @block.vector
                def _(dve):
                    def result(t):
                        return bank(t // 2)[:, t % 2 * D:(t % 2 + 1) * D]

                    def add_result(ready, t, gate):
                        dve.wait_ge(ready, (b - 1) * T + (t // 2 + 1) * 2)
                        x_t = tokens(b - 1)[:, t, :]
                        return nc.vector.scalar_tensor_tensor(out=x_t, in0=result(t), scalar=gate, in1=x_bias[:, t, :],
                                                              op0=ALU.mult, op1=ALU.add)

                    def split_projected(t):
                        dve.wait_ge(qk_psum, b * T + t + 1)
                        dve.wait_ge(tr_psum, b * NI + NCTX + t - 1)
                        qk = projected(t)[0]
                        split_keys(qk[:, D:2 * D], NCTX + t).then_inc(split, 1)
                        split_parts(qk[:, 0:D], q_stack[:, t], LAST).then_inc(q_split, 1)

                    if before:
                        dve.wait_ge(oT_psum, 2 * b)
                        nc.vector.tensor_copy(oT[:, 1, :], bank(3)).then_inc(oT_dve, 1)
                    if now:
                        split_context(dve, b, 2)
                    if before:
                        for t in range(T):
                            dve.wait_ge(bias_added, 2 * (b - 1) * T + t + 1)
                            add_result(proj_psum, t, g["gates"][:, 0:1]).then_inc(resid, 1)
                        dve.drain()
                        norm_ffn.statistics(dve, lambda t: tokens(b - 1)[:, t, :], LN_EPS)
                        for t in range(T):
                            norm_ffn.apply(ffn_xn[:, t, :], tokens(b - 1)[:, t, :], t).then_inc(xn2_ready, 1)
                        dve.wait_ge(xT2_psum, 2 * b)
                        nc.vector.tensor_copy(ffn_xT[:, 1, :], bank(3)).then_inc(xT2_dve, 1)
                    if now:
                        split_context(dve, b, 3)
                    if before:
                        dve.wait_ge(sin_psum, b)
                        nc.vector.tensor_scalar(s_in[:], bank(2), b_in[:, 0:1], None, ALU.add).then_inc(sin_ready, 1)
                    if now:
                        dve.wait_ge(xT_psum, 2 * b + 2)
                        nc.vector.tensor_copy(xT[:, 1, :], bank(5)).then_inc(xT_dve, 1)
                    if before:
                        for i in range(8):
                            dve.wait_ge(unit_ready, 8 * (b - 1) + i + 1)
                            if i == 0:
                                nc.vector.tensor_scalar(gated[:], units[:, 0, :], w2[:, 0:1], b2[:, 0:1], ALU.mult,
                                                        ALU.add).then_inc(unit_used, 1)
                            else:
                                dve.drain()
                                nc.vector.scalar_tensor_tensor(out=gated[:], in0=units[:, i % 2, :], scalar=w2[:, i:i + 1],
                                                               in1=gated[:], op0=ALU.mult, op1=ALU.add).then_inc(unit_used, 1)
                    if now:
                        split_projected(0)
                    if before:
                        dve.wait_ge(bias_added, 2 * b * T)
                        for t in range(T):
                            add_result(ffn_psum, t, g["gates"][:, 1:2])
                    if now:
                        for t in range(1, T):
                            split_projected(t)

            if not now:
                break

            UNITS = QUADS * KT * 2
            MAXES = H * T * 2
            FIRST_BANKS = (4, 5, 0, 1, 2, 3)

            def max_bank(n):
                return FIRST_BANKS[n % len(FIRST_BANKS)] if n < 8 * T else 4 + n % 2

            COVER = 1
            STACK_AT = (3, 5)
            with nc.Block() as block:
                @block.tensor
                def _(pe):
                    def stack_queries(quad, c):
                        p = 2 * quad + c
                        if p >= 1:
                            pe.wait_ge(q_ready, b * PAIRS + p)
                        for t in range(T):
                            src = q_stack[:, t].rearrange("p h r -> p (h r)")
                            last = nc.tensor.transpose(bank(7)[:, t * P:(t + 1) * P],
                                                       src[:, p * P:(p + 1) * P], g["ident"][:])
                        last.then_inc(q_psum, 1)

                    def transpose_max(quad):
                        pe.wait_ge(negmax, b * QUADS + quad + 1)
                        pe.wait_ge(q_ready, b * PAIRS + min(2 * quad + 4, PAIRS))
                        if quad >= 2:
                            pe.wait_ge(o_ready, b * QUADS + quad - 1)
                        for t in range(T):
                            last = nc.tensor.transpose(bank(7)[:, t * P:(t + 1) * P], max_cols[:, t, :], g["ident"][:])
                        last.then_inc(negmaxT, 1)

                    def max_scores(n):
                        h, r = divmod(n, 2 * T)
                        t, half = divmod(r, 2)
                        ring = len(FIRST_BANKS) if n < 8 * T else 2
                        if n >= 8 * T + 2 or ring <= n < 8 * T:
                            pe.wait_ge(max_read, b * MAXES + n - ring + 1)
                        nc.tensor.matmul(bank(max_bank(n)), qT[:, (h // 4) % SLOTS, h % 4, t * P:(t + 1) * P],
                                         kT[:, h // 2, half * BANK:(half + 1) * BANK],
                                         start=True, stop=True).then_inc(max_psum, 1)

                    def scores(n):
                        quad, r = divmod(n, 2 * KT)
                        kt, c = divmod(r, 2)
                        if n >= 2:
                            pe.wait_ge(exp_done, b * UNITS + n - 1)
                        for i in range(2):
                            last = nc.tensor.matmul(bank(2 * (n % 2) + i),
                                                    kT[:, 2 * quad + c, kt * P:(kt + 1) * P],
                                                    qT[:, quad % SLOTS, 2 * c + i, :], start=True, stop=True)
                        last.then_inc(s_psum, 1)

                    def weigh_values(quad, kt):
                        n = 2 * (quad * KT + kt)
                        pe.wait_ge(exp_done, b * UNITS + n + 2)
                        if kt == 0 and quad >= 1:
                            pe.wait_ge(pv_copied, b * QUADS + quad)
                        for j in range(4):
                            last = nc.tensor.matmul(bank(6)[32 * j:32 * j + 32, :], v_ones[:, kt, 4 * quad + j, :],
                                                    probs[:, (n + j // 2) % PT_RING, j % 2, :],
                                                    start=(kt == 0), stop=(kt == KT - 1), tile_position=(0, 32 * j),
                                                    skip_group_check=True)
                        last.then_inc(pv_done, 1)

                    def tokens_first(quad):
                        pe.wait_ge(pv_copied, b * QUADS + quad + 1)
                        if quad == QUADS - 1:
                            pe.wait_ge(o_ready, b * QUADS + quad)
                        for t in range(T):
                            last = nc.tensor.transpose(bank(7)[:, t * P:(t + 1) * P], pv[:, t * P:(t + 1) * P], g["ident"][:])
                        last.then_inc(o_psum, 1)

                    for c in range(2):
                        stack_queries(0, c)
                    for n in range(8 * T):
                        if n % (4 * T) == 0:
                            pe.wait_ge(q_ready, b * PAIRS + n // (4 * T) + 1)
                        max_scores(n)
                        if n in (T, 2 * T):
                            stack_queries(1, n // T - 1)
                    transpose_max(0)
                    for m in range(COVER):
                        max_scores(8 * T + m)
                    for quad in range(QUADS):
                        pe.wait_ge(rows_act, b * QUADS + quad + 1)
                        pe.wait_ge(rows_dve, b * QUADS + quad + 1)
                        for kt in range(KT):
                            first = 4 * kt + COVER
                            later = iter(range(first, min(first + 4, 8 * T)) if quad + 1 < QUADS else ())
                            for c in range(2):
                                scores(2 * KT * quad + 2 * kt + c)
                                for m in later:
                                    max_scores(8 * T * (quad + 1) + m)
                                    break
                            if kt >= 1:
                                weigh_values(quad, kt - 1)
                            for m in later:
                                max_scores(8 * T * (quad + 1) + m)
                            if kt == 1 and quad >= 1:
                                tokens_first(quad - 1)
                            if kt in STACK_AT and quad + 2 < QUADS:
                                if quad >= 1:
                                    pe.wait_ge(o_ready, b * QUADS + quad)
                                stack_queries(quad + 2, STACK_AT.index(kt))
                        weigh_values(quad, KT - 1)
                        if quad + 1 < QUADS:
                            transpose_max(quad + 1)
                        if quad + 2 < QUADS:
                            for m in range(COVER):
                                max_scores(8 * T * (quad + 2) + m)
                    tokens_first(QUADS - 1)

                @block.scalar
                def _(act):
                    def place_queries(quad, c):
                        act.wait_ge(q_psum, b * PAIRS + 2 * quad + c + 1)
                        for i in range(2):
                            rows = slice(i * ST, (i + 1) * ST)
                            last = nc.scalar.activation(qT[rows, quad % SLOTS, 2 * c + i, :], bank(7)[rows, :], ACT.Copy)
                        last.then_inc(q_ready, 1)

                    def place_max(quad):
                        act.wait_ge(negmaxT, b * QUADS + quad + 1)
                        for i in range(2):
                            row = i * ST + M_ROW
                            last = nc.scalar.activation(qT[row:row + 1, quad % SLOTS, i, :], bank(7)[32 * i:32 * i + 1, :],
                                                        ACT.Copy)
                        last.then_inc(rows_act, 1)

                    def copy_values(quad):
                        act.wait_ge(pv_done, b * QUADS * KT + (quad + 1) * KT)
                        if quad >= 1:
                            act.wait_ge(o_psum, b * QUADS + quad)
                        nc.scalar.activation(pv[:], bank(6), ACT.Copy).then_inc(pv_copied, 1)

                    for c in range(4):
                        place_queries(c // 2, c % 2)
                    place_max(0)
                    for quad in range(QUADS):
                        for u in range(2 * KT):
                            n = 2 * KT * quad + u
                            act.wait_ge(s_psum, b * UNITS + n + 1)
                            if n >= PT_RING:
                                act.wait_ge(pv_done, b * QUADS * KT + (n - PT_RING) // 2 + 1)
                            nc.scalar.activation(probs[:, n % PT_RING], wide(2 * (n % 2)), ACT.Exp,
                                                 scale=SCALE).then_inc(exp_done, 1)
                            if u % 2 and u // 2 in STACK_AT and quad + 2 < QUADS:
                                place_queries(quad + 2, STACK_AT.index(u // 2))
                        if quad + 1 < QUADS:
                            place_max(quad + 1)
                        copy_values(quad)

                @block.vector
                def _(dve):
                    def normalize(quad):
                        dve.wait_ge(o_psum, b * QUADS + quad + 1)
                        o = bank(7).rearrange("p (t j d) -> p t j d", t=T, j=4)
                        nc.vector.reciprocal(recip[:], o[:, :, :, DH])
                        dve.drain()
                        for t in range(T):
                            last = nc.vector.tensor_tensor(o_tok[:, t, 4 * quad:4 * quad + 4, :], o[:, t, :, 0:DH],
                                                           recip[:, t, :].unsqueeze(2).to_broadcast([P, 4, DH]), ALU.mult)
                        last.then_inc(o_ready, 1)

                    for quad in range(QUADS):
                        for n in range(8 * T * quad, 8 * T * (quad + 1)):
                            h, r = divmod(n, 2 * T)
                            t, half = divmod(r, 2)
                            dve.wait_ge(max_psum, b * MAXES + n + 1)
                            nc.vector.reduce_max(tile_max[:, t, h, half:half + 1], bank(max_bank(n)), AX_X).then_inc(max_read, 1)
                            if quad >= 2 and n == 8 * T * quad + 4 * T:
                                normalize(quad - 2)
                        dve.drain()
                        nc.vector.tensor_reduce(out=max_cols[:, :, 0:P:32].bitcast(F32R),
                                                in_=tile_max[:, :, 4 * quad:4 * quad + 4, :], axis=AX_X, op=ALU.max,
                                                negate=True).then_inc(negmax, 1)
                        dve.wait_ge(negmaxT, b * QUADS + quad + 1)
                        for i in range(2):
                            row = i * ST + M_ROW
                            last = nc.vector.tensor_copy(qT[row:row + 1, quad % SLOTS, 2 + i, :],
                                                         bank(7)[64 + 32 * i:64 + 32 * i + 1, :])
                        last.then_inc(rows_dve, 1)
                    if b + 1 < s.B:
                        norm_tokens(dve, b + 1)
                    normalize(QUADS - 2)
                    if b + 1 < s.B:
                        dve.wait_ge(ctx_ready, 16 * (b + 2))
                        for t in range(EARLY):
                            split_context(dve, b + 1, t)
                    normalize(QUADS - 1)

                if b + 1 < s.B:
                    @block.sync
                    def _(sp):
                        sp.dma_start(ctx_sb[:], dram["ctx"][b + 1].rearrange("(t p) n -> p t n", p=P)).then_inc(ctx_ready, 16)

                    @block.gpsimd
                    def _(pool):
                        for t in range(EARLY):
                            copy_high(pool, b + 1, t)


def layer1(nc, s, g, bank, dram):
    T, H, DH, N, D = s.TT, s.H, s.DH1, s.N, s.D
    PAIRS = H // 2
    KT = s.KT1
    SCALE = float(DH) ** -0.5
    RING = 8
    UNITS = 2 * KT
    NULL_COL = DH // 2

    ident, x_resid, gates, routed = g["ident"], g["x"], g["gates"], g["routed"][:, :, 0:s.D]

    with ExitStack() as ctx:
        def sb(name, shape, dt=F32):
            return ctx.enter_context(nc.sbuf_tensor("l1_" + name, shape, dt))

        def sem(name):
            return ctx.enter_context(nc.semaphore(name))

        wq = sb("wq", [P, s.DC, s.I1])
        wk = sb("wk", [P, s.CC, s.I1])
        wv = sb("wv", [P, s.CC, s.I1])
        wo = sb("wo", [P, PAIRS, D])
        null_k = sb("null_k", [P, DH])
        null_v = sb("null_v", [1, DH])
        w_null = sb("w_null", [P, s.DC, H])
        ln_scale = sb("ln_scale", [P, D])
        ln_bias = sb("ln_bias", [P, D])
        ctxT = sb("ctxT", [P, s.CC, s.M])
        xn = sb("xn", [P, T, D])
        xT = sb("xT", [P, s.DC, N])
        v_sb = sb("v_sb", [P, KT, s.I1])
        s_null = sb("s_null", [P, T, H])
        q1 = sb("q1", [P, 2, 2, N], F32R)
        q2 = sb("q2", [P, 2, 2, N], F32R)
        k1 = sb("k1", [P, 2, 2, s.M], F32R)
        k2 = sb("k2", [P, 2, 2, s.M], F32R)
        probs = sb("probs", [P, RING, N])
        null_p = sb("null_p", [1, 2, N])
        p_sum = sb("p_sum", [P, 2, N])
        ones = sb("ones", [P, DH])
        denom = sb("denom", [P, N])
        oT = sb("oT", [P, PAIRS, N])
        tile_max = sb("tile_max", [P, 2, T])
        max_tmp = sb("max_tmp", [P, 2, T])
        max_cols = sb("max_cols", [P, T, P])
        x_bias = sb("x_bias", [P, T, D])
        out_n = sb("out_n", [P, T, D])
        w_null_tmp = out_n[:].rearrange("p t (a k) -> p (t a) k", k=DH)
        stats = sb("stats", [P, T, 6])
        mv = sb("mv", [P, T, 2])
        work = sb("work", [P, 4, T])
        norm = Norm(nc, T, stats, mv, work)
        norm_out = Norm(nc, T, sb("out_stats", [P, T, 6]), sb("out_mv", [P, T, 2]), sb("out_work", [P, 4, T]))

        small_loaded = sem("l1_small_loaded")
        wv_loaded = [sem(f"l1_wv_loaded_{half}") for half in range(2)]
        wqk_loaded = sem("l1_wqk_loaded")
        wo_loaded = sem("l1_wo_loaded")
        filled = sem("l1_constants_filled")
        null_exp = sem("l1_null_exp")
        null_added = sem("l1_null_added")
        w_null_ready = sem("l1_w_null_ready")
        biases_ready = sem("l1_biases_ready")
        ctx_ready = sem("l1_ctx_ready")
        xn_ready = sem("l1_xn_ready")
        xT_psum = sem("l1_xT_psum")
        xT_act = sem("l1_xT_act")
        xT_dve = sem("l1_xT_dve")
        v_psum = sem("l1_v_psum")
        v_act = sem("l1_v_act")
        v_dve = sem("l1_v_dve")
        null_psum = sem("l1_null_psum")

        qk_psum = sem("l1_qk_psum")
        hi_done = sem("l1_hi_done")
        lo_done = sem("l1_lo_done")
        max_psum = sem("l1_max_psum")
        max_read = sem("l1_max_read")
        negmax = sem("l1_negmax")
        negmaxT = sem("l1_negmaxT")
        max_rows = sem("l1_max_rows")
        s_psum = sem("l1_s_psum")
        exp_done = sem("l1_exp_done")
        pv_done = sem("l1_pv_done")
        summed = sem("l1_summed")
        sums_psum = sem("l1_sums_psum")
        sums_read = sem("l1_sums_read")
        norm_done = sem("l1_norm_done")

        out_psum = sem("l1_out_psum")
        out_normed = sem("l1_out_normed")
        scaled = sem("l1_scaled")

        def tokens(b):
            return x_resid[:, b * T:(b + 1) * T, :]

        with nc.Block() as block:
            @block.sync
            def _(sp):
                sp.dma_start(ctxT[:], dram["ctxT"][0].rearrange("(c p) n -> p c n", p=P)).then_inc(ctx_ready, 16)
                for half in range(2):
                    sp.dma_start(wv[:, :, half * BANK:(half + 1) * BANK],
                                 dram["wkv"][:, s.I1 + half * BANK:s.I1 + (half + 1) * BANK]
                                 .rearrange("(c p) n -> p c n", p=P)).then_inc(wv_loaded[half], 16)
                sp.dma_start(wq[:], dram["wq"].rearrange("(c p) n -> p c n", p=P)).then_inc(wqk_loaded, 16)
                sp.dma_start(wk[:], dram["wkv"][:, 0:s.I1].rearrange("(c p) n -> p c n", p=P)).then_inc(wqk_loaded, 16)
                sp.dma_start(null_k[:], dram["null_kv"][0].partition_broadcast(P)).then_inc(small_loaded, 16)
                sp.dma_start(null_v[:], dram["null_kv"][1:2, :]).then_inc(small_loaded, 16)
                sp.dma_start(ln_scale[:], dram["ln_scale"].partition_broadcast(P)).then_inc(small_loaded, 16)
                sp.dma_start(ln_bias[:], dram["ln_bias"].partition_broadcast(P)).then_inc(small_loaded, 16)
                sp.dma_start(wo[:], dram["wo"].rearrange("(c p) n -> p c n", p=P)).then_inc(wo_loaded, 16)
                for b in range(1, s.B):
                    sp.wait_ge(qk_psum, b * PAIRS)
                    sp.dma_start(ctxT[:], dram["ctxT"][b].rearrange("(c p) n -> p c n", p=P)).then_inc(ctx_ready, 16)

            @block.tensor
            def _(pe):
                def project(g, i):
                    p = g % PAIRS
                    if i == 0 and g >= 1:
                        pe.wait_ge(lo_done, g)
                    if i < s.DC:
                        nc.tensor.matmul(bank(6), wq[:, i, p * P:(p + 1) * P], xT[:, i, :],
                                         start=(i == 0), stop=(i == s.DC - 1))
                    else:
                        c = i - s.DC
                        last = nc.tensor.matmul(bank(7), wk[:, c, p * P:(p + 1) * P], ctxT[:, c, :],
                                                start=(c == 0), stop=(c == s.CC - 1))
                        if c == s.CC - 1:
                            last.then_inc(qk_psum, 1)

                def max_scores(g, i):
                    j, t = divmod(i, T)
                    if i == 0:
                        pe.wait_ge(lo_done, g + 1)
                        if g >= 1:
                            pe.wait_ge(null_exp, g)
                    elif i == 1:
                        if g >= 2:
                            pe.wait_ge(sums_read, g - 1)
                    else:
                        pe.wait_ge(max_read, g * 2 * T + i - 1)
                    out = bank(2 + i % 2)
                    nc.tensor.matmul(out, q1[:, g % 2, j, t * P:(t + 1) * P], k1[:, g % 2, j, :],
                                     start=True, stop=False)
                    nc.tensor.matmul(out, q2[0:DH, g % 2, j, t * P:(t + 1) * P], k2[0:DH, g % 2, j, :],
                                     start=False, stop=True).then_inc(max_psum, 1)

                def transpose_max(g):
                    pe.wait_ge(negmax, g + 1)
                    for t in range(T):
                        last = nc.tensor.transpose(bank(2)[:, t * P:(t + 1) * P], max_cols[:, t, :], ident[:])
                    last.then_inc(negmaxT, 1)

                def scores(g, u):
                    kt, j = divmod(u, 2)
                    n = g * UNITS + u
                    if n >= 2:
                        pe.wait_ge(exp_done, n - 1)
                    if u == 0:
                        pe.wait_ge(max_rows, g + 1)
                    first, second = k1[:, g % 2, j, kt * P:(kt + 1) * P], k2[0:DH + 1, g % 2, j, kt * P:(kt + 1) * P]
                    nc.tensor.matmul(bank(n % 2), first, q1[:, g % 2, j, :], start=True, stop=False)
                    nc.tensor.matmul(bank(n % 2), second, q2[0:DH + 1, g % 2, j, :],
                                     start=False, stop=True).then_inc(s_psum, 1)

                def weigh_null(g):
                    pe.wait_ge(null_exp, g + 1)
                    for j in range(2):
                        last = nc.tensor.matmul(bank(4 + g % 2)[j * DH:(j + 1) * DH, :], null_v[:], null_p[:, j, :], start=False,
                                                stop=False, tile_position=(0, j * DH), skip_group_check=True)
                    last.then_inc(pv_done, 1)

                def weigh_values(g, kt):
                    pe.wait_ge(exp_done, g * UNITS + 2 * kt + 2)
                    if kt == 0 and g >= 2:
                        pe.wait_ge(norm_done, g - 1)
                    for j in range(2):
                        h = 2 * (g % PAIRS) + j
                        last = nc.tensor.matmul(bank(4 + g % 2)[j * DH:(j + 1) * DH, :], v_sb[:, kt, h * DH:(h + 1) * DH],
                                                probs[:, (g * UNITS + 2 * kt + j) % RING, :], start=(kt == 0),
                                                stop=(kt == KT - 1), tile_position=(0, j * DH), skip_group_check=True)
                    last.then_inc(pv_done, 1)

                def sums(g):
                    pe.wait_ge(summed, g + 1)
                    if g % PAIRS == PAIRS - 1:
                        pe.wait_ge(sums_read, g)
                    else:
                        pe.wait_ge(max_read, (g + 2) * 2 * T)
                    for j in range(2):
                        last = nc.tensor.matmul(bank(3)[j * DH:(j + 1) * DH, :], ones[:], p_sum[:, j, :], start=True,
                                                stop=True, tile_position=(0, j * DH), skip_group_check=True)
                    last.then_inc(sums_psum, 1)

                def maxima_and_project(g, with_next):
                    products = iter(range(s.DC + s.CC) if with_next else ())
                    for i in range(2 * T):
                        max_scores(g, i)
                        if i % 2 == 0 and i < 2 * T - 2:
                            for c in products:
                                project(g + 1, c)
                                break
                    for c in products:
                        project(g + 1, c)
                        if c == s.DC + s.CC - 2:
                            break
                    transpose_max(g)
                    for c in products:
                        project(g + 1, c)

                def values(b, n):
                    kt, half = divmod(n, 2)
                    if n == 0:
                        pe.wait_ge(ctx_ready, 16 * (b + 1))
                    if b == 0 and n < 2:
                        pe.wait_ge(wv_loaded[n], 16)
                    if n < 2:
                        if b >= 1:
                            pe.wait_ge(exp_done, b * PAIRS * UNITS)
                    else:
                        pe.wait_ge(v_act if n % 2 else v_dve, b * KT + n // 2)
                    for c in range(s.CC):
                        last = nc.tensor.matmul(bank(n % 2), ctxT[:, c, kt * P:(kt + 1) * P],
                                                wv[:, c, half * BANK:(half + 1) * BANK],
                                                start=(c == 0), stop=(c == s.CC - 1))
                    last.then_inc(v_psum, 1)

                def transpose_tokens(b):
                    pe.wait_ge(xn_ready, (b + 1) * T)
                    if b >= 1:
                        pe.wait_ge(lo_done, b * PAIRS)
                    for c in range(s.DC):
                        for t in range(T):
                            last = nc.tensor.transpose(bank(6 + c)[:, t * P:(t + 1) * P],
                                                       xn[:, t, c * P:(c + 1) * P], ident[:])
                        last.then_inc(xT_psum, 1)

                def project_output(b):
                    if b == 0:
                        pe.wait_ge(wo_loaded, 16)
                    pe.wait_ge(norm_done, (b + 1) * PAIRS)
                    for t in range(T):
                        for p in range(PAIRS):
                            last = nc.tensor.matmul(bank(2 + t)[:, 0:D], oT[:, p, t * P:(t + 1) * P], wo[:, p, :],
                                                    start=(p == 0), stop=(p == PAIRS - 1))
                        last.then_inc(out_psum, 1)

                def null_scores():
                    for t in range(T):
                        for c in range(s.DC):
                            last = nc.tensor.matmul(bank(4)[:, t * H:(t + 1) * H], xT[:, c, t * P:(t + 1) * P],
                                                    w_null[:, c, :], start=(c == 0), stop=(c == s.DC - 1))
                    last.then_inc(null_psum, 1)

                for b in range(s.B + 1):
                    if b < s.B:
                        transpose_tokens(b)
                        early_values = 2
                        for n in range(early_values):
                            values(b, n)
                    if b >= 1:
                        sums(b * PAIRS - 1)
                    if b < s.B:
                        pe.wait_ge(xT_act, b + 1)
                        pe.wait_ge(xT_dve, b + 1)
                        if b == 0:
                            pe.wait_ge(wqk_loaded, 32)
                        for c in range(s.DC + s.CC):
                            project(b * PAIRS, c)
                    if b >= 1:
                        project_output(b - 1)
                    if b == s.B:
                        break
                    for n in range(early_values, 2 * KT):
                        values(b, n)
                    if b >= 1:
                        pe.wait_ge(out_normed, b * T)
                    else:
                        pe.wait_ge(w_null_ready, 1)
                        pe.wait_ge(filled, 1)
                        pe.wait_ge(small_loaded, 16 * 4)
                    null_scores()
                    maxima_and_project(b * PAIRS, True)
                    pe.wait_ge(v_act, (b + 1) * KT)
                    pe.wait_ge(v_dve, (b + 1) * KT)
                    for p in range(PAIRS):
                        g = b * PAIRS + p
                        for kt in range(KT):
                            for j in range(2):
                                scores(g, 2 * kt + j)
                            if kt == 0 and p >= 1:
                                sums(g - 1)
                            if kt >= 1:
                                weigh_values(g, kt - 1)
                        weigh_null(g)
                        weigh_values(g, KT - 1)
                        if p + 1 < PAIRS:
                            maxima_and_project(g + 1, p + 2 < PAIRS)

            @block.scalar
            def _(act):
                def high_parts(g):
                    q, k, i = bank(6), bank(7), g % 2
                    copies = 0
                    for j in range(2):
                        rows = slice(j * DH, (j + 1) * DH)
                        for dst, src in ((q1[0:DH, i, j, :], q), (q1[DH:P, i, j, :], q),
                                         (k1[rows, i, j, :], k)):
                            if copies == 0:
                                act.wait_ge(qk_psum, g + 1)
                            last = nc.scalar.activation(dst, src[rows, :], ACT.Copy)
                            copies += 1
                            if copies % 3 == 0:
                                last.then_inc(hi_done, 1)
                            yield

                def place_max(g):
                    act.wait_ge(negmaxT, g + 1)
                    for j in range(2):
                        last = nc.scalar.activation(q2[DH:DH + 1, g % 2, j, :], bank(2)[j * DH:j * DH + 1, :], ACT.Copy)
                    last.then_inc(max_rows, 1)

                def null_probs(g, j):
                    if j == 0 and g >= 1:
                        act.wait_ge(null_added, g)
                        act.wait_ge(pv_done, (g - 1) * (KT + 1) + KT)
                    row = j * DH + NULL_COL
                    last = nc.scalar.activation(null_p[:, j, :], bank(2)[row:row + 1, :], ACT.Exp, scale=SCALE)
                    if j == 1:
                        last.then_inc(null_exp, 1)

                def keep_values(b, n):
                    act.wait_ge(v_psum, 2 * KT * b + n + 1)
                    if b >= 1:
                        act.wait_ge(pv_done, b * PAIRS * (KT + 1))
                    nc.scalar.activation(v_sb[:, n // 2, BANK:2 * BANK], bank(1), ACT.Copy).then_inc(v_act, 1)

                for b in range(s.B):
                    act.wait_ge(xT_psum, 2 * b + 1)
                    nc.scalar.activation(xT[:, 0, :], bank(6), ACT.Copy).then_inc(xT_act, 1)
                    keep_values(b, 1)
                    for _ in high_parts(b * PAIRS):
                        pass
                    for n in range(3, 2 * KT, 2):
                        keep_values(b, n)
                    place_max(b * PAIRS)
                    for p in range(PAIRS):
                        g = b * PAIRS + p
                        parts = high_parts(g + 1) if p + 1 < PAIRS else iter(())
                        for u in range(UNITS):
                            n = g * UNITS + u
                            act.wait_ge(s_psum, n + 1)
                            if n >= RING:
                                back_g, back_u = divmod(n - RING, UNITS)
                                back_kt = back_u // 2
                                act.wait_ge(pv_done, back_g * (KT + 1) + back_kt + 1 + (back_kt == KT - 1))
                                act.wait_ge(summed, back_g + 1)
                            nc.scalar.activation(probs[:, n % RING, :], bank(n % 2), ACT.Exp, scale=SCALE).then_inc(exp_done, 1)
                            if u == UNITS - 2:
                                for j in range(2):
                                    null_probs(g, j)
                            next(parts, None)
                        if p + 1 < PAIRS:
                            place_max(g + 1)

            @block.gpsimd
            def _(pool):
                nc.gpsimd.memset(ones[:], 1.0)
                nc.gpsimd.memset(max_cols[:], 0.0)
                pool.drain()
                nc.gpsimd.memset(k2[DH:DH + 1].bitcast(F32), 1.0).then_inc(filled, 1)

                def add_probs(g):
                    if g >= 1:
                        pool.wait_ge(sums_psum, g)
                    for kt in range(1, KT):
                        pool.wait_ge(exp_done, g * UNITS + 2 * kt + 2)
                        if kt == KT - 1:
                            pool.wait_ge(null_exp, g + 1)
                            for j in range(2):
                                last = nc.gpsimd.tensor_tensor(p_sum[0:1, j, :], p_sum[0:1, j, :], null_p[:, j, :], ALU.add)
                            last.then_inc(null_added, 1)
                            pool.drain()
                        for j in range(2):
                            m = g * UNITS + 2 * kt + j
                            first = probs[:, (m - 2) % RING, :] if kt == 1 else p_sum[:, j, :]
                            last = nc.gpsimd.tensor_tensor(p_sum[:, j, :], first, probs[:, m % RING, :], ALU.add)
                        if kt == KT - 1:
                            last.then_inc(summed, 1)
                        pool.drain()

                def end_batch(b):
                    x_b = tokens(b)
                    if b == 0:
                        pool.wait_ge(biases_ready, 1)
                    for t in range(T):
                        nc.gpsimd.tensor_tensor(x_bias[:, t, :], x_b[:, t, :], ln_bias[:], ALU.add)
                    for t in range(T):
                        pool.wait_ge(out_normed, b * T + t + 1)
                        nc.gpsimd.tensor_tensor(out_n[:, t, :], out_n[:, t, :], ln_scale[:], ALU.mult).then_inc(scaled, 1)

                for b in range(s.B):
                    for p in range(PAIRS):
                        add_probs(b * PAIRS + p)
                    end_batch(b)

            @block.vector
            def _(dve):
                def split_low(g):
                    q, k, i = bank(6), bank(7), g % 2
                    for j in range(2):
                        dve.wait_ge(hi_done, 2 * g + j + 1)
                        rows, other = slice(j * DH, (j + 1) * DH), slice((1 - j) * DH, (2 - j) * DH)
                        nc.vector.tensor_copy(k2[0:DH, i, j, :], k[rows, :])
                        nc.vector.tensor_tensor(q2[0:DH, i, j, :], q[rows, :], q1[rows, i, j, :].bitcast(F32), ALU.subtract)
                        last = nc.vector.tensor_tensor(k1[other, i, j, :], k[rows, :], k1[rows, i, j, :].bitcast(F32), ALU.subtract)
                    last.then_inc(lo_done, 1)

                def maxima(g):
                    p = g % PAIRS
                    for i in range(2 * T):
                        j, t = divmod(i, T)
                        dve.wait_ge(max_psum, g * 2 * T + i + 1)
                        nc.vector.reduce_max(tile_max[:, j, t:t + 1], bank(2 + i % 2), AX_X).then_inc(max_read, 1)
                    dve.drain()
                    nc.vector.tensor_tensor(max_tmp[:], tile_max[:],
                                            s_null[:, :, 2 * p:2 * p + 2].rearrange("p t j -> p j t"), ALU.max)
                    dve.drain()
                    nc.vector.tensor_scalar(max_cols[:, :, 0:P:DH].bitcast(F32R), max_tmp[:].rearrange("p j t -> p t j"),
                                            -1.0, None, ALU.mult)
                    dve.drain()
                    nc.vector.tensor_tensor(max_cols[:, :, NULL_COL:P:DH], s_null[:, :, 2 * p:2 * p + 2],
                                            max_cols[:, :, 0:P:DH], ALU.add).then_inc(negmax, 1)

                def normalize(g):
                    dve.wait_ge(sums_psum, g + 1)
                    dve.drain()
                    nc.vector.reciprocal(denom[:], bank(3)).then_inc(sums_read, 1)
                    dve.drain()
                    nc.vector.tensor_tensor(oT[:, g % PAIRS, :], bank(4 + g % 2), denom[:], ALU.mult).then_inc(norm_done, 1)

                def norm_tokens(b):
                    x_b = tokens(b)
                    dve.drain()
                    norm.statistics(dve, lambda t: x_b[:, t, :], LN_EPS)
                    for t in range(T):
                        norm.apply(xn[:, t, :], x_b[:, t, :], t).then_inc(xn_ready, 1)

                def keep_values(b, n):
                    dve.wait_ge(v_psum, 2 * KT * b + n + 1)
                    if b >= 1:
                        dve.wait_ge(pv_done, b * PAIRS * (KT + 1))
                    nc.vector.tensor_copy(v_sb[:, n // 2, 0:BANK], bank(0)).then_inc(v_dve, 1)

                def norm_output(b):
                    dve.wait_ge(out_psum, (b + 1) * T)
                    dve.drain()
                    norm_out.statistics(dve, lambda t: bank(2 + t)[:, 0:D], LN_OUT_EPS)
                    for t in range(T):
                        norm_out.apply(out_n[:, t, :], bank(2 + t)[:, 0:D], t).then_inc(out_normed, 1)

                def add_output(b):
                    x_b = tokens(b)
                    for t in range(T):
                        dve.wait_ge(scaled, b * T + t + 1)
                        nc.vector.tensor_tensor(x_b[:, t, :], x_bias[:, t, :], out_n[:, t, :], ALU.add)

                def prepare_biases():
                    dve.wait_ge(small_loaded, 16 * 4)
                    nc.vector.tensor_scalar(ln_scale[:], ln_scale[:], gates[:, 2:3], None, ALU.mult)
                    nc.vector.tensor_scalar(ln_bias[:], ln_bias[:], gates[:, 2:3], None, ALU.mult).then_inc(biases_ready, 1)
                    dve.wait_ge(filled, 1)

                def prepare_w_null(c):
                    dve.wait_ge(wqk_loaded, 32)
                    nc.vector.tensor_tensor(w_null_tmp, wq[:, c, :].rearrange("p (h k) -> p h k", h=H),
                                            null_k[:].unsqueeze(1).to_broadcast([P, H, DH]), ALU.mult)
                    dve.drain()
                    last = nc.vector.reduce_sum(w_null[:, c, :], w_null_tmp, AX_X)
                    if c == s.DC - 1:
                        last.then_inc(w_null_ready, 1)
                    dve.drain()

                norm_tokens(0)
                for b in range(s.B + 1):
                    if b < s.B:
                        dve.wait_ge(xT_psum, 2 * b + 2)
                        nc.vector.tensor_copy(xT[:, 1, :], bank(7)).then_inc(xT_dve, 1)
                        keep_values(b, 0)
                    if b >= 1:
                        normalize(b * PAIRS - 1)
                    if b == 0:
                        prepare_biases()
                        prepare_w_null(0)
                    if b < s.B:
                        split_low(b * PAIRS)
                    if b >= 1:
                        norm_output(b - 1)
                    if b < s.B:
                        keep_values(b, 2)
                    if b >= 1:
                        add_output(b - 1)
                    if b == s.B:
                        break
                    for n in range(4, 2 * KT, 2):
                        if b == 0 and n // 2 < s.DC + 1:
                            prepare_w_null(n // 2 - 1)
                        keep_values(b, n)
                    dve.wait_ge(null_psum, b + 1)
                    nc.vector.tensor_copy(s_null[:], bank(4)[:, 0:T * H].rearrange("p (t h) -> p t h", t=T))
                    maxima(b * PAIRS)
                    for p in range(PAIRS):
                        g = b * PAIRS + p
                        if b >= 1 and p == 1:
                            dve.drain()
                            norm.statistics(dve, lambda t: tokens(b - 1)[:, t, :], LN_EPS)
                        elif b >= 1 and p == 2:
                            norm_rows(dve, norm, x_resid, routed, b - 1, T, with_statistics=False)
                        if p >= 1:
                            normalize(g - 1)
                        if p + 1 < PAIRS:
                            split_low(g + 1)
                            maxima(g + 1)
                        elif b + 1 < s.B:
                            norm_tokens(b + 1)


def experts(nc, s, g, bank, dram, out):
    T, D, E, N, B = s.T, s.D, s.E, s.N, s.B
    TB = s.TT
    NB = T // TB
    TOP = 2
    ROWS = 256
    HALVES = ROWS // P
    TILES = TOP * T * P // ROWS + E - 1
    MOST = -(-T * P // ROWS)
    FT = s.FT
    PIECE = 2
    W_SLOTS = 8
    SPLITS = 8
    AHEAD = 5
    DELAY = 2

    WIDE = D + ROW_PAD
    xs_dram = nc.dram_tensor("moe_sorted_x", [TILES * ROWS, WIDE], F32).ap()
    RESULTS = TILES * ROWS
    y_dram = nc.dram_tensor("moe_y", [RESULTS + TOP * T * P, D], F32).ap()

    with ExitStack() as ctx:
        def sb(name, shape, dt=F32):
            return ctx.enter_context(nc.sbuf_tensor("moe_" + name, shape, dt))

        def sem(name):
            return ctx.enter_context(nc.semaphore(name))

        w_router = sb("w_router", [P, s.DC, E])
        b_router = sb("b_router", [P, E])
        xn = g["routed"]
        zeros = sb("zeros", [P, WIDE])
        lower = sb("lower", [P, P])
        ones = sb("ones", [P, P])
        logits = sb("logits", [P, T, E])
        before = sb("before", [P, E, E])
        steps = sb("steps", [P, MOST])
        tile_no = sb("tile_no", [P, TILES])
        rank = sb("rank", [P, T, E])
        chosen = sb("chosen", [P, TOP, T, E])
        either = sb("either", [P, T, E])
        work8 = sb("work8", [P, T, E])
        top = sb("top", [P, 4, T])
        weight = sb("weight", [P, TOP, T])
        sums = sb("sums", [P, 2, T + 1, E])
        full = sb("full", [P, E, MOST])
        n_tiles = sb("n_tiles", [P, 2, E + 1])
        past = sb("past", [P, TILES, E])
        tile_expert = sb("tile_expert", [P, TILES])
        expert_ids = sb("expert_ids", [P, TILES], U32)
        slot = sb("slot", [P, TOP, T])
        slot_ids = sb("slot_ids", [P, TOP, T], U32)
        first_rows = sb("first_rows", [P, T, WIDE])
        token_places = sb("token_places", [P, TOP, T], U32)
        row_places = sb("row_places", [P, TILES, HALVES], U32)
        places = sb("places", [P, 3, HALVES], U32)
        rows = (first_rows, xn)
        w13 = sb("w13", [P, W_SLOTS, 2 * s.DC, PIECE * P])
        w2 = sb("w2", [P, W_SLOTS, PIECE, D])
        stats = sb("stats", [P, TB, 6])
        mv = sb("mv", [P, TB, 2])
        work = sb("work", [P, 4, TB])
        norm = Norm(nc, TB, stats, mv, work)

        loaded = sem("moe_router_loaded")
        zeroed = sem("moe_zeroed")
        cleared = sem("moe_cleared")
        xn_ready = sem("moe_xn_ready")
        xT_psum = sem("moe_xT_psum")
        xT_act = sem("moe_xT_act")
        xT_dve = sem("moe_xT_dve")
        lg_psum = sem("moe_lg_psum")
        tops = sem("moe_tops")
        exped = sem("moe_exped")
        either_ready = sem("moe_either_ready")
        prefix_psum = sem("moe_prefix_psum")
        weights_ready = sem("moe_weights_ready")
        second_scaled = sem("moe_second_scaled")
        scattered = sem("moe_scattered")

        with ExitStack() as inner:
            xT = inner.enter_context(nc.sbuf_tensor("moe_xT", [P, s.DC, T * P], F32))
            cmp = inner.enter_context(nc.sbuf_tensor("moe_cmp", [P, T, E, E], F32))
            tie = inner.enter_context(nc.sbuf_tensor("moe_tie", [P, T, E, E], F32))

            with nc.Block() as block:
                @block.sync
                def _(sp):
                    sp.dma_start(w_router[:], dram["w_router"].rearrange("(c p) n -> p c n", p=P)).then_inc(loaded, 16)
                    sp.dma_start(b_router[:], dram["b_router"].partition_broadcast(P)).then_inc(loaded, 16)
                    sp.wait_ge(zeroed, 1)
                    sp.dma_start(xs_dram.rearrange("(n p) d -> p n d", p=P),
                                 zeros[:].unsqueeze(1).to_broadcast([P, TILES * HALVES, WIDE])).then_inc(cleared, 16)

                @block.gpsimd
                def _(pool):
                    nc.gpsimd.memset(zeros[:], 0.0).then_inc(zeroed, 1)
                    nc.gpsimd.memset(before[:], 1.0)
                    nc.gpsimd.memset(ones[:], 1.0)
                    nc.gpsimd.memset(lower[:], 1.0)
                    nc.gpsimd.iota(steps[:], pattern=[[ROWS, MOST]], base=0, channel_multiplier=0,
                                   allow_small_or_imprecise_dtypes=True)
                    nc.gpsimd.iota(token_places[:], pattern=[[T * P, TOP], [P, T]], base=RESULTS, channel_multiplier=1)
                    nc.gpsimd.iota(row_places[:], pattern=[[ROWS, TILES], [P, HALVES]], base=0, channel_multiplier=1)
                    for k in range(TOP):
                        nc.gpsimd.memset(rows[k][:, :, D:WIDE], 0.0)
                    nc.gpsimd.iota(tile_no[:], pattern=[[1, TILES]], base=0, channel_multiplier=0,
                                   allow_small_or_imprecise_dtypes=True)
                    pool.drain()
                    nc.gpsimd.affine_select(out=before[:], in_=before[:], compare_op=ALU.is_gt, fill=0.0, base=0,
                                            pattern=[[1, E], [-1, E]], channel_multiplier=0)
                    nc.gpsimd.affine_select(out=lower[:], in_=lower[:], compare_op=ALU.is_gt, fill=0.0, base=0,
                                            pattern=[[1, P]], channel_multiplier=-1)

                @block.vector
                def _(dve):
                    for b in range(NB):
                        if b == NB - 1:
                            norm_rows(dve, norm, g["x"], xn[:, :, 0:D], b, TB).then_inc(xn_ready, 1)
                        dve.wait_ge(xT_psum, 2 * b + 2)
                        nc.vector.tensor_copy(xT[:, 1, b * N:(b + 1) * N], bank(2 * (b % 2) + 1)).then_inc(xT_dve, 1)
                    dve.wait_ge(lg_psum, 2)
                    dve.wait_ge(loaded, 32)
                    nc.vector.tensor_tensor(logits[:], bank(4)[:, 0:T * E].rearrange("p (t e) -> p t e", t=T),
                                            b_router[:].unsqueeze(1).to_broadcast([P, T, E]), ALU.add)

                @block.scalar
                def _(act):
                    for b in range(NB):
                        act.wait_ge(xT_psum, 2 * b + 1)
                        nc.scalar.activation(xT[:, 0, b * N:(b + 1) * N], bank(2 * (b % 2)), ACT.Copy).then_inc(xT_act, 1)

                @block.tensor
                def _(pe):
                    def logits_of(blocks):
                        pe.wait_ge(loaded, 32)
                        pe.wait_ge(xT_act, blocks[-1] + 1)
                        pe.wait_ge(xT_dve, blocks[-1] + 1)
                        for t in range(blocks[0] * TB, (blocks[-1] + 1) * TB):
                            for c in range(s.DC):
                                last = nc.tensor.matmul(bank(4)[:, t * E:(t + 1) * E], xT[:, c, t * P:(t + 1) * P],
                                                        w_router[:, c, :], start=(c == 0), stop=(c == s.DC - 1))
                        last.then_inc(lg_psum, 1)

                    for b in range(NB):
                        if b == NB - 1:
                            logits_of(range(0, b))
                            pe.wait_ge(xn_ready, 1)
                        if b >= 2:
                            pe.wait_ge(xT_act, b - 1)
                            pe.wait_ge(xT_dve, b - 1)
                        for c in range(s.DC):
                            for t in range(TB):
                                last = nc.tensor.transpose(bank(2 * (b % 2) + c)[:, t * P:(t + 1) * P],
                                                           xn[:, b * TB + t, c * P:(c + 1) * P], g["ident"][:])
                            last.then_inc(xT_psum, 1)
                    logits_of(range(NB - 1, NB))

            with nc.Block() as block:
                @block.vector
                def _(dve):
                    for k in range(TOP):
                        nc.vector.tensor_copy(rows[k][:, :, D:D + 1].bitcast(U32), token_places[:, k, :].unsqueeze(2))
                    mine = logits[:].unsqueeze(3).to_broadcast([P, T, E, E])
                    other = logits[:].unsqueeze(2).to_broadcast([P, T, E, E])
                    nc.vector.tensor_tensor(cmp[:], other, mine, ALU.is_gt)
                    nc.vector.tensor_tensor(tie[:], other, mine, ALU.is_equal)
                    dve.drain()
                    nc.vector.tensor_tensor(tie[:].rearrange("p t e j -> p t (e j)"), tie[:].rearrange("p t e j -> p t (e j)"),
                                            before[:].rearrange("p e j -> p (e j)").unsqueeze(1).to_broadcast([P, T, E * E]),
                                            ALU.mult)
                    dve.drain()
                    nc.vector.tensor_tensor(cmp[:], cmp[:], tie[:], ALU.add)
                    dve.drain()
                    nc.vector.reduce_sum(rank[:], cmp[:], AX_X)
                    dve.drain()
                    for k in range(TOP):
                        nc.vector.tensor_scalar(chosen[:, k], rank[:], float(k), None, ALU.is_equal)
                    nc.vector.tensor_scalar(either[:], rank[:], float(TOP), None, ALU.is_lt).then_inc(either_ready, 1)
                    dve.drain()
                    nc.vector.tensor_tensor(work8[:], chosen[:, 1], logits[:], ALU.mult)
                    nc.vector.reduce_max(top[:, 0, :], logits[:], AX_X)
                    dve.drain()
                    nc.vector.reduce_sum(top[:, 1, :], work8[:], AX_X)
                    dve.drain()
                    nc.vector.tensor_tensor(top[:, 2, :], top[:, 1, :], top[:, 0, :], ALU.subtract).then_inc(tops, 1)
                    dve.wait_ge(exped, 1)
                    nc.vector.tensor_scalar(top[:, 0, :], top[:, 3, :], 1.0, None, ALU.add)
                    dve.drain()
                    nc.vector.reciprocal(weight[:, 0, :], top[:, 0, :])
                    dve.drain()
                    nc.vector.tensor_tensor(weight[:, 1, :], top[:, 3, :], weight[:, 0, :],
                                            ALU.mult).then_inc(weights_ready, 1)
                    dve.wait_ge(prefix_psum, 2)
                    nc.vector.memset(sums[:, 0, 0:1, :], 0.0)
                    nc.vector.tensor_copy(sums[:, 0, 1:T + 1, :], bank(1)[:, 0:T * E].rearrange("p (t e) -> p t e", t=T))
                    src, d = 0, 1
                    while d <= T:
                        dve.drain()
                        nc.vector.tensor_copy(sums[:, 1 - src, 0:d, :], sums[:, src, 0:d, :])
                        nc.vector.tensor_tensor(sums[:, 1 - src, d:T + 1, :], sums[:, src, d:T + 1, :],
                                                sums[:, src, 0:T + 1 - d, :], ALU.add)
                        src, d = 1 - src, 2 * d
                    dve.drain()
                    nc.vector.tensor_tensor(full[:], sums[:, src, T, :].unsqueeze(2).to_broadcast([P, E, MOST]),
                                            steps[:].unsqueeze(1).to_broadcast([P, E, MOST]), ALU.is_gt)
                    nc.vector.tensor_tensor(work8[:], sums[:, src, 0:T, :],
                                            bank(0)[:, 0:T * E].rearrange("p (t e) -> p t e", t=T), ALU.add)
                    dve.drain()
                    nc.vector.memset(n_tiles[:, 0, 0:1], 0.0)
                    nc.vector.reduce_sum(n_tiles[:, 0, 1:E + 1], full[:], AX_X)
                    src, d = 0, 1
                    while d <= E:
                        dve.drain()
                        nc.vector.tensor_copy(n_tiles[:, 1 - src, 0:d], n_tiles[:, src, 0:d])
                        nc.vector.tensor_tensor(n_tiles[:, 1 - src, d:E + 1], n_tiles[:, src, d:E + 1],
                                                n_tiles[:, src, 0:E + 1 - d], ALU.add)
                        src, d = 1 - src, 2 * d
                    dve.drain()
                    nc.vector.tensor_tensor(past[:], tile_no[:].unsqueeze(2).to_broadcast([P, TILES, E]),
                                            n_tiles[:, src, 1:E + 1].unsqueeze(1).to_broadcast([P, TILES, E]), ALU.is_ge)
                    nc.vector.tensor_scalar(n_tiles[:, 1 - src, 0:E], n_tiles[:, src, 0:E], float(ROWS), None, ALU.mult)
                    dve.drain()
                    nc.vector.reduce_sum(tile_expert[:], past[:], AX_X)
                    nc.vector.tensor_tensor(work8[:], work8[:], n_tiles[:, 1 - src, 0:E].unsqueeze(1).to_broadcast([P, T, E]),
                                            ALU.add)
                    dve.drain()
                    nc.vector.tensor_scalar(expert_ids[:], tile_expert[:], float(E - 1), None, ALU.min)
                    for k in range(TOP):
                        nc.vector.tensor_tensor(chosen[:, k], chosen[:, k], work8[:], ALU.mult)
                    dve.drain()
                    for k in range(TOP):
                        nc.vector.reduce_sum(slot[:, k, :], chosen[:, k], AX_X)
                    dve.drain()
                    nc.vector.tensor_copy(slot_ids[:], slot[:])
                    for t in range(T):
                        nc.vector.scalar_tensor_tensor(out=g["x"][:, t, :], in0=xn[:, t, 0:D], scalar=g["gates"][:, 3:4],
                                                       in1=g["x"][:, t, :], op0=ALU.mult, op1=ALU.add)

                @block.scalar
                def _(act):
                    act.wait_ge(tops, 1)
                    nc.scalar.activation(top[:, 3, :], top[:, 2, :], ACT.Exp).then_inc(exped, 1)
                    act.wait_ge(weights_ready, 1)
                    for t in range(T):
                        nc.scalar.activation(first_rows[:, t, 0:D], xn[:, t, 0:D], ACT.Copy,
                                             scale=weight[:, 0, t:t + 1])

                @block.tensor
                def _(pe):
                    pe.wait_ge(either_ready, 1)
                    flat = either[:].rearrange("p t e -> p (t e)")
                    nc.tensor.matmul(bank(0)[:, 0:T * E], lower[:], flat, start=True, stop=True).then_inc(prefix_psum, 1)
                    nc.tensor.matmul(bank(1)[:, 0:T * E], ones[:], flat, start=True, stop=True).then_inc(prefix_psum, 1)

        w13_hi = sb("w13_hi", [P, SPLITS, 2 * s.DC, P], F32R)
        w13_lo = sb("w13_lo", [P, SPLITS, 2 * s.DC, P], F32R)
        w2_hi = sb("w2_hi", [P, SPLITS, D], F32R)
        w2_lo = sb("w2_lo", [P, SPLITS, D], F32R)
        xs = sb("xs", [P, 2, HALVES, WIDE])
        xs_hi = sb("xs_hi", [P, 2, s.DC, ROWS], F32R)
        xs_lo = sb("xs_lo", [P, 2, s.DC, ROWS], F32R)
        gate = sb("gate", [P, 3, ROWS])
        hid = sb("hid", [P, 3, ROWS])
        hid_hi = sb("hid_hi", [P, 3, ROWS], F32R)
        hid_lo = sb("hid_lo", [P, 3, ROWS], F32R)
        y_sb = sb("y_sb", [P, 2, HALVES, D])

        w_ready = [sem(f"moe_w_ready_{i}") for i in range(W_SLOTS)]
        xs_ready = [sem(f"moe_xs_ready_{i}") for i in range(2)]
        w13_rounded = sem("moe_w13_rounded")
        w2_rounded = sem("moe_w2_rounded")
        w13_split = sem("moe_w13_split")
        w2_split = sem("moe_w2_split")
        xsT_psum = sem("moe_xsT_psum")
        xs_rounded = sem("moe_xs_rounded")
        xsT_ready = sem("moe_xsT_ready")
        up_psum = sem("moe_up_psum")
        gate_done = sem("moe_gate_done")
        hid_raw = sem("moe_hid_raw")
        hid_rounded = sem("moe_hid_rounded")
        hid_ready = sem("moe_hid_ready")
        y_psum = sem("moe_y_psum")
        y_ready = sem("moe_y_ready")
        y_stored = [sem(f"moe_y_stored_{i}") for i in range(2)]
        STEPS = TILES * FT

        PIECES = STEPS // PIECE

        def arrived(k):
            return (k // PIECE) % W_SLOTS, slice(k % PIECE * P, (k % PIECE + 1) * P), k % PIECE

        with nc.Block() as block:
            @block.sync
            def _(sp):
                def load_weights(m):
                    if m >= W_SLOTS:
                        sp.wait_ge(w13_split, PIECE * (m - W_SLOTS + 1))
                        sp.wait_ge(w2_split, PIECE * (m - W_SLOTS + 1))
                    first = m * PIECE % FT
                    for dst, name in ((w13[:, m % W_SLOTS, 0:s.DC], "moe_w1"), (w13[:, m % W_SLOTS, s.DC:2 * s.DC], "moe_w3")):
                        sp.dma_start(dst, dram[name][bass.ds(e, 1), :, first * P:(first + PIECE) * P]
                                     .rearrange("o (c p) n -> p (o c) n", p=P)).then_inc(w_ready[m % W_SLOTS], 16)
                    sp.dma_start(w2[:, m % W_SLOTS], dram["moe_w2"][bass.ds(e, 1), first * P:(first + PIECE) * P, :]
                                 .rearrange("o (c p) n -> p (o c) n", p=P)).then_inc(w_ready[m % W_SLOTS], 16)

                def load_rows(i):
                    if i >= 2:
                        sp.wait_ge(xsT_ready, i - 1)
                    sp.dma_start(xs[:, i % 2], xs_dram[i * ROWS:(i + 1) * ROWS, :].rearrange("(h p) d -> p h d", p=P)
                                 ).then_inc(xs_ready[i % 2], 16)

                for m in range(PIECES):
                    if m == W_SLOTS:
                        sp.wait_ge(scattered, 16 * TOP * T)
                        load_rows(0)
                        load_rows(1)
                    i, part = divmod(m * PIECE, FT)
                    if part == 0:
                        e = sp.value_load(expert_ids[0:1, i:i + 1], min_val=0, max_val=E - 1)
                        if m >= W_SLOTS:
                            load_rows(i)
                    load_weights(m)

            @block.tensor
            def _(pe):
                def transposes(i):
                    pe.wait_ge(xs_ready[i % 2], 16 * (i // 2 + 1))
                    if i >= 1:
                        pe.wait_ge(xsT_ready, i)
                    for c in range(s.DC):
                        for h in range(HALVES):
                            last = nc.tensor.transpose(bank(7)[:, c * ROWS + h * P:c * ROWS + (h + 1) * P],
                                                       xs[:, i % 2, h, c * P:(c + 1) * P], g["ident"][:])
                    last.then_inc(xsT_psum, 1)

                def up(k):
                    i, f = divmod(k, FT)
                    pe.wait_ge(w13_split, k + 1)
                    if k >= 3:
                        pe.wait_ge(hid_raw, k - 2)
                    for n in range(2):
                        for c in range(s.DC):
                            hi, lo = w13_hi[:, k % SPLITS, n * s.DC + c, :], w13_lo[:, k % SPLITS, n * s.DC + c, :]
                            for j, (w, x_part) in enumerate(((hi, xs_hi), (hi, xs_lo), (lo, xs_hi))):
                                last = nc.tensor.matmul(bank(k % 3)[:, n * ROWS:(n + 1) * ROWS], w, x_part[:, i % 2, c, :],
                                                        start=(c == 0 and j == 0), stop=(c == s.DC - 1 and j == 2))
                    last.then_inc(up_psum, 1)

                def down(k):
                    i, f = divmod(k, FT)
                    pe.wait_ge(w2_split, k + 1)
                    pe.wait_ge(hid_ready, k + 1)
                    if f == 0 and i >= 2:
                        pe.wait_ge(y_ready, i - 1)
                    hi, lo = w2_hi[:, k % SPLITS, :], w2_lo[:, k % SPLITS, :]
                    for h in range(HALVES):
                        rows_h = slice(h * P, (h + 1) * P)
                        for j, (h_part, w) in enumerate(((hid_hi, hi), (hid_hi, lo), (hid_lo, hi))):
                            last = nc.tensor.matmul(bank(3 + 2 * (i % 2) + h)[:, 0:D], h_part[:, k % 3, rows_h], w,
                                                    start=(f == 0 and j == 0), stop=(f == FT - 1 and j == 2))
                    if f == FT - 1:
                        last.then_inc(y_psum, 1)

                transposes(0)
                for k in range(STEPS + DELAY):
                    i, f = divmod(k, FT)
                    if k < STEPS:
                        if f == 0:
                            pe.wait_ge(xsT_ready, i + 1)
                        up(k)
                    if k >= DELAY:
                        down(k - DELAY)
                    if f == FT - 3 and i + 1 < TILES:
                        transposes(i + 1)

            @block.scalar
            def _(act):
                def round_weights(k):
                    slot_k, cols, row = arrived(k)
                    if k % PIECE == 0:
                        act.wait_ge(w_ready[slot_k], 48 * (k // PIECE // W_SLOTS + 1))
                    nc.scalar.activation(w13_hi[:, k % SPLITS], w13[:, slot_k, :, cols], ACT.Copy).then_inc(w13_rounded, 1)
                    nc.scalar.activation(w2_hi[:, k % SPLITS, :], w2[:, slot_k, row, :], ACT.Copy).then_inc(w2_rounded, 1)

                def round_rows(i):
                    act.wait_ge(xsT_psum, i + 1)
                    nc.scalar.activation(xs_hi[:, i % 2], bank(7).rearrange("p (c n) -> p c n", c=s.DC),
                                         ACT.Copy).then_inc(xs_rounded, 1)

                for t in range(T):
                    nc.scalar.activation(xn[:, t, 0:D], xn[:, t, 0:D], ACT.Copy,
                                         scale=weight[:, 1, t:t + 1]).then_inc(second_scaled, 1)
                for k in range(AHEAD):
                    round_weights(k)
                round_rows(0)
                for k in range(STEPS + 1):
                    i, f = divmod(k, FT)
                    if k < STEPS:
                        act.wait_ge(up_psum, k + 1)
                        nc.scalar.activation(gate[:, k % 3, :], bank(k % 3)[:, 0:ROWS], ACT.Silu).then_inc(gate_done, 1)
                    if k >= 1:
                        act.wait_ge(hid_raw, k)
                        nc.scalar.activation(hid_hi[:, (k - 1) % 3, :], hid[:, (k - 1) % 3, :], ACT.Copy).then_inc(hid_rounded, 1)
                    if k + AHEAD < STEPS:
                        round_weights(k + AHEAD)
                    if f == FT - 2 and i + 1 < TILES:
                        round_rows(i + 1)

            @block.vector
            def _(dve):
                def split_down(k):
                    slot_k, _, row = arrived(k)
                    dve.wait_ge(w2_rounded, k + 1)
                    nc.vector.tensor_tensor(w2_lo[:, k % SPLITS, :], w2[:, slot_k, row, :],
                                            w2_hi[:, k % SPLITS, :].bitcast(F32), ALU.subtract).then_inc(w2_split, 1)

                def split_rows(i):
                    dve.wait_ge(xs_rounded, i + 1)
                    if i >= 3:
                        dve.wait_ge(y_stored[(i - 3) % 2], 16 * HALVES * ((i - 3) // 2 + 1))
                    nc.vector.tensor_tensor(places[:, i % 3, :].unsqueeze(2), xs[:, i % 2, :, D:D + 1].bitcast(U32),
                                            row_places[:, i, :].unsqueeze(2), ALU.max)
                    nc.vector.tensor_tensor(xs_lo[:, i % 2], bank(7).rearrange("p (c n) -> p c n", c=s.DC),
                                            xs_hi[:, i % 2].bitcast(F32), ALU.subtract).then_inc(xsT_ready, 1)

                def evacuate_y(i):
                    dve.wait_ge(y_psum, i + 1)
                    if i >= 2:
                        dve.wait_ge(y_stored[i % 2], 16 * HALVES * (i // 2))
                    for h in range(HALVES):
                        last = nc.vector.tensor_copy(y_sb[:, i % 2, h, :], bank(3 + 2 * (i % 2) + h)[:, 0:D])
                    last.then_inc(y_ready, 1)

                for k in range(AHEAD):
                    split_down(k)
                split_rows(0)
                for k in range(STEPS + 1):
                    i, f = divmod(k, FT)
                    if k < STEPS:
                        dve.wait_ge(gate_done, k + 1)
                        nc.vector.tensor_tensor(hid[:, k % 3, :], bank(k % 3)[:, ROWS:2 * ROWS], gate[:, k % 3, :],
                                                ALU.mult).then_inc(hid_raw, 1)
                    if k >= 1:
                        dve.wait_ge(hid_rounded, k)
                        nc.vector.tensor_tensor(hid_lo[:, (k - 1) % 3, :], hid[:, (k - 1) % 3, :],
                                                hid_hi[:, (k - 1) % 3, :].bitcast(F32), ALU.subtract).then_inc(hid_ready, 1)
                    if k + AHEAD < STEPS:
                        split_down(k + AHEAD)
                    if f == FT - 2 and i + 1 < TILES:
                        split_rows(i + 1)
                    if f == 3 and 1 <= i < TILES:
                        evacuate_y(i - 1)
                evacuate_y(TILES - 1)

            @block.gpsimd
            def _(pool):
                def split_up(k):
                    slot_k, cols, _ = arrived(k)
                    pool.wait_ge(w13_rounded, k + 1)
                    nc.gpsimd.tensor_tensor(w13_lo[:, k % SPLITS], w13[:, slot_k, :, cols],
                                            w13_hi[:, k % SPLITS].bitcast(F32), ALU.subtract).then_inc(w13_split, 1)

                pool.wait_ge(cleared, 16)
                for k in range(TOP):
                    for t in range(T):
                        if k == 1:
                            pool.wait_ge(second_scaled, t + 1)
                        nc.gpsimd.indirect_dma_start(
                            out=xs_dram, out_offset=bass.IndirectOffsetOnAxis(ap=slot_ids[:, k, t:t + 1], axis=0),
                            in_=rows[k][:, t, :], in_offset=None).then_inc(scattered, 16)
                def store_results(i):
                    pool.wait_ge(y_ready, i + 1)
                    for h in range(HALVES):
                        nc.gpsimd.indirect_dma_start(
                            out=y_dram, out_offset=bass.IndirectOffsetOnAxis(ap=places[:, i % 3, h:h + 1], axis=0),
                            in_=y_sb[:, i % 2, h, :], in_offset=None).then_inc(y_stored[i % 2], 16)

                for k in range(AHEAD):
                    split_up(k)
                for k in range(STEPS):
                    i, f = divmod(k, FT)
                    if k + AHEAD < STEPS:
                        split_up(k + AHEAD)
                    if f == 4 and i >= 1:
                        store_results(i - 1)
                store_results(TILES - 1)
                pool.wait_ge(y_stored[0], 16 * HALVES * ((TILES + 1) // 2))
                pool.wait_ge(y_stored[1], 16 * HALVES * (TILES // 2))

        results_loaded = [sem(f"moe_results_loaded_{b}") for b in range(NB)]
        fin = sem("moe_fin")
        stored = sem("moe_stored")
        with nc.Block() as block:
            def block_rows(a, b):
                return a[:, b * TB:(b + 1) * TB, 0:D]

            def load_results(queue, k, b):
                first = RESULTS + (k * T + b * TB) * P
                queue.dma_start(block_rows(rows[k], b), y_dram[first:first + TB * P, :].rearrange("(t p) d -> p t d", p=P)
                                ).then_inc(results_loaded[b], 16)

            @block.scalar
            def _(act):
                for b in range(NB):
                    load_results(act, 1, b)

            @block.vector
            def _(dve):
                for b in range(NB):
                    dve.wait_ge(results_loaded[b], 16 * TOP)
                    nc.vector.tensor_tensor(block_rows(first_rows, b), block_rows(first_rows, b), block_rows(xn, b), ALU.add)
                    dve.drain()
                    nc.vector.scalar_tensor_tensor(out=block_rows(g["x"], b), in0=block_rows(first_rows, b),
                                                   scalar=g["gates"][:, 3:4], in1=block_rows(g["x"], b), op0=ALU.mult,
                                                   op1=ALU.add).then_inc(fin, 1)

            @block.sync
            def _(sp):
                for b in range(NB):
                    load_results(sp, 0, b)
                for b in range(NB):
                    sp.wait_ge(fin, b + 1)
                    sp.dma_start(out[b].rearrange("(t p) n -> p t n", p=P), block_rows(g["x"], b)).then_inc(stored, 16)
                sp.wait_ge(stored, 16 * NB)


def flamingo(nc, dram, out):
    s = Shapes(dram["x"], dram["ctx"], dram["w_in"], dram["w_router"], dram["moe_w1"], dram["null_kv"], dram["wq"])
    with ExitStack() as ctx:
        def sb(name, shape, dt=F32):
            return ctx.enter_context(nc.sbuf_tensor(name, shape, dt))

        psum = ctx.enter_context(nc.psum_tensor("psum", [P, 8 * BANK], F32))

        def bank(i):
            return psum[:, i * BANK:(i + 1) * BANK]

        def wide(i):
            return psum[:, i * BANK:(i + 2) * BANK]

        g = {"x": sb("x_resid", [P, s.T, s.D]), "ident": sb("ident", [P, P]), "gates": sb("gates", [P, 4])}
        layer0(nc, s, g, bank, wide, dram)
        g["routed"] = sb("routed_xn", [P, s.T, s.D + ROW_PAD])
        layer1(nc, s, g, bank, dram)
        experts(nc, s, g, bank, dram, out)


def kernel(**inputs):
    import numpy as np
    import concourse.bacc as bacc
    from concourse.bass_utils import run_bass_kernel_spmd

    a = {k: np.asarray(v) for k, v in inputs.items()}
    arrays = {
        "x": a["x"], "ctx": a["ctx_2048"], "ctxT": a["ctx_2048"].transpose(0, 2, 1),
        "g_xattn": a["g_xattn"], "g_ffn": a["g_ffn"],
        "w_qkvT": a["L0_xattn_w_qkv"].T, "w_projT": a["L0_xattn_w_proj"].T, "b_proj": a["L0_xattn_b_proj"],
        "w_in": a["L0_ffn_Win"], "b_in": a["L0_ffn_bin_"], "w1": a["L0_ffn_W1"], "b1": a["L0_ffn_b1"],
        "w2": a["L0_ffn_W2"], "b2": a["L0_ffn_b2"], "w_out": a["L0_ffn_Wout"], "b_out": a["L0_ffn_bout"],
        "wq": a["L1_xattn_Wq"], "wkv": a["L1_xattn_Wkv"], "null_kv": a["L1_xattn_null_kv"], "wo": a["L1_xattn_Wout"],
        "ln_scale": a["L1_xattn_ln_scale"], "ln_bias": a["L1_xattn_ln_bias"],
        "w_router": a["L1_ffn_Wg"], "b_router": a["L1_ffn_bg"],
        "moe_w1": a["L1_ffn_W1"], "moe_w2": a["L1_ffn_W2"], "moe_w3": a["L1_ffn_W3"],
    }
    arrays = {f"in_{k}": np.ascontiguousarray(v) for k, v in arrays.items()}
    nc = bacc.Bacc("TRN2", target_bir_lowering=False, num_devices=1)
    dram = {k[3:]: nc.dram_tensor(k, v.shape, mybir.dt.from_np(v.dtype), kind="ExternalInput").ap()
            for k, v in arrays.items()}
    out = nc.dram_tensor("out_x", a["x"].shape, F32, kind="ExternalOutput").ap()
    flamingo(nc, dram, out)
    result = run_bass_kernel_spmd(nc, [arrays], core_ids=[0])
    return result.results[0]["out_x"]
```
